# Optimizing a Trainium2 kernel written in Bass

```python
import numpy as np
import jax
import jax.numpy as jnp

def _softmax(x, axis=-1):
    return jax.nn.softmax(x, axis=axis)

def _gelu(x):
    return jax.nn.gelu(x, approximate=True)

def _silu(x):
    return jax.nn.silu(x)

def _sigmoid(x):
    return jax.nn.sigmoid(x)

def _layernorm(x, axis=-1, eps=1e-05):
    m = jnp.mean(x, axis=axis, keepdims=True)
    v = jnp.var(x, axis=axis, keepdims=True)
    return (x - m) / jnp.sqrt(v + eps)

def _scatter_add(tgt, idx, src, axis=0):
    return tgt.at[idx].add(src)

def _segment_sum(src, seg, n):
    return jax.ops.segment_sum(src, seg, n)
kernel_name = 'mk_adaln_attn_ffn_d1_seqx_r4_4112a3'

def setup_inputs(seed: int=0):
    np.random.seed(seed)
    _w = jnp.asarray

    def _rec_inputs():
        import jax
        import jax.numpy as jnp
        _rk = jax.random.key(seed)
        x = 7.22e-05 + 1 * jax.random.normal(jax.random.fold_in(_rk, 1), (8, 256, 512), jnp.float32)
        _lenS = 256 - jax.random.randint(jax.random.fold_in(_rk, 7), (8,), 0, max(1, 256 // 4) + 1, jnp.int32)
        _lenS2 = 256 - jax.random.randint(jax.random.fold_in(_rk, 8), (8,), 0, max(1, 256 // 4) + 1, jnp.int32)
        cond_2048 = jax.random.bernoulli(jax.random.fold_in(_rk, 11), 0.8975, (8, 512)).astype(jnp.float32)
        return (x, cond_2048)
    x, cond_2048 = _rec_inputs()

    def _L0_cond_setup():
        import jax, jax.numpy as jnp
        import numpy as np
        import math
        D_MODEL = 256
        NUM_HEAD = 16
        NEG_INF = -1e+30
        key = jax.random.key(seed)
        k_x, k_m, k_q, k_k, k_v = jax.random.split(key, 5)
        B, C, T = (4, D_MODEL, 512)
        x = jax.random.normal(k_x, (B, C, T), dtype=jnp.float32)
        mask = (jax.random.uniform(k_m, (B, T)) < 0.9).astype(jnp.float32)
        limit = math.sqrt(6.0 / (C + C))
        Wq = jax.random.uniform(k_q, (C, C), minval=-limit, maxval=limit, dtype=jnp.float32)
        Wk = jax.random.uniform(k_k, (C, C), minval=-limit, maxval=limit, dtype=jnp.float32)
        Wv = jax.random.uniform(k_v, (C, C), minval=-limit, maxval=limit, dtype=jnp.float32)
        b = jnp.zeros((1,), dtype=jnp.float32)
        return {'x': x, 'mask': mask, 'Wq': Wq, 'Wk': Wk, 'Wv': Wv, 'b': b}
    _L0_cond_all = _L0_cond_setup()
    _L0_cond_in = {k: v for k, v in _L0_cond_all.items() if k in ('Wq', 'Wk', 'Wv', 'b')}
    del _L0_cond_all

    def _L0_attn_setup():
        import jax, jax.numpy as jnp
        import numpy as np
        import math
        NUM_HEADS = 16
        HEAVY_RATIO = 0.1
        RECENT_RATIO = 0.1
        ROPE_THETA = 10000.0

        def _rotate_half(x):
            d = x.shape[-1]
            return jnp.concatenate([-x[..., d // 2:], x[..., :d // 2]], axis=-1)

        def _rope(q, k, seq_len, head_dim, dtype):
            inv_freq = 1.0 / ROPE_THETA ** (jnp.arange(0, head_dim, 2, dtype=jnp.float32) / head_dim)
            pos = jnp.arange(seq_len, dtype=jnp.float32)
            freqs = pos[:, None] * inv_freq[None, :]
            emb = jnp.concatenate([freqs, freqs], axis=-1)
            cos = jnp.cos(emb).astype(dtype)[None, None]
            sin = jnp.sin(emb).astype(dtype)[None, None]
            q = q * cos + _rotate_half(q) * sin
            k = k * cos + _rotate_half(k) * sin
            return (q, k)
        key = jax.random.key(seed)
        ks = jax.random.split(key, 5)
        b, s, h = (1, 512, 512)
        return {'hidden_states': jax.random.normal(ks[0], (b, s, h), dtype=jnp.float32), 'Wq': jax.random.normal(ks[1], (h, h), dtype=jnp.float32) * 0.02, 'Wk': jax.random.normal(ks[2], (h, h), dtype=jnp.float32) * 0.02, 'Wv': jax.random.normal(ks[3], (h, h), dtype=jnp.float32) * 0.02, 'Wo': jax.random.normal(ks[4], (h, h), dtype=jnp.float32) * 0.02}
    _L0_attn_all = _L0_attn_setup()
    _L0_attn_in = {k: v for k, v in _L0_attn_all.items() if k in ('Wq', 'Wk', 'Wv', 'Wo')}
    del _L0_attn_all

    def _L0_cond2_setup():
        import jax, jax.numpy as jnp
        import numpy as np
        B, T, D = (16, 128, 512)
        key = jax.random.key(seed)
        k0, k1, k2, k3 = jax.random.split(key, 4)
        scale = 1.0 / np.sqrt(D)
        return {'initial_state': jax.random.normal(k0, (B, D), jnp.float32), 'inputs': jax.random.normal(k1, (B, T, D), jnp.float32), 'W_ih': jax.random.normal(k2, (D, 3 * D), jnp.float32) * scale, 'W_hh': jax.random.normal(k3, (D, 3 * D), jnp.float32) * scale, 'b_ih': jnp.zeros((3 * D,), jnp.float32), 'b_hh': jnp.zeros((3 * D,), jnp.float32)}
    _L0_cond2_all = _L0_cond2_setup()
    _L0_cond2_in = {k: v for k, v in _L0_cond2_all.items() if k in ('W_ih', 'W_hh', 'b_ih', 'b_hh')}
    del _L0_cond2_all

    def _L0_ffn_setup():
        import jax, jax.numpy as jnp
        import numpy as np
        E, TOP_K, D, H = (8, 2, 512, 352)
        B, S = (2, 512)
        key = jax.random.key(seed)
        ks = jax.random.split(key, 8)
        x = jax.random.normal(ks[0], (B, S, D), dtype=jnp.float32)
        gate_w = jax.random.normal(ks[1], (E, D), dtype=jnp.float32) * (1.0 / np.sqrt(D))
        gate_b = jax.random.normal(ks[2], (E,), dtype=jnp.float32) * 0.01
        bias = jnp.zeros((E,), dtype=jnp.float32)
        w1 = jax.random.normal(ks[3], (E, H, D), dtype=jnp.float32) * (1.0 / np.sqrt(D))
        b1 = jax.random.normal(ks[4], (E, H), dtype=jnp.float32) * 0.01
        w2 = jax.random.normal(ks[5], (E, D, H), dtype=jnp.float32) * (1.0 / np.sqrt(H))
        b2 = jax.random.normal(ks[6], (E, D), dtype=jnp.float32) * 0.01
        return {'x': x, 'gate_w': gate_w, 'gate_b': gate_b, 'bias': bias, 'w1': w1, 'b1': b1, 'w2': w2, 'b2': b2}
    _L0_ffn_all = _L0_ffn_setup()
    _L0_ffn_in = {k: v for k, v in _L0_ffn_all.items() if k in ('gate_w', 'gate_b', 'bias', 'w1', 'b1', 'w2', 'b2')}
    del _L0_ffn_all
    return {'x': x, 'cond_2048': cond_2048, 'L0_cond_Wq': _L0_cond_in['Wq'], 'L0_cond_Wk': _L0_cond_in['Wk'], 'L0_cond_Wv': _L0_cond_in['Wv'], 'L0_cond_b': _L0_cond_in['b'], 'L0_attn_Wq': _L0_attn_in['Wq'], 'L0_attn_Wk': _L0_attn_in['Wk'], 'L0_attn_Wv': _L0_attn_in['Wv'], 'L0_attn_Wo': _L0_attn_in['Wo'], 'L0_cond2_W_ih': _L0_cond2_in['W_ih'], 'L0_cond2_W_hh': _L0_cond2_in['W_hh'], 'L0_cond2_b_ih': _L0_cond2_in['b_ih'], 'L0_cond2_b_hh': _L0_cond2_in['b_hh'], 'L0_ffn_gate_w': _L0_ffn_in['gate_w'], 'L0_ffn_gate_b': _L0_ffn_in['gate_b'], 'L0_ffn_bias': _L0_ffn_in['bias'], 'L0_ffn_w1': _L0_ffn_in['w1'], 'L0_ffn_b1': _L0_ffn_in['b1'], 'L0_ffn_w2': _L0_ffn_in['w2'], 'L0_ffn_b2': _L0_ffn_in['b2']}

def reference(x, cond_2048, L0_cond_Wq, L0_cond_Wk, L0_cond_Wv, L0_cond_b, L0_attn_Wq, L0_attn_Wk, L0_attn_Wv, L0_attn_Wo, L0_cond2_W_ih, L0_cond2_W_hh, L0_cond2_b_ih, L0_cond2_b_hh, L0_ffn_gate_w, L0_ffn_gate_b, L0_ffn_bias, L0_ffn_w1, L0_ffn_b1, L0_ffn_w2, L0_ffn_b2):
    import jax
    import jax.numpy as jnp

    def _L0_cond_ref(x, mask, Wq, Wk, Wv, b):
        import jax, jax.numpy as jnp
        import numpy as np
        import math
        D_MODEL = 256
        NUM_HEAD = 16
        NEG_INF = -1e+30
        B, C, T = x.shape
        H = NUM_HEAD
        Dh = C // H

        def proj(W):
            y = jnp.einsum('oc,bct->bto', W, x)
            return y.reshape(B, T, H, Dh).transpose(0, 2, 1, 3)
        Q, K, V = (proj(Wq), proj(Wk), proj(Wv))
        att = jnp.einsum('bhqd,bhkd->bhqk', Q, K) * (1.0 / math.sqrt(Dh))
        att = att + b[0]
        m = mask[:, None, None, :]
        att = att * m + (1.0 - m) * NEG_INF
        att = jax.nn.softmax(att, axis=-1)
        y = jnp.einsum('bhqk,bhkd->bhqd', att, V)
        y = y.transpose(0, 2, 1, 3).reshape(B, T, C)
        return y.transpose(0, 2, 1)

    def _L0_attn_ref(hidden_states, Wq, Wk, Wv, Wo):
        import jax, jax.numpy as jnp
        import numpy as np
        import math
        NUM_HEADS = 16
        HEAVY_RATIO = 0.1
        RECENT_RATIO = 0.1
        ROPE_THETA = 10000.0

        def _rotate_half(x):
            d = x.shape[-1]
            return jnp.concatenate([-x[..., d // 2:], x[..., :d // 2]], axis=-1)

        def _rope(q, k, seq_len, head_dim, dtype):
            inv_freq = 1.0 / ROPE_THETA ** (jnp.arange(0, head_dim, 2, dtype=jnp.float32) / head_dim)
            pos = jnp.arange(seq_len, dtype=jnp.float32)
            freqs = pos[:, None] * inv_freq[None, :]
            emb = jnp.concatenate([freqs, freqs], axis=-1)
            cos = jnp.cos(emb).astype(dtype)[None, None]
            sin = jnp.sin(emb).astype(dtype)[None, None]
            q = q * cos + _rotate_half(q) * sin
            k = k * cos + _rotate_half(k) * sin
            return (q, k)
        b, s, hidden = hidden_states.shape
        H = NUM_HEADS
        d = hidden // H

        def proj(W):
            return (hidden_states @ W.T).reshape(b, s, H, d).transpose(0, 2, 1, 3)
        q, k, v = (proj(Wq), proj(Wk), proj(Wv))
        q, k = _rope(q, k, s, d, hidden_states.dtype)
        scores = jnp.einsum('bhqd,bhkd->bhqk', q, k) / math.sqrt(d)
        neg = jnp.finfo(scores.dtype).min
        i = jnp.arange(s)[:, None]
        j = jnp.arange(s)[None, :]
        causal = jnp.where(j <= i, jnp.array(0.0, scores.dtype), neg)
        scores = jnp.maximum(scores + causal, neg)
        heavy_budget = int(HEAVY_RATIO * s)
        recent_budget = int(RECENT_RATIO * s)
        tmp_attn = jax.nn.softmax(scores.astype(jnp.float32), axis=-1).astype(scores.dtype)
        tmp_sum = jnp.sum(tmp_attn, axis=-2)
        _, topk_idx = jax.lax.top_k(tmp_sum, heavy_budget)
        heavy_mask = jnp.any(topk_idx[..., :, None] == jnp.arange(s)[None, None, None, :], axis=-2)
        band = jnp.abs(i - j) <= recent_budget
        mask = heavy_mask[:, :, None, :] | band[None, None]
        scores = jnp.where(mask, scores, neg)
        probs = jax.nn.softmax(scores.astype(jnp.float32), axis=-1).astype(q.dtype)
        attn = jnp.einsum('bhqk,bhkd->bhqd', probs, v)
        attn = attn.transpose(0, 2, 1, 3).reshape(b, s, hidden)
        return attn @ Wo.T

    def _L0_cond2_ref(initial_state, inputs, W_ih, W_hh, b_ih, b_hh):
        import jax, jax.numpy as jnp
        import numpy as np
        B, T, D = (16, 128, 512)
        "ScanOverTime(GRU cell): sequential per-timestep module call with\n            dict-state passing; merge_dict_trees stacks the per-step\n            'state_predicted' tensors along axis=1 -> [B, T, D]."

        def cell(h, x):
            gi = x @ W_ih + b_ih
            gh = h @ W_hh + b_hh
            i_r, i_z, i_n = jnp.split(gi, 3, axis=-1)
            h_r, h_z, h_n = jnp.split(gh, 3, axis=-1)
            r = jax.nn.sigmoid(i_r + h_r)
            z = jax.nn.sigmoid(i_z + h_z)
            n = jnp.tanh(i_n + r * h_n)
            h_new = (1.0 - z) * n + z * h
            return (h_new, h_new)
        xs = jnp.swapaxes(inputs, 0, 1)
        _, hs = jax.lax.scan(cell, initial_state, xs)
        return jnp.swapaxes(hs, 0, 1)

    def _L0_ffn_ref(x, gate_w, gate_b, bias, w1, b1, w2, b2):
        import jax, jax.numpy as jnp
        import numpy as np
        E, TOP_K, D, H = (8, 2, 512, 352)
        B, S = (2, 512)
        b, s, d = x.shape
        xf = x.reshape(-1, d)
        scores = xf @ gate_w.T + gate_b + bias
        top_scores, top_idx = jax.lax.top_k(scores, TOP_K)
        gates = jax.nn.softmax(top_scores, axis=-1)
        comb = jnp.sum(jax.nn.one_hot(top_idx, E, dtype=gates.dtype) * gates[..., None], axis=1)
        h = jax.nn.silu(jnp.einsum('td,ehd->teh', xf, w1) + b1)
        y = jnp.einsum('teh,edh->ted', h, w2) + b2
        out = jnp.einsum('ted,te->td', y, comb)
        return out.reshape(b, s, d)
    x = x + _L0_attn_ref(_L0_cond_ref(x, cond_2048, L0_cond_Wq, L0_cond_Wk, L0_cond_Wv, L0_cond_b), L0_attn_Wq, L0_attn_Wk, L0_attn_Wv, L0_attn_Wo)
    x = x + _L0_ffn_ref(_L0_cond2_ref(cond_2048, x, L0_cond2_W_ih, L0_cond2_W_hh, L0_cond2_b_ih, L0_cond2_b_hh), L0_ffn_gate_w, L0_ffn_gate_b, L0_ffn_bias, L0_ffn_w1, L0_ffn_b1, L0_ffn_w2, L0_ffn_b2)
    return x

_drawn_inputs = setup_inputs


def setup_inputs(seed=0):
    import zlib

    import numpy as np

    out = dict(_drawn_inputs(seed))
    spreads = {'L0_cond2_b_ih': (0.0, 0.39), 'L0_cond2_b_hh': (0.0, 0.384), 'L0_ffn_bias': (0.0, 0.1)}
    factors = {'cond_2048': 4.037,
     'L0_cond_Wq': 6.267,
     'L0_cond_Wk': 5.752,
     'L0_cond_Wv': 6.202,
     'L0_attn_Wq': 8.0,
     'L0_attn_Wk': 8.0,
     'L0_attn_Wv': 5.785,
     'L0_attn_Wo': 6.358,
     'L0_ffn_gate_b': 12.611,
     'L0_ffn_b1': 38.665,
     'L0_ffn_b2': 22.497}
    for name, (base, spread) in spreads.items():
        noise = np.random.default_rng([zlib.crc32(name.encode()), seed]).standard_normal(out[name].shape)
        drawn = base * np.exp(spread * noise) if base else spread * noise
        out[name] = jnp.asarray(drawn.astype(out[name].dtype))
    for name, factor in factors.items():
        out[name] = (out[name] * factor).astype(out[name].dtype)
    return out
```

```python
from contextlib import ExitStack

import concourse.bass as bass
from concourse import mybir

F32 = mybir.dt.float32
F16 = mybir.dt.float16
BF16 = mybir.dt.bfloat16
I32 = mybir.dt.int32
ALU = mybir.AluOpType
ACT = mybir.ActivationFunctionType
AX = mybir.AxisListType

P = 128
B, S, D = 8, 256, 512
KD = D // P
KS = S // P
NH = 16
DH1 = S // NH
DH2 = D // NH
HPC = P // DH2
NEG = -1e30
HEAVY = int(0.1 * S)
RECENT = int(0.1 * S)
G3 = 3 * D
NQ = G3 // P
NE, HF = 8, 352
TOK = B * S
FC = (HF + P - 1) // P
HL = HF - (FC - 1) * P
TT = 512

C_ID = 0
C_ROT = C_ID + P
C_CAUS = C_ROT + P
C_NB0 = C_CAUS + P
C_NB1 = C_NB0 + P
C_COSQ = C_NB1 + P
C_SINQ = C_COSQ + S
C_COSK = C_SINQ + S
C_SINK = C_COSK + S
C_HEAD = C_SINK + S
C_SEL = C_HEAD + HPC
C_DESC = C_SEL + B * P
C_ALL = C_DESC + S


def program(nc, ins, out):
    ctx = ExitStack()
    with ctx:
        def sb(stack, name, shape, dt=F32):
            return stack.enter_context(nc.sbuf_tensor(name, shape, dt))

        def sem(stack, name):
            return stack.enter_context(nc.semaphore(name))

        ps = ctx.enter_context(nc.psum_tensor("ps", [P, 8, 512], F32))
        cst = sb(ctx, "cst", [P, C_ALL])
        x1T = sb(ctx, "x1T", [P, KD, S, B])
        ident = cst[:, C_ID:C_ID + P]

        att = ExitStack()
        with att:
            hT = sb(att, "hT", [P, KD, B, S])
            first_attention_uniform_and_general(nc, ins, ps, cst, ident, x1T, hT, sb, sem)
            second_attention(nc, ins, ps, cst, ident, x1T, hT, sb, sem)
        gru_and_ffn(nc, ins, out, ps, cst, ident, x1T, sb, sem)


def first_attention_uniform_and_general(nc, ins, ps, cst, ident, x1T, hT, sb, sem):
    st = ExitStack()
    with st:
        xall = sb(st, "xall", [P, KS, B, D])
        wv = sb(st, "wv", [P, KS, S])
        mask = sb(st, "mask", [B, D])
        b0 = sb(st, "b0", [B, 1])
        pen = sb(st, "pen", [B, D])
        top = sb(st, "top", [B, 1])
        zf = sb(st, "zf", [B, 1])
        wm = sb(st, "wm", [B, D])
        cnt = sb(st, "cnt", [B, 1])
        rcnt = sb(st, "rcnt", [B, 1])
        bz = sb(st, "bz", [B, 1])
        bias = sb(st, "bias", [B, D])
        ksc = sb(st, "ksc", [B, D])
        xw = sb(st, "xw", [P, KS, B])
        junk = sb(st, "junk", [P, D])
        ones = sb(st, "ones", [P, P])
        xwb = sb(st, "xwb", [P, KS, B, P])
        flag = sb(st, "flag", [1, 1], I32)
        scr_bias = nc.dram_tensor("scr_bias", [B, D], F32).ap()
        scr_ksc = nc.dram_tensor("scr_ksc", [B, D], F32).ap()

        d_mask = sem(st, "d_mask")
        d_cst = sem(st, "d_cst")
        d_x = sem(st, "d_x")
        d_xT = sem(st, "d_xT")
        d_wv = sem(st, "d_wv")
        d_scr = sem(st, "d_scr")
        v_step = sem(st, "v_step")
        v_ones = sem(st, "v_ones")
        v_w = sem(st, "v_w")
        v_rows = sem(st, "v_rows")
        p_w = sem(st, "p_w")
        v_xw = sem(st, "v_xw")
        v_xwb = sem(st, "v_xwb")
        p_y = sem(st, "p_y")
        a_hT = sem(st, "a_hT")
        p_flag = sem(st, "p_flag")

        with nc.Block() as block:
            @block.sync
            def _(sp):
                sp.dma_start(mask[:, :], ins["cond"]).then_inc(d_mask, 16)
                sp.dma_start(b0[:, :], ins["cond_b"]).then_inc(d_mask, 16)
                sp.dma_start(cst[:, :], ins["consts"]).then_inc(d_cst, 16)
                for k in range(KS):
                    for b in range(0, B, 4):
                        sp.dma_start(xall[:, k, b:b + 4, :],
                                     ins["x"][b:b + 4, k * P:(k + 1) * P, :].rearrange("b p t -> p b t"))\
                            .then_inc(d_x, 16)
                sp.dma_start(wv[:, :, :], ins["cond_WvT"].rearrange("(k p) o -> p k o", p=P)).then_inc(d_wv, 16)
                sp.dma_start(x1T[:, :, :, :].rearrange("p k s b -> p k (s b)"),
                             ins["xT"].rearrange("(k p) n -> p k n", p=P)).then_inc(d_xT, 16)
                sp.wait_ge(v_rows, 2)
                sp.dma_start(scr_bias, bias[:, :]).then_inc(d_scr, 16)
                sp.dma_start(scr_ksc, ksc[:, :]).then_inc(d_scr, 16)
                sp.wait_ge(d_scr, 32)
                sp.wait_ge(d_xT, 16)

            @block.vector
            def _(dve):
                n = [0]

                def step(ins_):
                    n[0] += 1
                    ins_.then_inc(v_step, 1)
                    dve.wait_ge(v_step, n[0])

                nc.vector.memset(ones[:, :], 1.0).then_inc(v_ones, 1)
                dve.wait_ge(d_mask, 32)
                step(nc.vector.tensor_scalar(pen[:, :], mask[:, :], -1.0, 1.0, ALU.mult, ALU.add))
                step(nc.vector.tensor_scalar(pen[:, :], pen[:, :], NEG, None, ALU.mult))
                step(nc.vector.tensor_reduce(top[:, :], pen[:, :], AX.X, ALU.max))
                step(nc.vector.tensor_scalar(wm[:, :], pen[:, :], top[:, 0:1], None, ALU.is_equal))
                step(nc.vector.tensor_reduce(cnt[:, :], wm[:, :], AX.X, ALU.add))
                step(nc.vector.reciprocal(rcnt[:, :], cnt[:, :]))
                nc.vector.tensor_scalar(wm[:, :], wm[:, :], rcnt[:, 0:1], None, ALU.mult).then_inc(v_w, 1)
                step(nc.vector.tensor_scalar(zf[:, :], top[:, :], 0.0, None, ALU.is_equal))
                step(nc.vector.tensor_tensor(bz[:, :], b0[:, :], zf[:, :], ALU.mult))
                step(nc.vector.tensor_scalar(pen[:, :], pen[:, :], top[:, 0:1], None, ALU.subtract))
                nc.vector.scalar_tensor_tensor(out=bias[:, :], in0=mask[:, :], scalar=bz[:, 0:1],
                                               in1=pen[:, :], op0=ALU.mult, op1=ALU.add).then_inc(v_rows, 1)
                nc.vector.tensor_scalar(ksc[:, :], mask[:, :], zf[:, 0:1], DH1 ** -0.5, ALU.mult, ALU.mult)\
                    .then_inc(v_rows, 1)
                dve.wait_ge(d_x, 16 * 2 * KS)
                for b in range(B):
                    dve.wait_ge(p_w, b + 1)
                    for k in range(KS):
                        step(nc.vector.tensor_tensor_reduce(junk[:, :], xall[:, k, b, :], ps[:, b, :], 1.0, 0.0,
                                                            ALU.mult, ALU.add, xw[:, k, b:b + 1]))
                for b in range(B):
                    for k in range(KS):
                        nc.vector.tensor_scalar(xwb[:, k, b, :], ones[:, :], xw[:, k, b:b + 1], None, ALU.mult)\
                            .then_inc(v_xwb, 1)
                dve.wait_ge(p_flag, 1)
                nc.vector.tensor_copy(flag[:, :], ps[0:1, 7, 0:1]).then_inc(v_step, 1)
                dve.wait_ge(v_step, n[0] + 1)

            @block.tensor
            def _(pe):
                pe.wait_ge(v_w, 1)
                pe.wait_ge(d_cst, 16)
                for b in range(B):
                    nc.tensor.matmul(ps[:, b, :], cst[0:B, C_SEL + b * P:C_SEL + (b + 1) * P], wm[:, :],
                                     start=True, stop=True).then_inc(p_w, 1)
                pe.wait_ge(d_wv, 16)
                pe.wait_ge(v_xwb, B * KS)
                for b in range(B):
                    bank = b % 4
                    if b >= 4:
                        pe.wait_ge(a_hT, KD * (b - 3))
                    for k in range(KS):
                        last = nc.tensor.matmul(ps[:, bank, 0:S], xwb[:, k, b, :], wv[:, k, :],
                                                start=(k == 0), stop=(k == KS - 1))
                    last.then_inc(p_y, 1)
                nc.tensor.matmul(ps[0:1, 7, 0:1], zf[:, :], ones[0:B, 0:1], start=True, stop=True)\
                    .then_inc(p_flag, 1)

            @block.scalar
            def _(act):
                for b in range(B):
                    act.wait_ge(p_y, b + 1)
                    for t in range(KD):
                        nc.scalar.activation(hT[:, t, b, :], ps[:, b % 4, 0:S], ACT.Copy).then_inc(a_hT, 1)
                act.wait_ge(a_hT, B * KD)

        general = ExitStack()
        with general:
            wh = sb(general, "g_wh", [P, KS, 3, DH1])
            gbias = sb(general, "g_bias", [1, D])
            gks = sb(general, "g_ks", [DH1, D])
            qh = sb(general, "g_q", [DH1, D])
            kh = sb(general, "g_k", [DH1, D])
            vh = sb(general, "g_v", [DH1, D])
            vT = sb(general, "g_vT", [P, KD, DH1])
            nmax = sb(general, "g_nmax", [P, KD])
            lsum = sb(general, "g_lsum", [P, KD])
            rl = sb(general, "g_rl", [P, KD])
            e = sb(general, "g_e", [P, D])
            eT = sb(general, "g_eT", [P, KD, P])
            g_in = sem(general, "g_in")
            g_proj = sem(general, "g_proj")
            g_qkv = sem(general, "g_qkv")
            g_vt = sem(general, "g_vt")
            g_vs = sem(general, "g_vs")
            g_s = sem(general, "g_s")
            g_m = sem(general, "g_m")
            g_e = sem(general, "g_e")
            g_t = sem(general, "g_t")
            g_ts = sem(general, "g_ts")
            g_o = sem(general, "g_o")
            g_r = sem(general, "g_r")
            g_done = sem(general, "g_done")

            with nc.Block() as block:
                @block.sync
                def _(sp):
                    go = sp.value_load(flag[0:1, 0:1], min_val=0, max_val=B)
                    with sp.If(go > 0):
                        with sp.Fori(0, B) as b:
                            with sp.Fori(0, NH) as h:
                                n = b * NH + h
                                sp.wait_ge(g_done, n * KD + 1)
                                sp.dma_start(wh[:, :, :, :],
                                             ins["cond_Wh"][bass.ds(h, 1)].rearrange("a p k w d -> p (a k) w d"))\
                                    .then_inc(g_in, 16)
                                sp.dma_start(gbias[:, :], scr_bias[bass.ds(b, 1), :]).then_inc(g_in, 16)
                                sp.dma_start(gks[:, :], scr_ksc[bass.ds(b, 1), :].broadcast_to((DH1, D)))\
                                    .then_inc(g_in, 16)

                @block.tensor
                def _(pe):
                    go = pe.value_load(flag[0:1, 0:1], min_val=0, max_val=B)
                    with pe.If(go > 0):
                        with pe.Fori(0, B) as b:
                            with pe.Fori(0, NH) as h:
                                n = b * NH + h
                                pe.wait_ge(g_in, (n + 1) * 48)
                                for w in range(3):
                                    for k in range(KS):
                                        last = nc.tensor.matmul(
                                            ps[0:DH1, w, :], wh[:, k, w, :],
                                            xall[:, k, bass.ds(b, 1), :].rearrange("p a t -> p (a t)"),
                                            start=(k == 0), stop=(k == KS - 1))
                                last.then_inc(g_proj, 1)
                                pe.wait_ge(g_qkv, (n + 1) * 3)
                                for t in range(KD):
                                    last = nc.tensor.matmul(ps[:, 3, t * DH1:(t + 1) * DH1],
                                                            vh[:, t * P:(t + 1) * P], ident[0:DH1, 0:DH1],
                                                            start=True, stop=True)
                                last.then_inc(g_vt, 1)
                                for q in range(KD):
                                    nq = n * KD + q
                                    pe.wait_ge(g_e, nq + 1)
                                    nc.tensor.matmul(ps[:, 4, :], qh[:, q * P:(q + 1) * P], kh[:, :],
                                                     start=True, stop=False)
                                    nc.tensor.matmul(ps[:, 4, :], ones[0:1, :], gbias[:, :],
                                                     start=False, stop=True).then_inc(g_s, 1)
                                    pe.wait_ge(g_e, nq + 2)
                                    for t in range(KD):
                                        last = nc.tensor.transpose(ps[:, 5, t * P:(t + 1) * P],
                                                                   e[:, t * P:(t + 1) * P], ident)
                                    last.then_inc(g_t, 1)
                                    pe.wait_ge(g_ts, nq + 1)
                                    pe.wait_ge(g_vs, n + 1)
                                    for t in range(KD):
                                        last = nc.tensor.matmul(ps[:, 6, 0:DH1], eT[:, t, :], vT[:, t, :],
                                                                start=(t == 0), stop=(t == KD - 1))
                                    last.then_inc(g_o, 1)
                                pe.wait_ge(g_done, (n + 1) * KD + 1)

                @block.vector
                def _(dve):
                    go = dve.value_load(flag[0:1, 0:1], min_val=0, max_val=B)
                    with dve.If(go > 0):
                        dve.nop().then_inc(g_done, 1)
                        with dve.Fori(0, B) as b:
                            with dve.Fori(0, NH) as h:
                                n = b * NH + h
                                dve.wait_ge(g_proj, n + 1)
                                nc.vector.tensor_copy(qh[:, :], ps[0:DH1, 0, :]).then_inc(g_qkv, 1)
                                nc.vector.tensor_tensor(kh[:, :], ps[0:DH1, 1, :], gks[:, :], ALU.mult)\
                                    .then_inc(g_qkv, 1)
                                nc.vector.tensor_copy(vh[:, :], ps[0:DH1, 2, :]).then_inc(g_qkv, 1)
                                dve.wait_ge(g_vt, n + 1)
                                nc.vector.tensor_copy(vT[:, :, :].rearrange("p t d -> p (t d)"),
                                                      ps[:, 3, 0:KD * DH1]).then_inc(g_vs, 1)
                                for q in range(KD):
                                    nq = n * KD + q
                                    dve.wait_ge(g_s, nq + 1)
                                    nc.vector.tensor_reduce(nmax[:, q:q + 1], ps[:, 4, :], AX.X, ALU.max,
                                                            negate=True).then_inc(g_m, 1)
                                    dve.wait_ge(g_t, nq + 1)
                                    nc.vector.tensor_copy(eT[:, :, :].rearrange("p t d -> p (t d)"), ps[:, 5, :])\
                                        .then_inc(g_ts, 1)
                                    dve.wait_ge(g_e, nq + 2)
                                    nc.vector.reciprocal(rl[:, q:q + 1], lsum[:, q:q + 1]).then_inc(g_r, 1)
                                    dve.wait_ge(g_r, nq + 1)
                                    dve.wait_ge(g_o, nq + 1)
                                    nc.vector.tensor_scalar(
                                        hT[:, q, bass.ds(b, 1), bass.ds(h * DH1, DH1)].rearrange("p a d -> p (a d)"),
                                        ps[:, 6, 0:DH1], rl[:, q:q + 1], None, ALU.mult).then_inc(g_done, 1)

                @block.scalar
                def _(act):
                    go = act.value_load(flag[0:1, 0:1], min_val=0, max_val=B)
                    with act.If(go > 0):
                        act.nop().then_inc(g_e, 1)
                        with act.Fori(0, B) as b:
                            with act.Fori(0, NH) as h:
                                n = b * NH + h
                                for q in range(KD):
                                    nq = n * KD + q
                                    act.wait_ge(g_m, nq + 1)
                                    nc.scalar.activation(e[:, :], ps[:, 4, :], ACT.Exp, bias=nmax[:, q:q + 1],
                                                         accum_out=lsum[:, q:q + 1]).then_inc(g_e, 1)


def second_attention(nc, ins, ps, cst, ident, x1T, hT, sb, sem):
    st = ExitStack()
    with st:
        wq = sb(st, "wq", [P, KD, D])
        wk = sb(st, "wk", [P, KD, D])
        wv = sb(st, "wv2", [P, KD, D])
        wo = sb(st, "wo", [P, KD, D])
        masks = sb(st, "masks", [P, 4, P], BF16)
        hb = sb(st, "hb", [P, KD, S])
        raw = sb(st, "raw", [P, 2, KD, S])
        rot = sb(st, "rot", [P, 2, KD, S])
        kz = sb(st, "kz", [P, HPC, KD, S])
        v = sb(st, "v", [P, KS, D])
        tmp = sb(st, "tmp", [P, KD, S])
        E = sb(st, "E", [P, 2, P + S])
        En = sb(st, "En", [P, 2, P + S])
        ET = sb(st, "ET", [P, HPC, P + S])
        nm = sb(st, "nm", [P, 2, NH, 2])
        ls = sb(st, "ls", [P, 2, NH, 2])
        rl = sb(st, "rl", [P, 2, NH, 2])
        rdiag = sb(st, "rdiag", [P, NH, 2, NH])
        tsum = sb(st, "tsum", [NH, S])
        work = sb(st, "work", [NH, S])
        top8 = sb(st, "top8", [NH, 8])
        code = sb(st, "code", [NH, S])
        cmax = sb(st, "cmax", [NH, 1])
        light = sb(st, "light", [NH, S])
        lcol = sb(st, "lcol", [P, KS, NH])
        dg = sb(st, "dg", [P, 2, KS, P], BF16)
        oT = sb(st, "oT", [P, KD, S])

        d_w = sem(st, "e_w")
        v_init = sem(st, "e_init")
        c_hb = sem(st, "c_hb")
        p_qk = sem(st, "p_qk")
        a_raw = sem(st, "a_raw")
        p_rot = sem(st, "p_rot")
        v_rot = sem(st, "v_rot")
        a_kz = sem(st, "a_kz")
        p_v = sem(st, "p_v")
        a_v = sem(st, "a_v")
        p_s = sem(st, "p_s")
        v_m = sem(st, "v_m")
        a_e = sem(st, "a_e")
        v_r = sem(st, "v_r")
        v_d = sem(st, "v_d")
        p_c = sem(st, "p_c")
        v_k = sem(st, "v_k")
        p_l = sem(st, "p_l")
        v_l = sem(st, "v_l")
        g_d = sem(st, "g_d")
        v_n = sem(st, "v_n")
        p_t = sem(st, "p_t")
        a_t = sem(st, "a_t")
        p_av = sem(st, "p_av")
        a_o = sem(st, "a_o")
        p_o = sem(st, "p_o")
        v_x = sem(st, "v_x")

        with nc.Block() as block:
            @block.sync
            def _(sp):
                for t, name in ((wq, "attn_WqT"), (wk, "attn_WkT"), (wv, "attn_WvT"), (wo, "attn_WoT")):
                    sp.dma_start(t[:, :, :], ins[name].rearrange("(k p) o -> p k o", p=P)).then_inc(d_w, 16)

            @block.gpsimd
            def _(pool):
                with pool.Fori(0, B) as b:
                    pool.wait_ge(p_v, b + 1)
                    nc.gpsimd.tensor_copy(hb[:, :, :], hT[:, :, bass.ds(b, 1), :].rearrange("p k a s -> p k (a s)"))\
                        .then_inc(c_hb, 1)

            @block.tensor
            def _(pe):
                pe.nop().then_inc(p_v, 1)
                pe.nop().then_inc(p_s, 1)
                pe.wait_ge(d_w, 64)
                pe.wait_ge(v_init, 3)

                def scores(b, r, h):
                    n = b * (2 * NH) + r * NH + h
                    bank = h % 4
                    m, q = h // HPC, h % HPC
                    if r == 0 and h < 4:
                        if h == 0:
                            pe.wait_ge(v_x, b * KD + 1)
                    else:
                        pe.wait_ge(a_e, (n - 4 + 1) * 2)
                    if r == 0 and h == 0:
                        pe.wait_ge(a_kz, (b + 1) * HPC + 1)
                        pe.wait_ge(v_rot, b * 6 + 6)
                    kw = dict(stop=False, skip_group_check=True)
                    nc.tensor.matmul(ps[:, bank, 0:P], masks[:, 0, :], masks[:, 1, :], start=True, **kw)
                    nc.tensor.matmul(ps[:, bank, 2 * P:3 * P], masks[:, 0, :], masks[:, 1, :], start=False, **kw)
                    if r == 1:
                        pe.wait_ge(g_d, (b * NH + h + 1) * KS)
                        d = dg[:, h % 2, :, :]
                        nc.tensor.matmul(ps[:, bank, 0:P], masks[:, 2, :], d[:, 0, :], start=False, **kw)
                        nc.tensor.matmul(ps[:, bank, P:2 * P], masks[:, 3, :], d[:, 0, :], start=False, **kw)
                        nc.tensor.matmul(ps[:, bank, 2 * P:3 * P], masks[:, 2, :], d[:, 1, :], start=False, **kw)
                    nc.tensor.matmul(ps[:, bank, 0:P], rot[:, 0, m, 0:P], kz[:, q, m, 0:P],
                                     start=False, stop=True, skip_group_check=True)
                    nc.tensor.matmul(ps[:, bank, P:P + S], rot[:, 0, m, P:S], kz[:, q, m, :],
                                     start=False, stop=True, skip_group_check=True).then_inc(p_s, 1)

                with pe.Fori(0, B) as b:
                    pe.wait_ge(c_hb, b + 1)
                    pe.wait_ge(v_x, b * KD + 1)
                    for i, w in enumerate((wq, wk)):
                        for m in range(KD):
                            for k in range(KD):
                                last = nc.tensor.matmul(ps[:, 2 * i + m // 2, (m % 2) * S:(m % 2 + 1) * S],
                                                        w[:, k, m * P:(m + 1) * P], hb[:, k, :],
                                                        start=(k == 0 and m % 2 == 0), stop=(k == KD - 1),
                                                        skip_group_check=True)
                        last.then_inc(p_qk, 1)
                    for i in range(2):
                        pe.wait_ge(a_raw, b * 2 + i + 1)
                        for m in range(KD):
                            last = nc.tensor.matmul(ps[:, 4 + 2 * i + m // 2, (m % 2) * S:(m % 2 + 1) * S],
                                                    cst[:, C_ROT:C_ROT + P], raw[:, i, m, :],
                                                    start=(m % 2 == 0), stop=True, skip_group_check=True)
                        last.then_inc(p_rot, 1)
                    for c in range(KS):
                        for k in range(KD):
                            last = nc.tensor.matmul(ps[:, c, :], hb[:, k, c * P:(c + 1) * P], wv[:, k, :],
                                                    start=(k == 0), stop=(k == KD - 1))
                    last.then_inc(p_v, 1)
                    pe.wait_ge(a_v, b + 1)
                    for h in range(NH + 1):
                        if h < NH:
                            scores(b, 0, h)
                        if h >= 1:
                            g = h - 1
                            pe.wait_ge(v_d, b * NH + g + 1)
                            nc.tensor.matmul(ps[0:NH, 4, 0:P], rdiag[:, g, 0, :], E[:, g % 2, 0:P],
                                             start=(g == 0), stop=False, skip_group_check=True)
                            nc.tensor.matmul(ps[0:NH, 4, 0:S], rdiag[:, g, 1, :], E[:, g % 2, P:P + S],
                                             start=False, stop=(g == NH - 1),
                                             skip_group_check=True).then_inc(p_c, 1)
                    pe.wait_ge(v_k, b * K_STEPS + K_STEPS)
                    for c in range(KS):
                        last = nc.tensor.matmul(ps[:, 5, c * NH:(c + 1) * NH], light[:, c * P:(c + 1) * P],
                                                ident[0:NH, 0:NH], start=True, stop=True)
                    last.then_inc(p_l, 1)
                    for h in range(NH + 2):
                        if h < NH:
                            scores(b, 1, h)
                        g = h - 1
                        if 0 <= g < NH:
                            n = b * NH + g
                            pe.wait_ge(v_n, (n + 1) * 2 + 1)
                            if g < 2:
                                if g == 0:
                                    pe.wait_ge(v_l, b + 1)
                            else:
                                pe.wait_ge(a_t, n - 1)
                            bank = 4 + g % 2
                            for c in range(3):
                                last = nc.tensor.transpose(ps[:, bank, c * P:(c + 1) * P],
                                                           En[:, g % 2, c * P:(c + 1) * P], ident)
                            last.then_inc(p_t, 1)
                        g = h - 2
                        if g >= 0 and g % HPC == HPC - 1:
                            m = g // HPC
                            pe.wait_ge(a_t, b * NH + g + 1)
                            if m >= 2:
                                pe.wait_ge(a_o, b * KD + m - 1)
                            for q in range(HPC):
                                hh = m * HPC + q
                                o = ps[q * DH2:(q + 1) * DH2, 6 + m % 2, :]
                                nc.tensor.matmul(o[:, 0:S], v[:, 0, hh * DH2:(hh + 1) * DH2], ET[:, q, 0:S],
                                                 start=True, stop=False, tile_position=(0, q * DH2),
                                                 skip_group_check=True)
                                last = nc.tensor.matmul(o[:, P:S], v[:, 1, hh * DH2:(hh + 1) * DH2], ET[:, q, S:S + P],
                                                        start=False, stop=True, tile_position=(0, q * DH2),
                                                        skip_group_check=True)
                            last.then_inc(p_av, 1)
                    pe.wait_ge(a_o, (b + 1) * KD)
                    for m in range(KD):
                        for k in range(KD):
                            last = nc.tensor.matmul(ps[:, m, 0:S], wo[:, k, m * P:(m + 1) * P], oT[:, k, :],
                                                    start=(k == 0), stop=(k == KD - 1))
                        last.then_inc(p_o, 1)

            @block.scalar
            def _(act):
                def exps(b, r, h):
                    n = b * (2 * NH) + r * NH + h
                    act.wait_ge(v_m, n + 1)
                    if r == 0:
                        if h >= 2:
                            act.wait_ge(p_c, b * NH + h - 1)
                        else:
                            act.wait_ge(v_n, b * (2 * NH) + 1)
                    else:
                        if h >= 2:
                            act.wait_ge(v_n, (b * NH + h - 1) * 2 + 1)
                        else:
                            act.wait_ge(p_c, (b + 1) * NH)
                    bank = h % 4
                    nc.scalar.activation(E[:, h % 2, 0:P], ps[:, bank, 0:P], ACT.Exp, bias=nm[:, r, h, 0:1],
                                         accum_out=ls[:, r, h, 0:1]).then_inc(a_e, 1)
                    nc.scalar.activation(E[:, h % 2, P:P + S], ps[:, bank, P:P + S], ACT.Exp,
                                         bias=nm[:, r, h, 1:2], accum_out=ls[:, r, h, 1:2]).then_inc(a_e, 1)

                act.nop().then_inc(a_kz, 1)
                with act.Fori(0, B) as b:
                    for i in range(2):
                        act.wait_ge(p_qk, b * 2 + i + 1)
                        nc.scalar.activation(raw[:, i, :, :].rearrange("p m s -> p (m s)"),
                                             ps[:, 2 * i:2 * i + 2, :].rearrange("p a n -> p (a n)"),
                                             ACT.Copy).then_inc(a_raw, 1)
                    act.wait_ge(p_v, b + 2)
                    nc.scalar.activation(v[:, :, :].rearrange("p c d -> p (c d)"),
                                         ps[:, 0:2, :].rearrange("p a n -> p (a n)"), ACT.Copy).then_inc(a_v, 1)
                    act.wait_ge(v_rot, b * 6 + 6)
                    for q in range(HPC):
                        nc.scalar.activation(kz[:, q, :, :].rearrange("p m s -> p (m s)"),
                                             rot[:, 1, :, :].rearrange("p m s -> p (m s)"), ACT.Copy,
                                             scale=cst[:, C_HEAD + q:C_HEAD + q + 1]).then_inc(a_kz, 1)
                    for h in range(NH):
                        exps(b, 0, h)
                    for h in range(NH + 1):
                        if h < NH:
                            exps(b, 1, h)
                        g = h - 1
                        if g >= 0:
                            n = b * NH + g
                            act.wait_ge(p_t, n + 1)
                            if g % HPC == 0 and g >= HPC:
                                act.wait_ge(p_av, b * KD + g // HPC)
                            nc.scalar.activation(ET[:, g % HPC, :], ps[:, 4 + g % 2, 0:P + S], ACT.Copy)\
                                .then_inc(a_t, 1)
                            if g % HPC == 1 and g >= HPC:
                                m = g // HPC - 1
                                act.wait_ge(p_av, b * KD + m + 1)
                                nc.scalar.activation(oT[:, m, :], ps[:, 6 + m % 2, 0:S], ACT.Copy).then_inc(a_o, 1)
                    act.wait_ge(p_av, (b + 1) * KD)
                    nc.scalar.activation(oT[:, KD - 1, :], ps[:, 6 + (KD - 1) % 2, 0:S], ACT.Copy).then_inc(a_o, 1)

            @block.vector
            def _(dve):
                for i, c in enumerate((C_ID, C_CAUS, C_NB0, C_NB1)):
                    last = nc.vector.tensor_copy(masks[:, i, :], cst[:, c:c + P])
                last.then_inc(v_init, 1)
                nc.vector.memset(rdiag[:, :, :, :], 0.0).then_inc(v_init, 1)
                nc.vector.memset(ls[:, :, :, :], 1.0).then_inc(v_init, 1)
                dve.nop().then_inc(v_x, 1)
                dve.nop().then_inc(v_n, 1)
                dve.wait_ge(v_init, 3)

                def maxima(b, r, h):
                    n = b * (2 * NH) + r * NH + h
                    dve.wait_ge(p_s, n + 2)
                    bank = h % 4
                    nc.vector.tensor_reduce(nm[:, r, h, 0:1], ps[:, bank, 0:P], AX.X, ALU.max, negate=True)
                    nc.vector.tensor_reduce(nm[:, r, h, 1:2], ps[:, bank, P:P + S], AX.X, ALU.max,
                                            negate=True).then_inc(v_m, 1)

                def recip(b, r, h):
                    n = b * (2 * NH) + r * NH + h
                    dve.wait_ge(a_e, (n + 1) * 2)
                    nc.vector.reciprocal(rl[:, r, h, :], ls[:, r, h, :]).then_inc(v_r, 1)
                    dve.wait_ge(v_r, n + 1)

                with dve.Fori(0, B) as b:
                    for i, (c, s) in enumerate(((C_COSQ, C_SINQ), (C_COSK, C_SINK))):
                        dve.wait_ge(p_rot, b * 2 + i + 1)
                        if i == 0:
                            dve.wait_ge(p_s, b * 2 * NH + 1)
                            dve.wait_ge(a_kz, b * HPC + 1)
                        cos = cst[:, c:c + S].unsqueeze(1).broadcast_to((P, KD, S))
                        sin = cst[:, s:s + S].unsqueeze(1).broadcast_to((P, KD, S))
                        nc.vector.tensor_tensor(tmp[:, :, :],
                                                ps[:, 4 + 2 * i:6 + 2 * i, :].rearrange("p a (m s) -> p (a m) s", s=S),
                                                sin, ALU.mult).then_inc(v_rot, 1)
                        nc.vector.tensor_tensor(rot[:, i, :, :], raw[:, i, :, :], cos, ALU.mult).then_inc(v_rot, 1)
                        dve.wait_ge(v_rot, b * 6 + 3 * i + 2)
                        nc.vector.tensor_tensor(rot[:, i, :, :], rot[:, i, :, :], tmp[:, :, :], ALU.add)\
                            .then_inc(v_rot, 1)
                        dve.wait_ge(v_rot, b * 6 + 3 * i + 3)
                    for h in range(NH + 1):
                        if h < NH:
                            maxima(b, 0, h)
                        if h >= 1:
                            g = h - 1
                            recip(b, 0, g)
                            nc.vector.tensor_copy(rdiag[:, g, :, g], rl[:, 0, g, :]).then_inc(v_d, 1)
                    dve.wait_ge(p_c, (b + 1) * NH)
                    c = [0]

                    def step(i_):
                        c[0] += 1
                        i_.then_inc(v_k, 1)
                        dve.drain()

                    step(nc.vector.tensor_copy(tsum[:, :], ps[0:NH, 4, 0:S]))
                    src = tsum
                    for _ in range(HEAVY // 8):
                        step(nc.vector.max(top8[:, :], src[:, :]))
                        step(nc.vector.match_replace(work[:, :], top8[:, :], src[:, :], -1.0))
                        src = work
                    for _ in range(HEAVY % 8):
                        step(nc.vector.max(top8[:, :], work[:, :]))
                        step(nc.vector.scalar_tensor_tensor(out=code[:, :], in0=work[:, :], scalar=top8[:, 0:1],
                                                            in1=cst[0:NH, C_DESC:C_DESC + S],
                                                            op0=ALU.is_equal, op1=ALU.mult))
                        step(nc.vector.tensor_reduce(cmax[:, :], code[:, :], AX.X, ALU.max))
                        step(nc.vector.tensor_scalar(code[:, :], code[:, :], cmax[:, 0:1], -1e6,
                                                     ALU.is_equal, ALU.mult))
                        step(nc.vector.tensor_tensor(work[:, :], work[:, :], code[:, :], ALU.add))
                    step(nc.vector.tensor_scalar(light[:, :], work[:, :], 0.0, None, ALU.is_ge))
                    assert c[0] == K_STEPS
                    dve.wait_ge(p_l, b + 1)
                    nc.vector.tensor_copy(lcol[:, :, :].rearrange("p c h -> p (c h)"), ps[:, 5, 0:KS * NH])\
                        .then_inc(v_l, 1)
                    dve.wait_ge(v_l, b + 1)

                    def diag(h):
                        if h >= 2:
                            dve.wait_ge(p_s, b * 2 * NH + NH + h)
                        for c_ in range(KS):
                            nc.vector.tensor_scalar(dg[:, h % 2, c_, :], masks[:, 0, :], lcol[:, c_, h:h + 1], None,
                                                    ALU.mult).then_inc(g_d, 1)

                    diag(0)
                    for h in range(NH + 1):
                        if h + 1 < NH:
                            diag(h + 1)
                        if h < NH:
                            maxima(b, 1, h)
                        if h >= 1:
                            g = h - 1
                            recip(b, 1, g)
                            if g >= 2:
                                dve.wait_ge(p_t, b * NH + g - 1)
                            nc.vector.tensor_scalar(En[:, g % 2, 0:P], E[:, g % 2, 0:P], rl[:, 1, g, 0:1], None,
                                                    ALU.mult).then_inc(v_n, 1)
                            nc.vector.tensor_scalar(En[:, g % 2, P:P + S], E[:, g % 2, P:P + S], rl[:, 1, g, 1:2],
                                                    None, ALU.mult).then_inc(v_n, 1)
                    for m in range(KD):
                        dve.wait_ge(p_o, b * KD + m + 1)
                        xv = x1T[:, m, :, bass.ds(b, 1)].rearrange("p s a -> p (s a)")
                        nc.vector.tensor_tensor(xv, ps[:, m, 0:S], xv, ALU.add).then_inc(v_x, 1)


K_STEPS = 2 + 2 * (HEAVY // 8) + 5 * (HEAVY % 8)


def gru_and_ffn(nc, ins, out, ps, cst, ident, x1T, sb, sem):
    top = ExitStack()
    with top:
        hs = sb(top, "hs", [P, KD, S, B])
        gru(nc, ins, ps, cst, ident, x1T, hs, sb, sem)
        ffn(nc, ins, out, ps, cst, ident, x1T, hs, sb, sem)


def gru(nc, ins, ps, cst, ident, x1T, hs, sb, sem):
    st = ExitStack()
    with st:
        gi = sb(st, "gi", [P, S, NQ, B])
        whp = sb(st, "whp", [P, KD, 2, G3], F16)
        bgi = sb(st, "bgi", [P, 2, NQ])
        bsum = sb(st, "bsum", [P, NQ])
        h32 = sb(st, "h32", [P, KD, B])
        hp = sb(st, "hp", [P, KD, 2, B], F16)
        sc = sb(st, "sc", [P, 2, 4])
        unscale = sb(st, "unscale", [P, 1])
        col = sb(st, "colT", [1, 2, P])
        mx1 = sb(st, "mx1", [1, 2])
        ones1 = sb(st, "ones1", [1, P])

        v_a = sem(st, "g1_step")
        d_a = sem(st, "g1_dma")
        p_a = sem(st, "g1_pe")
        wst = ExitStack()
        with wst:
            wf = hs[:, :, :, :].rearrange("p k s b -> p (k s b)")[:, 0:KD * G3].rearrange("p (k n) -> p k n", k=KD)
            with nc.Block() as block:
                @block.sync
                def _(sp):
                    sp.dma_start(wf, ins["W_hh"].rearrange("(k p) n -> p k n", p=P)).then_inc(d_a, 16)
                    sp.dma_start(h32[:, :, :], ins["condT"].rearrange("(k p) b -> p k b", p=P)).then_inc(d_a, 16)
                    sp.dma_start(bgi[:, 0, :], ins["b_ih"]).then_inc(d_a, 16)
                    sp.dma_start(bgi[:, 1, :], ins["b_hh"]).then_inc(d_a, 16)

                @block.tensor
                def _(pe):
                    pe.wait_ge(v_a, 3)
                    for i in range(2):
                        last = nc.tensor.transpose(ps[0:1, 0, i * P:(i + 1) * P], sc[:, i, 0:1], ident)
                    last.then_inc(p_a, 1)
                    pe.wait_ge(v_a, 5)
                    nc.tensor.matmul(ps[:, 1, 0:2], ones1[:, :], mx1[:, :], start=True, stop=True).then_inc(p_a, 1)

                @block.vector
                def _(dve):
                    n = [0]

                    def step(i_):
                        n[0] += 1
                        i_.then_inc(v_a, 1)
                        dve.wait_ge(v_a, n[0])

                    step(nc.vector.memset(ones1[:, :], 1.0))
                    dve.wait_ge(d_a, 64)
                    step(nc.vector.tensor_reduce(sc[:, 0, 0:1], wf, AX.XY, ALU.max,
                                                 apply_absolute_value=True))
                    step(nc.vector.tensor_reduce(sc[:, 1, 0:1], h32[:, :, :], AX.XY, ALU.max,
                                                 apply_absolute_value=True))
                    dve.wait_ge(p_a, 1)
                    step(nc.vector.tensor_reduce(mx1[:, :], ps[0:1, 0, 0:2 * P].rearrange("p (i n) -> p i n", i=2),
                                                 AX.X, ALU.max))
                    step(nc.vector.tensor_scalar(mx1[:, 1:2], mx1[:, 1:2], 1.0, None, ALU.max))
                    dve.wait_ge(p_a, 2)
                    step(nc.vector.tensor_scalar(sc[:, :, 1], ps[:, 1, 0:2], 1e-20, None, ALU.max))
                    step(nc.vector.tensor_scalar(sc[:, :, 1].bitcast(I32), sc[:, :, 1].bitcast(I32), 0x7F800000, None,
                                                 ALU.bitwise_and))
                    step(nc.vector.reciprocal(sc[:, :, 2], sc[:, :, 1]))
                    step(nc.vector.tensor_scalar(sc[:, :, 2], sc[:, :, 2], 2.0 ** 14, None, ALU.mult))
                    step(nc.vector.tensor_scalar(sc[:, :, 1], sc[:, :, 1], 2.0 ** -14, None, ALU.mult))
                    step(nc.vector.tensor_tensor(unscale[:, :], sc[:, 0, 1:2], sc[:, 1, 1:2], ALU.mult))
                    for k in range(KD):
                        step(nc.vector.tensor_scalar(wf[:, k, :], wf[:, k, :], sc[:, 0, 2:3], None, ALU.mult))
                        step(nc.vector.tensor_copy(whp[:, k, 0, :], wf[:, k, :]))
                        step(nc.vector.tensor_tensor(whp[:, k, 1, :], wf[:, k, :], whp[:, k, 0, :], ALU.subtract))
                    step(nc.vector.tensor_scalar(hp[:, :, 0, :], h32[:, :, :], sc[:, 1, 2:3], None, ALU.mult))
                    step(nc.vector.scalar_tensor_tensor(out=hp[:, :, 1, :], in0=h32[:, :, :], scalar=sc[:, 1, 2:3],
                                                        in1=hp[:, :, 0, :], op0=ALU.mult, op1=ALU.subtract))
                    step(nc.vector.tensor_copy(bsum[:, :], bgi[:, 0, :]))
                    step(nc.vector.tensor_tensor(bsum[:, 0:2 * KD], bgi[:, 0, 0:2 * KD], bgi[:, 1, 0:2 * KD], ALU.add))

        wst = ExitStack()
        with wst:
            wi = hs[:, :, :, :].rearrange("p k s b -> p (k s b)")[:, 0:KD * G3].rearrange("p (k n) -> p k n", k=KD)
            d_i = sem(wst, "gi_dma")
            p_i = sem(wst, "gi_pe")
            a_i = sem(wst, "gi_act")
            NT = TOK // 512
            ST = 512 // B
            with nc.Block() as block:
                @block.sync
                def _(sp):
                    sp.dma_start(wi, ins["W_ih"].rearrange("(k p) n -> p k n", p=P)).then_inc(d_i, 16)

                @block.tensor
                def _(pe):
                    pe.wait_ge(d_i, 16)
                    for q in range(NQ):
                        for t in range(NT):
                            n = q * NT + t
                            if n >= 8:
                                pe.wait_ge(a_i, n - 7)
                            for k in range(KD):
                                last = nc.tensor.matmul(
                                    ps[:, n % 8, :], wi[:, k, q * P:(q + 1) * P],
                                    x1T[:, k, t * ST:(t + 1) * ST, :].rearrange("p s b -> p (s b)"),
                                    start=(k == 0), stop=(k == KD - 1))
                            last.then_inc(p_i, 1)

                @block.scalar
                def _(act):
                    for q in range(NQ):
                        for t in range(NT):
                            n = q * NT + t
                            act.wait_ge(p_i, n + 1)
                            nc.scalar.activation(gi[:, t * ST:(t + 1) * ST, q, :],
                                                 ps[:, n % 8, :].rearrange("p (s b) -> p s b", b=B), ACT.Identity,
                                                 bias=bsum[:, q:q + 1]).then_inc(a_i, 1)

        wst = ExitStack()
        with wst:
            ev = sb(wst, "ev", [P, 3, P])
            s1 = sb(wst, "s1", [P, 2, KD, B])
            rz = sb(wst, "rz", [P, 2, KD, B])
            hn = sb(wst, "hn", [P, KD, B])
            nn = sb(wst, "nn", [P, KD, B])
            omz = sb(wst, "omz", [P, KD, B])
            zh = sb(wst, "zh", [P, KD, B])
            bhn = sb(wst, "bhn", [P, KD, B])
            one3 = sb(wst, "one3", [P, KD, B])
            v_0 = sem(wst, "r_init")
            p_rz = sem(wst, "r_p_rz")
            p_n = sem(wst, "r_p_n")
            a_rz = sem(wst, "r_a_rz")
            v_n = sem(wst, "r_v_n")
            t_rz = sem(wst, "r_t_rz")
            t_n = sem(wst, "r_t_n")
            v_p = sem(wst, "r_v_p")
            a_s = sem(wst, "r_a_s")
            v_c = sem(wst, "r_v_c")
            a_t = sem(wst, "r_a_t")
            g_z = sem(wst, "r_g_z")
            v_h = sem(wst, "r_v_h")
            g_h = sem(wst, "r_g_h")
            RZ, N_, TR, TN = 0, 1, 2, 3
            with nc.Block() as block:
                @block.tensor
                def _(pe):
                    pe.wait_ge(v_0, 3)
                    with pe.Fori(0, S) as s:
                        pe.wait_ge(v_h, s * 4 + 1)
                        pe.wait_ge(a_rz, s + 1)
                        for part, (c0, cn) in enumerate(((0, 2), (2, 1))):
                            for k in range(KD):
                                for w in range(2):
                                    for g in range(KD):
                                        wv = whp[:, k, w, :].rearrange("p (q n) -> p q n", q=3)
                                        last = nc.tensor.matmul(
                                            ps[32 * g:32 * g + 2 * B, part, 0:cn * P],
                                            hp[:, k, :, :].rearrange("p a b -> p (a b)"),
                                            wv[:, c0:c0 + cn, g * P:(g + 1) * P],
                                            start=(k == 0 and w == 0), stop=(k == KD - 1 and w == 1),
                                            tile_position=(0, 32 * g), skip_group_check=True)
                            last.then_inc(p_n if part else p_rz, 1)
                        pe.wait_ge(a_rz, s + 2)
                        for c in range(2):
                            last = nc.tensor.transpose(ps[:, TR, c * P:(c + 1) * P], ev[:, c, :], ident)
                        last.then_inc(t_rz, 1)
                        pe.wait_ge(v_n, s + 1)
                        nc.tensor.transpose(ps[:, TN, 0:P], ev[:, 2, :], ident).then_inc(t_n, 1)

                @block.scalar
                def _(act):
                    act.nop().then_inc(a_rz, 1)
                    with act.Fori(0, S) as s:
                        act.wait_ge(p_rz, s + 1)
                        act.wait_ge(v_h, s * 4 + 1)
                        nc.scalar.activation(ev[:, 0:2, :].rearrange("p c n -> p (c n)"), ps[:, RZ, 0:2 * P],
                                             ACT.Copy).then_inc(a_rz, 1)
                        act.wait_ge(v_p, (s + 1) * 2)
                        nc.scalar.activation(rz[:, :, :, :].rearrange("p c g b -> p (c g b)"),
                                             s1[:, :, :, :].rearrange("p c g b -> p (c g b)"),
                                             ACT.Sigmoid).then_inc(a_s, 1)
                        act.wait_ge(v_c, (s + 1) * 4)
                        nc.scalar.activation(nn[:, :, :].rearrange("p g b -> p (g b)"),
                                             hn[:, :, :].rearrange("p g b -> p (g b)"), ACT.Tanh).then_inc(a_t, 1)

                @block.gpsimd
                def _(pool):
                    pool.nop().then_inc(g_h, 1)
                    with pool.Fori(0, S) as s:
                        pool.wait_ge(a_s, s + 1)
                        pool.wait_ge(v_h, s * 4 + 1)
                        nc.gpsimd.tensor_tensor(omz[:, :, :], one3[:, :, :], rz[:, 1, :, :], ALU.subtract)\
                            .then_inc(g_z, 1)
                        nc.gpsimd.tensor_tensor(zh[:, :, :], rz[:, 1, :, :], h32[:, :, :], ALU.mult).then_inc(g_z, 1)
                        pool.wait_ge(v_h, s * 4 + 5)
                        nc.gpsimd.tensor_copy(hs[:, :, bass.ds(s, 1), :].rearrange("p k a b -> p k (a b)"),
                                              h32[:, :, :]).then_inc(g_h, 1)

                @block.vector
                def _(dve):
                    nc.vector.memset(ps[:, 0:2, :], 0.0).then_inc(v_0, 1)
                    nc.vector.memset(one3[:, :, :], 1.0).then_inc(v_0, 1)
                    nc.vector.tensor_copy(bhn[:, :, :], bgi[:, 1, 2 * KD:NQ].unsqueeze(2).broadcast_to((P, KD, B)))\
                        .then_inc(v_0, 1)
                    dve.wait_ge(v_0, 3)
                    tr = ps[:, TR, 0:2 * P].rearrange("p (c g a b) -> p c g a b", c=2, g=KD, b=B)
                    tn = ps[:, TN, 0:P].rearrange("p (g a b) -> p g a b", g=KD, b=B)
                    dve.nop().then_inc(v_h, 1)
                    with dve.Fori(0, S) as s:
                        gs = gi[:, bass.ds(s, 1), :, :]
                        dve.wait_ge(p_n, s + 1)
                        nc.vector.tensor_copy(ev[:, 2, :], ps[:, N_, 0:P]).then_inc(v_n, 1)
                        dve.wait_ge(t_rz, s + 1)
                        nc.vector.scalar_tensor_tensor(
                            out=s1[:, :, :, :].rearrange("p c g b -> p (c g) b"),
                            in0=ps[:, TR, 0:2 * P].rearrange("p (c a b) -> p c a b", a=4, b=B)[:, :, 0, :],
                            scalar=unscale[:, 0:1],
                            in1=gs[:, :, 0:2 * KD, :].rearrange("p a q b -> p (a q) b"),
                            op0=ALU.mult, op1=ALU.add).then_inc(v_p, 1)
                        dve.wait_ge(v_p, s * 2 + 1)
                        nc.vector.scalar_tensor_tensor(
                            out=s1[:, :, :, :].rearrange("p c g b -> p (c g) b"),
                            in0=ps[:, TR, 0:2 * P].rearrange("p (c a b) -> p c a b", a=4, b=B)[:, :, 1, :],
                            scalar=unscale[:, 0:1],
                            in1=s1[:, :, :, :].rearrange("p c g b -> p (c g) b"),
                            op0=ALU.mult, op1=ALU.add).then_inc(v_p, 1)
                        dve.wait_ge(t_n, s + 1)
                        nc.vector.scalar_tensor_tensor(out=hn[:, :, :], in0=tn[:, :, 0, :], scalar=unscale[:, 0:1],
                                                       in1=bhn[:, :, :], op0=ALU.mult, op1=ALU.add).then_inc(v_c, 1)
                        dve.wait_ge(v_c, s * 4 + 1)
                        nc.vector.scalar_tensor_tensor(out=hn[:, :, :], in0=tn[:, :, 1, :], scalar=unscale[:, 0:1],
                                                       in1=hn[:, :, :], op0=ALU.mult, op1=ALU.add).then_inc(v_c, 1)
                        dve.wait_ge(v_c, s * 4 + 2)
                        dve.wait_ge(a_s, s + 1)
                        nc.vector.tensor_tensor(hn[:, :, :], hn[:, :, :], rz[:, 0, :, :], ALU.mult).then_inc(v_c, 1)
                        dve.wait_ge(v_c, s * 4 + 3)
                        nc.vector.tensor_tensor(hn[:, :, :], hn[:, :, :],
                                                gs[:, :, 2 * KD:NQ, :].rearrange("p a q b -> p (a q) b"),
                                                ALU.add).then_inc(v_c, 1)
                        dve.wait_ge(a_t, s + 1)
                        dve.wait_ge(g_z, (s + 1) * 2)
                        nc.vector.tensor_tensor(nn[:, :, :], nn[:, :, :], omz[:, :, :], ALU.mult).then_inc(v_h, 1)
                        dve.wait_ge(v_h, s * 4 + 2)
                        dve.wait_ge(g_h, s + 1)
                        nc.vector.tensor_tensor(h32[:, :, :], nn[:, :, :], zh[:, :, :], ALU.add).then_inc(v_h, 1)
                        dve.wait_ge(v_h, s * 4 + 3)
                        nc.vector.tensor_scalar(hp[:, :, 0, :], h32[:, :, :], sc[:, 1, 2:3], None, ALU.mult)\
                            .then_inc(v_h, 1)
                        dve.wait_ge(v_h, s * 4 + 4)
                        nc.vector.scalar_tensor_tensor(out=hp[:, :, 1, :], in0=h32[:, :, :], scalar=sc[:, 1, 2:3],
                                                       in1=hp[:, :, 0, :], op0=ALU.mult, op1=ALU.subtract)\
                            .then_inc(v_h, 1)


def ffn(nc, ins, out, ps, cst, ident, x1T, hs, sb, sem):
    NT = TOK // TT
    NG = TOK // P
    ST = TT // B
    st = ExitStack()
    with st:
        w1 = sb(st, "w1", [P, KD, NE, HF])
        w2 = sb(st, "w2", [P, FC, NE, D])
        gw = sb(st, "gw", [P, KD, NE])
        b1 = sb(st, "b1", [P, FC, NE])
        b2 = sb(st, "b2", [NE, D])
        gb = sb(st, "gb", [1, 2, NE])
        one = sb(st, "one", [1, P])
        scr = sb(st, "scr", [P, NG, NE])
        m1 = sb(st, "m1", [P, NG])
        m2 = sb(st, "m2", [P, NG])
        o1 = sb(st, "o1", [P, NG, NE])
        o2 = sb(st, "o2", [P, NG, NE])
        cd = sb(st, "cd", [P, NG, NE])
        cm = sb(st, "cm", [P, NG])
        comb = sb(st, "comb", [P, NG, NE])
        combT = sb(st, "combT", [NE, TOK])
        cb = sb(st, "cb", [P, 2, TT])
        sg = sb(st, "sg", [P, 2, TT])
        hh = sb(st, "hh", [P, 2, FC, TT])
        f_w = sem(st, "f_w")
        f_v0 = sem(st, "f_v0")
        f_g = sem(st, "f_g")
        f_s = sem(st, "f_s")
        f_e = sem(st, "f_e")
        f_ct = sem(st, "f_ct")
        f_cts = sem(st, "f_cts")
        f_bc = sem(st, "f_bc")
        f_bcs = sem(st, "f_bcs")
        f_h = sem(st, "f_h")
        f_sg = sem(st, "f_sg")
        f_m = sem(st, "f_m")
        f_y = sem(st, "f_y")
        f_r = sem(st, "f_r")
        f_o = sem(st, "f_o")

        with nc.Block() as block:
            @block.sync
            def _(sp):
                sp.dma_start(gw[:, :, :], ins["gate_wT"].rearrange("(k p) e -> p k e", p=P)).then_inc(f_w, 16)
                sp.dma_start(gb[:, 0, :], ins["gate_b"]).then_inc(f_w, 16)
                sp.dma_start(gb[:, 1, :], ins["bias"]).then_inc(f_w, 16)
                sp.dma_start(w1[:, :, :, :].rearrange("p k e h -> p k (e h)"),
                             ins["w1T"].rearrange("(k p) n -> p k n", p=P)).then_inc(f_w, 16)
                for c in range(FC):
                    rows = P if c < FC - 1 else HL
                    sp.dma_start(w2[0:rows, c, :, :], ins["w2T"][c * P:c * P + rows]).then_inc(f_w, 16)
                    sp.dma_start(b1[0:rows, c, :], ins["b1T"][c * P:c * P + rows]).then_inc(f_w, 16)
                sp.dma_start(b2[:, :], ins["b2"]).then_inc(f_w, 16)
                for t in range(NT):
                    sp.wait_ge(f_r, (t + 1) * KD)
                    sp.dma_start(out[:, t * TT:(t + 1) * TT].rearrange("(k p) n -> p k n", p=P),
                                 x1T[:, :, t * ST:(t + 1) * ST, :].rearrange("p k s b -> p k (s b)"))\
                        .then_inc(f_o, 16)
                sp.wait_ge(f_o, 16 * NT)

            @block.tensor
            def _(pe):
                pe.wait_ge(f_w, 16 * (5 + 2 * FC))
                pe.wait_ge(f_v0, 1)
                for g in range(NG):
                    o = ps[:, 0, g * NE:(g + 1) * NE]
                    for k in range(KD):
                        nc.tensor.matmul(o, hs[:, k, g * P // B:(g + 1) * P // B, :].rearrange("p s b -> p (s b)"),
                                         gw[:, k, :], start=(k == 0 and g == 0), stop=False, skip_group_check=True)
                    for i in range(2):
                        last = nc.tensor.matmul(o, one[:, :], gb[:, i, :], start=False, stop=(i == 1),
                                                skip_group_check=True)
                last.then_inc(f_g, 1)
                pe.wait_ge(f_e, 1)
                for g in range(NG):
                    last = nc.tensor.transpose(ps[0:NE, 1 + g // 4, (g % 4) * P:(g % 4 + 1) * P], comb[:, g, :], ident)
                last.then_inc(f_ct, 1)
                pe.wait_ge(f_cts, 1)
                for t in range(NT):
                    for e in range(NE + 1):
                        if e < NE:
                            n = t * NE + e
                            if n:
                                pe.wait_ge(f_bcs, n)
                            nc.tensor.matmul(ps[:, 7, :], cst[0:NE, C_SEL + e * P:C_SEL + (e + 1) * P],
                                             combT[:, t * TT:(t + 1) * TT], start=True, stop=True).then_inc(f_bc, 1)
                            for c in range(FC):
                                rows = P if c < FC - 1 else HL
                                if n:
                                    pe.wait_ge(f_m, ((n - 1) * FC + c + 1) * 2)
                                for k in range(KD):
                                    last = nc.tensor.matmul(
                                        ps[0:rows, 4 + c, :], w1[:, k, e, c * P:c * P + rows],
                                        hs[:, k, t * ST:(t + 1) * ST, :].rearrange("p s b -> p (s b)"),
                                        start=(k == 0), stop=(k == KD - 1))
                                last.then_inc(f_h, 1)
                        if e >= 1:
                            n = t * NE + e - 1
                            if e == 1 and t:
                                pe.wait_ge(f_r, t * KD)
                            for c in range(FC):
                                rows = P if c < FC - 1 else HL
                                pe.wait_ge(f_m, (n * FC + c + 1) * 2)
                                for m in range(KD):
                                    last = nc.tensor.matmul(ps[:, m, :], w2[0:rows, c, e - 1, m * P:(m + 1) * P],
                                                            hh[0:rows, n % 2, c, :], start=(e == 1 and c == 0),
                                                            stop=False, skip_group_check=True)
                            if e == NE:
                                for m in range(KD):
                                    last = nc.tensor.matmul(ps[:, m, :], b2[:, m * P:(m + 1) * P],
                                                            combT[:, t * TT:(t + 1) * TT], start=False, stop=True,
                                                            skip_group_check=True)
                            last.then_inc(f_y, 1)

            @block.scalar
            def _(act):
                act.wait_ge(f_s, 1)
                nc.scalar.activation(m2[:, :], m2[:, :], ACT.Exp).then_inc(f_s, 1)
                for t in range(NT):
                    for e in range(NE):
                        n = t * NE + e
                        act.wait_ge(f_bc, n + 1)
                        if n >= 2:
                            act.wait_ge(f_m, (n - 1) * FC * 2)
                        nc.scalar.activation(cb[:, n % 2, :], ps[:, 7, :], ACT.Copy).then_inc(f_bcs, 1)
                        for c in range(FC):
                            rows = P if c < FC - 1 else HL
                            i = n * FC + c
                            act.wait_ge(f_h, i + 1)
                            if i >= 2:
                                act.wait_ge(f_m, (i - 1) * 2)
                            nc.scalar.activation(sg[0:rows, i % 2, :], ps[0:rows, 4 + c, :], ACT.Sigmoid,
                                                 bias=b1[0:rows, c, e:e + 1]).then_inc(f_sg, 1)

            @block.vector
            def _(dve):
                nc.vector.memset(one[:, :], 1.0).then_inc(f_v0, 1)
                n_ = [0]
                sem_v = f_v0
                n_[0] = 1

                def step(i_):
                    n_[0] += 1
                    i_.then_inc(sem_v, 1)
                    dve.wait_ge(sem_v, n_[0])

                bc = lambda t: t[:, :].unsqueeze(2).broadcast_to((P, NG, NE))
                desc = cst[:, C_DESC:C_DESC + NE].unsqueeze(1).broadcast_to((P, NG, NE))
                dve.wait_ge(f_g, 1)
                step(nc.vector.tensor_copy(scr[:, :, :].rearrange("p g e -> p (g e)"), ps[:, 0, 0:NG * NE]))

                def first_of_largest(m, o):
                    step(nc.vector.tensor_reduce(m[:, :], scr[:, :, :], AX.X, ALU.max))
                    step(nc.vector.tensor_tensor(o[:, :, :], scr[:, :, :], bc(m), ALU.is_equal))
                    step(nc.vector.tensor_tensor(cd[:, :, :], o[:, :, :], desc, ALU.mult))
                    step(nc.vector.tensor_reduce(cm[:, :], cd[:, :, :], AX.X, ALU.max))
                    step(nc.vector.tensor_tensor(o[:, :, :], cd[:, :, :], bc(cm), ALU.is_equal))

                first_of_largest(m1, o1)
                step(nc.vector.scalar_tensor_tensor(out=scr[:, :, :], in0=o1[:, :, :], scalar=-3e38,
                                                    in1=scr[:, :, :], op0=ALU.mult, op1=ALU.add))
                first_of_largest(m2, o2)
                nc.vector.tensor_tensor(m2[:, :], m2[:, :], m1[:, :], ALU.subtract).then_inc(f_s, 1)
                dve.wait_ge(f_s, 2)
                step(nc.vector.tensor_scalar(m1[:, :], m2[:, :], 1.0, None, ALU.add))
                step(nc.vector.reciprocal(m1[:, :], m1[:, :]))
                step(nc.vector.tensor_tensor(m2[:, :], m2[:, :], m1[:, :], ALU.mult))
                step(nc.vector.tensor_tensor(o1[:, :, :], o1[:, :, :], bc(m1), ALU.mult))
                step(nc.vector.tensor_tensor(o2[:, :, :], o2[:, :, :], bc(m2), ALU.mult))
                nc.vector.tensor_tensor(comb[:, :, :], o1[:, :, :], o2[:, :, :], ALU.add).then_inc(f_e, 1)
                dve.wait_ge(f_ct, 1)
                nc.vector.tensor_copy(combT[:, :], ps[0:NE, 1:5, :].rearrange("p a n -> p (a n)")).then_inc(f_cts, 1)
                for t in range(NT):
                    for e in range(NE):
                        n = t * NE + e
                        if n >= 2:
                            dve.wait_ge(f_y, n - 1)
                        for c in range(FC):
                            rows = P if c < FC - 1 else HL
                            i = n * FC + c
                            dve.wait_ge(f_sg, i + 1)
                            h = hh[0:rows, n % 2, c, :]
                            nc.vector.scalar_tensor_tensor(out=h, in0=ps[0:rows, 4 + c, :],
                                                           scalar=b1[0:rows, c, e:e + 1], in1=sg[0:rows, i % 2, :],
                                                           op0=ALU.add, op1=ALU.mult).then_inc(f_m, 1)
                            dve.wait_ge(f_m, 2 * i + 1)
                            dve.wait_ge(f_bcs, n + 1)
                            nc.vector.tensor_tensor(h, h, cb[0:rows, n % 2, :], ALU.mult).then_inc(f_m, 1)
                    dve.wait_ge(f_y, (t + 1) * NE)
                    for m in range(KD):
                        xr = x1T[:, m, t * ST:(t + 1) * ST, :].rearrange("p s b -> p (s b)")
                        nc.vector.tensor_tensor(xr, ps[:, m, :], xr, ALU.add).then_inc(f_r, 1)


def constants():
    import numpy as np

    c = np.zeros((P, C_ALL), np.float32)
    i = np.arange(P)
    c[:, C_ID:C_ID + P] = np.eye(P)
    half = DH2 // 2
    partner = np.where(i % DH2 < half, i + half, i - half)
    c[partner, C_ROT + i] = 1.0
    c[:, C_CAUS:C_CAUS + P] = np.where(i[None, :] <= i[:, None], 0.0, NEG)
    c[:, C_NB0:C_NB0 + P] = np.where(np.abs(i[None, :] - i[:, None]) <= RECENT, 0.0, NEG)
    c[:, C_NB1:C_NB1 + P] = np.where(np.abs(i[None, :] + P - i[:, None]) <= RECENT, 0.0, NEG)
    inv = (np.float32(1.0) / np.float32(10000.0) ** (np.arange(0, DH2, 2, dtype=np.float32) / np.float32(DH2)))
    ang = np.arange(S, dtype=np.float32)[None, :] * inv.astype(np.float32)[i % half][:, None]
    sign = np.where(i % DH2 < half, -1.0, 1.0)[:, None]
    cos, sin = np.cos(ang), np.sin(ang) * sign
    c[:, C_COSQ:C_COSQ + S] = cos * DH2 ** -0.5
    c[:, C_SINQ:C_SINQ + S] = sin * DH2 ** -0.5
    c[:, C_COSK:C_COSK + S] = cos
    c[:, C_SINK:C_SINK + S] = sin
    for q in range(HPC):
        c[q * DH2:(q + 1) * DH2, C_HEAD + q] = 1.0
    for b in range(B):
        c[b, C_SEL + b * P:C_SEL + (b + 1) * P] = 1.0
    c[:, C_DESC:C_DESC + S] = np.arange(S, 0, -1)
    return c


def kernel(x, cond_2048, L0_cond_Wq, L0_cond_Wk, L0_cond_Wv, L0_cond_b, L0_attn_Wq, L0_attn_Wk, L0_attn_Wv,
           L0_attn_Wo, L0_cond2_W_ih, L0_cond2_W_hh, L0_cond2_b_ih, L0_cond2_b_hh, L0_ffn_gate_w, L0_ffn_gate_b,
           L0_ffn_bias, L0_ffn_w1, L0_ffn_b1, L0_ffn_w2, L0_ffn_b2):
    import numpy as np
    import concourse.bacc as bacc
    from concourse.bass_utils import run_bass_kernel_spmd

    n = np.asarray
    heads = [n(w).reshape(NH, DH1, KS, P).transpose(0, 3, 2, 1) for w in (L0_cond_Wq, L0_cond_Wk, L0_cond_Wv)]
    arrays = {
        "consts": constants(),
        "x": n(x),
        "xT": n(x).transpose(2, 1, 0).reshape(D, S * B),
        "cond": n(cond_2048),
        "condT": n(cond_2048).T,
        "cond_b": np.broadcast_to(n(L0_cond_b).reshape(1, 1), (B, 1)),
        "cond_WvT": n(L0_cond_Wv).T,
        "cond_Wh": np.stack(heads, axis=3),
        "attn_WqT": n(L0_attn_Wq).T,
        "attn_WkT": n(L0_attn_Wk).T,
        "attn_WvT": n(L0_attn_Wv).T,
        "attn_WoT": n(L0_attn_Wo).T,
        "W_ih": n(L0_cond2_W_ih),
        "W_hh": n(L0_cond2_W_hh),
        "b_ih": n(L0_cond2_b_ih).reshape(NQ, P).T,
        "b_hh": n(L0_cond2_b_hh).reshape(NQ, P).T,
        "gate_wT": n(L0_ffn_gate_w).T,
        "gate_b": n(L0_ffn_gate_b).reshape(1, NE),
        "bias": n(L0_ffn_bias).reshape(1, NE),
        "w1T": n(L0_ffn_w1).transpose(2, 0, 1).reshape(D, NE * HF),
        "b1T": n(L0_ffn_b1).T,
        "w2T": n(L0_ffn_w2).transpose(2, 0, 1),
        "b2": n(L0_ffn_b2),
    }
    arrays = {k: np.ascontiguousarray(v) for k, v in arrays.items()}
    nc = bacc.Bacc("TRN2", target_bir_lowering=False, num_devices=1)
    ins = {k: nc.dram_tensor(f"in_{k}", v.shape, mybir.dt.from_np(v.dtype), kind="ExternalInput").ap()
           for k, v in arrays.items()}
    out = nc.dram_tensor("out_0", (D, S * B), F32, kind="ExternalOutput").ap()
    program(nc, ins, out)
    r = run_bass_kernel_spmd(nc, [{f"in_{k}": v for k, v in arrays.items()}], core_ids=[0])
    got = r.results[0]["out_0"]
    return np.ascontiguousarray(got.reshape(D, S, B).transpose(2, 1, 0))
```

```python
from contextlib import ExitStack

import concourse.bass as bass
from concourse import mybir

F32 = mybir.dt.float32
F16 = mybir.dt.float16
BF16 = mybir.dt.bfloat16
I32 = mybir.dt.int32
ALU = mybir.AluOpType
ACT = mybir.ActivationFunctionType
AX = mybir.AxisListType

P = 128
B, S, D = 8, 256, 512
KD = D // P
KS = S // P
NH = 16
DH1 = S // NH
DH2 = D // NH
HPC = P // DH2
NEG = -1e30
HEAVY = int(0.1 * S)
RECENT = int(0.1 * S)
G3 = 3 * D
NQ = G3 // P
NE, HF = 8, 352
TOK = B * S
FC = (HF + P - 1) // P
HL = HF - (FC - 1) * P
SPT = 32
TT = SPT * B
NT = S // SPT
HFP = FC * P
EH = NE // 2

C_ID = 0
C_DESC8 = C_ID + P
C_ALL = C_DESC8 + NE
C_ROT = 0
C_CAUS = C_ROT + P
C_NB0 = C_CAUS + P
C_NB1 = C_NB0 + P
C_COSQ = C_NB1 + P
C_SINQ = C_COSQ + S
C_COSK = C_SINQ + S
C_SINK = C_COSK + S
C_HEAD = C_SINK + S
C_DESC = C_HEAD + HPC
T_ALL = C_DESC + S


def program(nc, ins, out):
    ctx = ExitStack()
    with ctx:
        def sb(stack, name, shape, dt=F32):
            return stack.enter_context(nc.sbuf_tensor(name, shape, dt))

        def sem(stack, name):
            return stack.enter_context(nc.semaphore(name))

        ps = ctx.enter_context(nc.psum_tensor("ps", [P, 8, 512], F32))
        cst = sb(ctx, "cst", [P, C_ALL])
        x1T = sb(ctx, "x1T", [P, KD, S, B])
        ident = cst[:, C_ID:C_ID + P]

        att = ExitStack()
        with att:
            hT = sb(att, "hT", [P, KD, B, S])
            first_attention_uniform_and_general(nc, ins, ps, cst, ident, x1T, hT, sb, sem)
            second_attention(nc, ins, ps, cst, ident, x1T, hT, sb, sem)
        gru_and_ffn(nc, ins, out, ps, cst, ident, x1T, sb, sem)


def first_attention_uniform_and_general(nc, ins, ps, cst, ident, x1T, hT, sb, sem):
    st = ExitStack()
    with st:
        xall = sb(st, "xall", [P, KS, B, D])
        wv = sb(st, "wv", [P, KS, S])
        mask = sb(st, "mask", [B, D])
        b0 = sb(st, "b0", [B, 1])
        pen = sb(st, "pen", [B, D])
        top = sb(st, "top", [B, 1])
        zf = sb(st, "zf", [B, 1])
        wm = sb(st, "wm", [B, D])
        cnt = sb(st, "cnt", [B, 1])
        rcnt = sb(st, "rcnt", [B, 1])
        bz = sb(st, "bz", [B, 1])
        bias = sb(st, "bias", [B, D])
        ksc = sb(st, "ksc", [B, D])
        xw = sb(st, "xw", [P, KS, B])
        junk = sb(st, "junk", [P, D])
        ones = sb(st, "ones", [P, P])
        xwb = sb(st, "xwb", [P, KS, B, P])
        flag = sb(st, "flag", [1, 1], I32)
        scr_bias = nc.dram_tensor("scr_bias", [B, D], F32).ap()
        scr_ksc = nc.dram_tensor("scr_ksc", [B, D], F32).ap()

        d_mask = sem(st, "d_mask")
        d_cst = sem(st, "d_cst")
        d_x = sem(st, "d_x")
        d_xT = sem(st, "d_xT")
        d_wv = sem(st, "d_wv")
        d_scr = sem(st, "d_scr")
        v_step = sem(st, "v_step")
        v_ones = sem(st, "v_ones")
        v_w = sem(st, "v_w")
        v_rows = sem(st, "v_rows")
        p_w = sem(st, "p_w")
        v_xw = sem(st, "v_xw")
        v_xwb = sem(st, "v_xwb")
        p_y = sem(st, "p_y")
        a_hT = sem(st, "a_hT")
        p_flag = sem(st, "p_flag")

        with nc.Block() as block:
            @block.sync
            def _(sp):
                sp.dma_start(mask[:, :], ins["cond"]).then_inc(d_mask, 16)
                sp.dma_start(b0[:, :], ins["cond_b"]).then_inc(d_mask, 16)
                sp.dma_start(cst[:, :], ins["consts"]).then_inc(d_cst, 16)
                for k in range(KS):
                    for b in range(0, B, 4):
                        sp.dma_start(xall[:, k, b:b + 4, :],
                                     ins["x"][b:b + 4, k * P:(k + 1) * P, :].rearrange("b p t -> p b t"))\
                            .then_inc(d_x, 16)
                sp.dma_start(wv[:, :, :], ins["cond_WvT"].rearrange("(k p) o -> p k o", p=P)).then_inc(d_wv, 16)
                sp.dma_start(x1T[:, :, :, :].rearrange("p k s b -> p k (s b)"),
                             ins["xT"].rearrange("(k p) n -> p k n", p=P)).then_inc(d_xT, 16)
                sp.wait_ge(v_rows, 2)
                sp.dma_start(scr_bias, bias[:, :]).then_inc(d_scr, 16)
                sp.dma_start(scr_ksc, ksc[:, :]).then_inc(d_scr, 16)
                sp.wait_ge(d_scr, 32)
                sp.wait_ge(d_xT, 16)

            @block.vector
            def _(dve):
                n = [0]

                def step(ins_):
                    n[0] += 1
                    ins_.then_inc(v_step, 1)
                    dve.wait_ge(v_step, n[0])

                nc.vector.memset(ones[:, :], 1.0).then_inc(v_ones, 1)
                dve.wait_ge(d_mask, 32)
                step(nc.vector.tensor_scalar(pen[:, :], mask[:, :], -1.0, 1.0, ALU.mult, ALU.add))
                step(nc.vector.tensor_scalar(pen[:, :], pen[:, :], NEG, None, ALU.mult))
                step(nc.vector.tensor_reduce(top[:, :], pen[:, :], AX.X, ALU.max))
                step(nc.vector.tensor_scalar(wm[:, :], pen[:, :], top[:, 0:1], None, ALU.is_equal))
                step(nc.vector.tensor_reduce(cnt[:, :], wm[:, :], AX.X, ALU.add))
                step(nc.vector.reciprocal(rcnt[:, :], cnt[:, :]))
                nc.vector.tensor_scalar(wm[:, :], wm[:, :], rcnt[:, 0:1], None, ALU.mult).then_inc(v_w, 1)
                step(nc.vector.tensor_scalar(zf[:, :], top[:, :], 0.0, None, ALU.is_equal))
                step(nc.vector.tensor_tensor(bz[:, :], b0[:, :], zf[:, :], ALU.mult))
                step(nc.vector.tensor_scalar(pen[:, :], pen[:, :], top[:, 0:1], None, ALU.subtract))
                nc.vector.scalar_tensor_tensor(out=bias[:, :], in0=mask[:, :], scalar=bz[:, 0:1],
                                               in1=pen[:, :], op0=ALU.mult, op1=ALU.add).then_inc(v_rows, 1)
                nc.vector.tensor_scalar(ksc[:, :], mask[:, :], zf[:, 0:1], DH1 ** -0.5, ALU.mult, ALU.mult)\
                    .then_inc(v_rows, 1)
                dve.wait_ge(d_x, 16 * 2 * KS)
                for b in range(B):
                    dve.wait_ge(p_w, b + 1)
                    for k in range(KS):
                        step(nc.vector.tensor_tensor_reduce(junk[:, :], xall[:, k, b, :], ps[:, b, :], 1.0, 0.0,
                                                            ALU.mult, ALU.add, xw[:, k, b:b + 1]))
                for b in range(B):
                    for k in range(KS):
                        nc.vector.tensor_scalar(xwb[:, k, b, :], ones[:, :], xw[:, k, b:b + 1], None, ALU.mult)\
                            .then_inc(v_xwb, 1)
                dve.wait_ge(p_flag, 1)
                nc.vector.tensor_copy(flag[:, :], ps[0:1, 7, 0:1]).then_inc(v_step, 1)
                dve.wait_ge(v_step, n[0] + 1)

            @block.tensor
            def _(pe):
                pe.wait_ge(v_w, 1)
                pe.wait_ge(d_cst, 16)
                for b in range(B):
                    nc.tensor.matmul(ps[:, b, :], ident[0:B, b:b + 1].broadcast_to((B, P)), wm[:, :],
                                     start=True, stop=True).then_inc(p_w, 1)
                pe.wait_ge(d_wv, 16)
                pe.wait_ge(v_xwb, B * KS)
                for b in range(B):
                    bank = b % 4
                    if b >= 4:
                        pe.wait_ge(a_hT, KD * (b - 3))
                    for k in range(KS):
                        last = nc.tensor.matmul(ps[:, bank, 0:S], xwb[:, k, b, :], wv[:, k, :],
                                                start=(k == 0), stop=(k == KS - 1))
                    last.then_inc(p_y, 1)
                nc.tensor.matmul(ps[0:1, 7, 0:1], zf[:, :], ones[0:B, 0:1], start=True, stop=True)\
                    .then_inc(p_flag, 1)

            @block.scalar
            def _(act):
                for b in range(B):
                    act.wait_ge(p_y, b + 1)
                    for t in range(KD):
                        nc.scalar.activation(hT[:, t, b, :], ps[:, b % 4, 0:S], ACT.Copy).then_inc(a_hT, 1)
                act.wait_ge(a_hT, B * KD)

        general = ExitStack()
        with general:
            wh = sb(general, "g_wh", [P, KS, 3, DH1])
            gbias = sb(general, "g_bias", [1, D])
            gks = sb(general, "g_ks", [DH1, D])
            qh = sb(general, "g_q", [DH1, D])
            kh = sb(general, "g_k", [DH1, D])
            vh = sb(general, "g_v", [DH1, D])
            vT = sb(general, "g_vT", [P, KD, DH1])
            nmax = sb(general, "g_nmax", [P, KD])
            lsum = sb(general, "g_lsum", [P, KD])
            rl = sb(general, "g_rl", [P, KD])
            e = sb(general, "g_e", [P, D])
            eT = sb(general, "g_eT", [P, KD, P])
            g_in = sem(general, "g_in")
            g_proj = sem(general, "g_proj")
            g_qkv = sem(general, "g_qkv")
            g_vt = sem(general, "g_vt")
            g_vs = sem(general, "g_vs")
            g_s = sem(general, "g_s")
            g_m = sem(general, "g_m")
            g_e = sem(general, "g_e")
            g_t = sem(general, "g_t")
            g_ts = sem(general, "g_ts")
            g_o = sem(general, "g_o")
            g_r = sem(general, "g_r")
            g_done = sem(general, "g_done")

            with nc.Block() as block:
                @block.sync
                def _(sp):
                    go = sp.value_load(flag[0:1, 0:1], min_val=0, max_val=B)
                    with sp.If(go > 0):
                        with sp.Fori(0, B) as b:
                            with sp.Fori(0, NH) as h:
                                n = b * NH + h
                                sp.wait_ge(g_done, n * KD + 1)
                                sp.dma_start(wh[:, :, :, :],
                                             ins["cond_Wh"][bass.ds(h, 1)].rearrange("a p k w d -> p (a k) w d"))\
                                    .then_inc(g_in, 16)
                                sp.dma_start(gbias[:, :], scr_bias[bass.ds(b, 1), :]).then_inc(g_in, 16)
                                sp.dma_start(gks[:, :], scr_ksc[bass.ds(b, 1), :].broadcast_to((DH1, D)))\
                                    .then_inc(g_in, 16)

                @block.tensor
                def _(pe):
                    go = pe.value_load(flag[0:1, 0:1], min_val=0, max_val=B)
                    with pe.If(go > 0):
                        with pe.Fori(0, B) as b:
                            with pe.Fori(0, NH) as h:
                                n = b * NH + h
                                pe.wait_ge(g_in, (n + 1) * 48)
                                for w in range(3):
                                    for k in range(KS):
                                        last = nc.tensor.matmul(
                                            ps[0:DH1, w, :], wh[:, k, w, :],
                                            xall[:, k, bass.ds(b, 1), :].rearrange("p a t -> p (a t)"),
                                            start=(k == 0), stop=(k == KS - 1))
                                last.then_inc(g_proj, 1)
                                pe.wait_ge(g_qkv, (n + 1) * 3)
                                for t in range(KD):
                                    last = nc.tensor.matmul(ps[:, 3, t * DH1:(t + 1) * DH1],
                                                            vh[:, t * P:(t + 1) * P], ident[0:DH1, 0:DH1],
                                                            start=True, stop=True)
                                last.then_inc(g_vt, 1)
                                for q in range(KD):
                                    nq = n * KD + q
                                    pe.wait_ge(g_e, nq + 1)
                                    nc.tensor.matmul(ps[:, 4, :], qh[:, q * P:(q + 1) * P], kh[:, :],
                                                     start=True, stop=False)
                                    nc.tensor.matmul(ps[:, 4, :], ones[0:1, :], gbias[:, :],
                                                     start=False, stop=True).then_inc(g_s, 1)
                                    pe.wait_ge(g_e, nq + 2)
                                    for t in range(KD):
                                        last = nc.tensor.transpose(ps[:, 5, t * P:(t + 1) * P],
                                                                   e[:, t * P:(t + 1) * P], ident)
                                    last.then_inc(g_t, 1)
                                    pe.wait_ge(g_ts, nq + 1)
                                    pe.wait_ge(g_vs, n + 1)
                                    for t in range(KD):
                                        last = nc.tensor.matmul(ps[:, 6, 0:DH1], eT[:, t, :], vT[:, t, :],
                                                                start=(t == 0), stop=(t == KD - 1))
                                    last.then_inc(g_o, 1)
                                pe.wait_ge(g_done, (n + 1) * KD + 1)

                @block.vector
                def _(dve):
                    go = dve.value_load(flag[0:1, 0:1], min_val=0, max_val=B)
                    with dve.If(go > 0):
                        dve.nop().then_inc(g_done, 1)
                        with dve.Fori(0, B) as b:
                            with dve.Fori(0, NH) as h:
                                n = b * NH + h
                                dve.wait_ge(g_proj, n + 1)
                                nc.vector.tensor_copy(qh[:, :], ps[0:DH1, 0, :]).then_inc(g_qkv, 1)
                                nc.vector.tensor_tensor(kh[:, :], ps[0:DH1, 1, :], gks[:, :], ALU.mult)\
                                    .then_inc(g_qkv, 1)
                                nc.vector.tensor_copy(vh[:, :], ps[0:DH1, 2, :]).then_inc(g_qkv, 1)
                                dve.wait_ge(g_vt, n + 1)
                                nc.vector.tensor_copy(vT[:, :, :].rearrange("p t d -> p (t d)"),
                                                      ps[:, 3, 0:KD * DH1]).then_inc(g_vs, 1)
                                for q in range(KD):
                                    nq = n * KD + q
                                    dve.wait_ge(g_s, nq + 1)
                                    nc.vector.tensor_reduce(nmax[:, q:q + 1], ps[:, 4, :], AX.X, ALU.max,
                                                            negate=True).then_inc(g_m, 1)
                                    dve.wait_ge(g_t, nq + 1)
                                    nc.vector.tensor_copy(eT[:, :, :].rearrange("p t d -> p (t d)"), ps[:, 5, :])\
                                        .then_inc(g_ts, 1)
                                    dve.wait_ge(g_e, nq + 2)
                                    nc.vector.reciprocal(rl[:, q:q + 1], lsum[:, q:q + 1]).then_inc(g_r, 1)
                                    dve.wait_ge(g_r, nq + 1)
                                    dve.wait_ge(g_o, nq + 1)
                                    nc.vector.tensor_scalar(
                                        hT[:, q, bass.ds(b, 1), bass.ds(h * DH1, DH1)].rearrange("p a d -> p (a d)"),
                                        ps[:, 6, 0:DH1], rl[:, q:q + 1], None, ALU.mult).then_inc(g_done, 1)

                @block.scalar
                def _(act):
                    go = act.value_load(flag[0:1, 0:1], min_val=0, max_val=B)
                    with act.If(go > 0):
                        act.nop().then_inc(g_e, 1)
                        with act.Fori(0, B) as b:
                            with act.Fori(0, NH) as h:
                                n = b * NH + h
                                for q in range(KD):
                                    nq = n * KD + q
                                    act.wait_ge(g_m, nq + 1)
                                    nc.scalar.activation(e[:, :], ps[:, 4, :], ACT.Exp, bias=nmax[:, q:q + 1],
                                                         accum_out=lsum[:, q:q + 1]).then_inc(g_e, 1)


def second_attention(nc, ins, ps, cst, ident, x1T, hT, sb, sem):
    st = ExitStack()
    with st:
        tab = sb(st, "tab", [P, T_ALL])
        wq = sb(st, "wq", [P, KD, D])
        wk = sb(st, "wk", [P, KD, D])
        wv = sb(st, "wv2", [P, KD, D])
        wo = sb(st, "wo", [P, KD, D])
        masks = sb(st, "masks", [P, 4, P], BF16)
        hb = sb(st, "hb", [P, KD, S])
        raw = sb(st, "raw", [P, 2, KD, S])
        rot = sb(st, "rot", [P, 2, KD, S])
        kz = sb(st, "kz", [P, HPC, KD, S])
        v = sb(st, "v", [P, KS, D])
        tmp = sb(st, "tmp", [P, KD, S])
        E = sb(st, "E", [P, NEX, P + S])
        En = sb(st, "En", [P, NEX, P + S])
        ET = sb(st, "ET", [P, HPC, P + S])
        nm = sb(st, "nm", [P, 2, NH, 2])
        ls = sb(st, "ls", [P, 2, NH, 2])
        rl = sb(st, "rl", [P, 2, NH, 2])
        rdiag = sb(st, "rdiag", [P, NH, 2, NH])
        tsum = sb(st, "tsum", [NH, S])
        work = sb(st, "work", [NH, S])
        top8 = sb(st, "top8", [NH, 8])
        code = sb(st, "code", [NH, S])
        cmax = sb(st, "cmax", [NH, 1])
        light = sb(st, "light", [NH, S])
        lcol = sb(st, "lcol", [P, KS, NH])
        dg = sb(st, "dg", [P, NDG, KS, P], BF16)
        oT = sb(st, "oT", [P, KD, S])

        d_w = sem(st, "e_w")
        d_tab = sem(st, "e_tab")
        v_init = sem(st, "e_init")
        c_hb = sem(st, "c_hb")
        p_qk = sem(st, "p_qk")
        a_raw = sem(st, "a_raw")
        p_rot = sem(st, "p_rot")
        v_rot = sem(st, "v_rot")
        a_kz = sem(st, "a_kz")
        v_kz = sem(st, "v_kz")
        p_v = sem(st, "p_v")
        a_v = sem(st, "a_v")
        p_s = sem(st, "p_s")
        v_m = sem(st, "v_m")
        a_e = sem(st, "a_e")
        v_r = sem(st, "v_r")
        v_d = sem(st, "v_d")
        p_c = sem(st, "p_c")
        v_k = sem(st, "v_k")
        p_l = sem(st, "p_l")
        v_l = sem(st, "v_l")
        g_d = sem(st, "g_d")
        v_n = sem(st, "v_n")
        p_t = sem(st, "p_t")
        a_t = sem(st, "a_t")
        p_av = sem(st, "p_av")
        a_o = sem(st, "a_o")
        p_o = sem(st, "p_o")
        v_x = sem(st, "v_x")

        with nc.Block() as block:
            @block.sync
            def _(sp):
                sp.dma_start(tab[:, :], ins["table"]).then_inc(d_tab, 16)
                for t, name in ((wq, "attn_WqT"), (wk, "attn_WkT"), (wv, "attn_WvT"), (wo, "attn_WoT")):
                    sp.dma_start(t[:, :, :], ins[name].rearrange("(k p) o -> p k o", p=P)).then_inc(d_w, 16)

            @block.gpsimd
            def _(pool):
                def diagonals(b):
                    pool.wait_ge(v_l, b + 1)
                    for h in range(NH):
                        if h >= NDG:
                            pool.wait_ge(p_s, b * 2 * NH + NH + h - NDG + 2)
                        nc.gpsimd.tensor_tensor(dg[:, h % NDG, :, :],
                                                masks[:, 0, :].unsqueeze(1).broadcast_to((P, KS, P)),
                                                lcol[:, :, h:h + 1].broadcast_to((P, KS, P)), ALU.mult)\
                            .then_inc(g_d, 1)

                with pool.Fori(0, B) as b:
                    pool.wait_ge(p_v, b + 1)
                    nc.gpsimd.tensor_copy(hb[:, :, :], hT[:, :, bass.ds(b, 1), :].rearrange("p k a s -> p k (a s)"))\
                        .then_inc(c_hb, 1)
                    diagonals(b)

            @block.tensor
            def _(pe):
                pe.nop().then_inc(p_v, 1)
                pe.nop().then_inc(p_s, 1)
                pe.wait_ge(d_w, 64)
                pe.wait_ge(d_tab, 16)
                pe.wait_ge(v_init, 3)

                def scores(b, r, h, more=False):
                    n = b * (2 * NH) + r * NH + h
                    bank = h % 4
                    m, q = h // HPC, h % HPC
                    if r == 0 and h < 4:
                        if h == 0:
                            pe.wait_ge(v_x, b * KD + 1)
                    else:
                        pe.wait_ge(a_e, (n - 4 + 1) * 2)
                    if r == 0 and h == 0:
                        pe.wait_ge(v_rot, b * 6 + 6)
                    if r == 0 and h < 2:
                        pe.wait_ge(a_kz, b * 2 + h + 2)
                    elif r == 0 and h < HPC:
                        pe.wait_ge(v_kz, b * 2 + h - 1)
                    if r == 1 and h == 0 and more:
                        pe.wait_ge(a_raw, b * 2 + 4)
                    kw = dict(stop=False, skip_group_check=True)
                    nc.tensor.matmul(ps[:, bank, 0:P], masks[:, 0, :], masks[:, 1, :], start=True, **kw)
                    nc.tensor.matmul(ps[:, bank, 2 * P:3 * P], masks[:, 0, :], masks[:, 1, :], start=False, **kw)
                    if r == 1:
                        pe.wait_ge(g_d, b * NH + h + 1)
                        d = dg[:, h % NDG, :, :]
                        nc.tensor.matmul(ps[:, bank, 0:P], masks[:, 2, :], d[:, 0, :], start=False, **kw)
                        nc.tensor.matmul(ps[:, bank, P:2 * P], masks[:, 3, :], d[:, 0, :], start=False, **kw)
                        nc.tensor.matmul(ps[:, bank, 2 * P:3 * P], masks[:, 2, :], d[:, 1, :], start=False, **kw)
                    nc.tensor.matmul(ps[:, bank, 0:P], rot[:, 0, m, 0:P], kz[:, q, m, 0:P],
                                     start=False, stop=True, skip_group_check=True)
                    nc.tensor.matmul(ps[:, bank, P:P + S], rot[:, 0, m, P:S], kz[:, q, m, :],
                                     start=False, stop=True, skip_group_check=True).then_inc(p_s, 1)

                def project(b):
                    for i, w in enumerate((wq, wk)):
                        for m in range(KD):
                            for k in range(KD):
                                last = nc.tensor.matmul(ps[:, 2 * i + m // 2, (m % 2) * S:(m % 2 + 1) * S],
                                                        w[:, k, m * P:(m + 1) * P],
                                                        hT[:, k, bass.ds(b, 1), :].rearrange("p a s -> p (a s)"),
                                                        start=(k == 0 and m % 2 == 0), stop=(k == KD - 1),
                                                        skip_group_check=True)
                        last.then_inc(p_qk, 1)

                def swap(b, i):
                    pe.wait_ge(a_raw, b * 2 + i + 1)
                    for m in range(KD):
                        last = nc.tensor.matmul(ps[:, 4 + 2 * i + m // 2, (m % 2) * S:(m % 2 + 1) * S],
                                                tab[:, C_ROT:C_ROT + P], raw[:, i, m, :],
                                                start=(m % 2 == 0), stop=True, skip_group_check=True)
                    last.then_inc(p_rot, 1)

                def batch(b, more):
                    for h in range(NH + AHEAD):
                        if h < NH:
                            scores(b, 0, h)
                        if h >= AHEAD:
                            g = h - AHEAD
                            pe.wait_ge(v_d, b * NH + g + 1)
                            nc.tensor.matmul(ps[0:NH, 4, 0:P], rdiag[:, g, 0, :], E[:, g % NEX, 0:P],
                                             start=(g == 0), stop=False, skip_group_check=True)
                            nc.tensor.matmul(ps[0:NH, 4, 0:S], rdiag[:, g, 1, :], E[:, g % NEX, P:P + S],
                                             start=False, stop=(g == NH - 1),
                                             skip_group_check=True).then_inc(p_c, 1)
                    pe.wait_ge(c_hb, b + 1)
                    for c in range(KS):
                        for k in range(KD):
                            last = nc.tensor.matmul(ps[:, 6 + c, :], hb[:, k, c * P:(c + 1) * P], wv[:, k, :],
                                                    start=(k == 0), stop=(k == KD - 1))
                    last.then_inc(p_v, 1)
                    if more:
                        pe.wait_ge(a_e, (b * 2 * NH + NH) * 2)
                        project(b + 1)
                    pe.wait_ge(v_k, b * K_STEPS + K_STEPS)
                    for c in range(KS):
                        last = nc.tensor.matmul(ps[:, 5, c * NH:(c + 1) * NH], light[:, c * P:(c + 1) * P],
                                                ident[0:NH, 0:NH], start=True, stop=True)
                    last.then_inc(p_l, 1)
                    for h in range(NH + AHEAD + 1):
                        if h < NH:
                            scores(b, 1, h, more)
                        g = h - AHEAD
                        if 0 <= g < NH:
                            n = b * NH + g
                            pe.wait_ge(v_n, (n + 1) * 2 + 1)
                            if g < 2:
                                if g == 0:
                                    pe.wait_ge(v_l, b + 1)
                            else:
                                pe.wait_ge(a_t, n - 1)
                            bank = 4 + g % 2
                            for c in range(3):
                                last = nc.tensor.transpose(ps[:, bank, c * P:(c + 1) * P],
                                                           En[:, g % NEX, c * P:(c + 1) * P], ident)
                            last.then_inc(p_t, 1)
                        g = h - AHEAD - 1
                        if g >= 0 and g % HPC == HPC - 1:
                            m = g // HPC
                            pe.wait_ge(a_t, b * NH + g + 1)
                            if m == 0:
                                pe.wait_ge(a_v, b + 1)
                            if m >= 2:
                                pe.wait_ge(a_o, b * KD + m - 1)
                            for q in range(HPC):
                                hh = m * HPC + q
                                o = ps[q * DH2:(q + 1) * DH2, 6 + m % 2, :]
                                nc.tensor.matmul(o[:, 0:S], v[:, 0, hh * DH2:(hh + 1) * DH2], ET[:, q, 0:S],
                                                 start=True, stop=False, tile_position=(0, q * DH2),
                                                 skip_group_check=True)
                                last = nc.tensor.matmul(o[:, P:S], v[:, 1, hh * DH2:(hh + 1) * DH2], ET[:, q, S:S + P],
                                                        start=False, stop=True, tile_position=(0, q * DH2),
                                                        skip_group_check=True)
                            last.then_inc(p_av, 1)
                    if more:
                        swap(b + 1, 0)
                    pe.wait_ge(a_o, (b + 1) * KD)
                    if more:
                        swap(b + 1, 1)
                    for m in range(KD):
                        for k in range(KD):
                            last = nc.tensor.matmul(ps[:, m, 0:S], wo[:, k, m * P:(m + 1) * P], oT[:, k, :],
                                                    start=(k == 0), stop=(k == KD - 1))
                        last.then_inc(p_o, 1)

                project(0)
                for i in range(2):
                    swap(0, i)
                with pe.Fori(0, B - 1) as b:
                    batch(b, True)
                batch(B - 1, False)

            @block.scalar
            def _(act):
                def exps(b, r, h):
                    n = b * (2 * NH) + r * NH + h
                    act.wait_ge(v_m, n + 1)
                    if r == 0:
                        if h >= NEX:
                            act.wait_ge(p_c, b * NH + h - NEX + 1)
                        else:
                            act.wait_ge(v_n, b * (2 * NH) + 1)
                    else:
                        if h >= NEX:
                            act.wait_ge(v_n, (b * NH + h - NEX + 1) * 2 + 1)
                        else:
                            act.wait_ge(p_c, (b + 1) * NH)
                    bank = h % 4
                    nc.scalar.activation(E[:, h % NEX, 0:P], ps[:, bank, 0:P], ACT.Exp, bias=nm[:, r, h, 0:1],
                                         accum_out=ls[:, r, h, 0:1]).then_inc(a_e, 1)
                    nc.scalar.activation(E[:, h % NEX, P:P + S], ps[:, bank, P:P + S], ACT.Exp,
                                         bias=nm[:, r, h, 1:2], accum_out=ls[:, r, h, 1:2]).then_inc(a_e, 1)

                act.nop().then_inc(a_kz, 1)
                act.wait_ge(d_tab, 16)
                def copy_raw(b):
                    for i in range(2):
                        act.wait_ge(p_qk, b * 2 + i + 1)
                        nc.scalar.activation(raw[:, i, :, :].rearrange("p m s -> p (m s)"),
                                             ps[:, 2 * i:2 * i + 2, :].rearrange("p a n -> p (a n)"),
                                             ACT.Copy).then_inc(a_raw, 1)

                def batch(b, more):
                    act.wait_ge(v_rot, b * 6 + 6)
                    for q in range(2):
                        nc.scalar.activation(kz[:, q, :, :].rearrange("p m s -> p (m s)"),
                                             rot[:, 1, :, :].rearrange("p m s -> p (m s)"), ACT.Copy,
                                             scale=tab[:, C_HEAD + q:C_HEAD + q + 1]).then_inc(a_kz, 1)
                    for h in range(NH):
                        exps(b, 0, h)
                    act.wait_ge(p_v, b + 2)
                    nc.scalar.activation(v[:, :, :].rearrange("p c d -> p (c d)"),
                                         ps[:, 6:8, :].rearrange("p a n -> p (a n)"), ACT.Copy).then_inc(a_v, 1)
                    if more:
                        copy_raw(b + 1)
                    for h in range(NH + 2):
                        if h < NH:
                            exps(b, 1, h)
                        g = h - 2
                        if g >= 0:
                            n = b * NH + g
                            act.wait_ge(p_t, n + 1)
                            if g % HPC == 0 and g >= HPC:
                                act.wait_ge(p_av, b * KD + g // HPC)
                            nc.scalar.activation(ET[:, g % HPC, :], ps[:, 4 + g % 2, 0:P + S], ACT.Copy)\
                                .then_inc(a_t, 1)
                            if g % HPC == 1 and g >= HPC:
                                m = g // HPC - 1
                                act.wait_ge(p_av, b * KD + m + 1)
                                nc.scalar.activation(oT[:, m, :], ps[:, 6 + m % 2, 0:S], ACT.Copy).then_inc(a_o, 1)
                    act.wait_ge(p_av, (b + 1) * KD)
                    nc.scalar.activation(oT[:, KD - 1, :], ps[:, 6 + (KD - 1) % 2, 0:S], ACT.Copy).then_inc(a_o, 1)

                copy_raw(0)
                with act.Fori(0, B - 1) as b:
                    batch(b, True)
                batch(B - 1, False)

            @block.vector
            def _(dve):
                dve.wait_ge(d_tab, 16)
                nc.vector.tensor_copy(masks[:, 0, :], ident)
                for i, c in enumerate((C_CAUS, C_NB0, C_NB1)):
                    last = nc.vector.tensor_copy(masks[:, i + 1, :], tab[:, c:c + P])
                last.then_inc(v_init, 1)
                nc.vector.memset(rdiag[:, :, :, :], 0.0).then_inc(v_init, 1)
                nc.vector.memset(ls[:, :, :, :], 1.0).then_inc(v_init, 1)
                dve.nop().then_inc(v_x, 1)
                dve.nop().then_inc(v_n, 1)
                dve.wait_ge(v_init, 3)

                def maxima(b, r, h):
                    n = b * (2 * NH) + r * NH + h
                    dve.wait_ge(p_s, n + 2)
                    bank = h % 4
                    nc.vector.tensor_reduce(nm[:, r, h, 0:1], ps[:, bank, 0:P], AX.X, ALU.max, negate=True)
                    nc.vector.tensor_reduce(nm[:, r, h, 1:2], ps[:, bank, P:P + S], AX.X, ALU.max,
                                            negate=True).then_inc(v_m, 1)

                def recip(b, r, h):
                    n = b * (2 * NH) + r * NH + h
                    dve.wait_ge(a_e, (n + 1) * 2)
                    nc.vector.reciprocal(rl[:, r, h, :], ls[:, r, h, :]).then_inc(v_r, 1)
                    dve.wait_ge(v_r, n + 1)

                def rotate(b):
                    for i, (c, s) in enumerate(((C_COSQ, C_SINQ), (C_COSK, C_SINK))):
                        dve.wait_ge(p_rot, b * 2 + i + 1)
                        if i == 0:
                            dve.wait_ge(p_s, b * 2 * NH + 1)
                            dve.wait_ge(a_kz, b * 2 + 1)
                        cos = tab[:, c:c + S].unsqueeze(1).broadcast_to((P, KD, S))
                        sin = tab[:, s:s + S].unsqueeze(1).broadcast_to((P, KD, S))
                        nc.vector.tensor_tensor(tmp[:, :, :],
                                                ps[:, 4 + 2 * i:6 + 2 * i, :].rearrange("p a (m s) -> p (a m) s", s=S),
                                                sin, ALU.mult).then_inc(v_rot, 1)
                        nc.vector.tensor_tensor(rot[:, i, :, :], raw[:, i, :, :], cos, ALU.mult).then_inc(v_rot, 1)
                        dve.wait_ge(v_rot, b * 6 + 3 * i + 2)
                        nc.vector.tensor_tensor(rot[:, i, :, :], rot[:, i, :, :], tmp[:, :, :], ALU.add)\
                            .then_inc(v_rot, 1)
                        dve.wait_ge(v_rot, b * 6 + 3 * i + 3)
                    for q in range(2, HPC):
                        nc.vector.tensor_scalar(kz[:, q, :, :], rot[:, 1, :, :], tab[:, C_HEAD + q:C_HEAD + q + 1],
                                                None, ALU.mult).then_inc(v_kz, 1)

                def batch(b, more):
                    for h in range(NH + 1):
                        if h < NH:
                            maxima(b, 0, h)
                        if h >= 1:
                            g = h - 1
                            recip(b, 0, g)
                            nc.vector.tensor_copy(rdiag[:, g, :, g], rl[:, 0, g, :]).then_inc(v_d, 1)
                    dve.wait_ge(p_c, (b + 1) * NH)
                    c = [0]

                    def step(i_):
                        c[0] += 1
                        i_.then_inc(v_k, 1)
                        dve.drain()

                    step(nc.vector.tensor_copy(tsum[:, :], ps[0:NH, 4, 0:S]))
                    src = tsum
                    for _ in range(HEAVY // 8):
                        step(nc.vector.max(top8[:, :], src[:, :]))
                        step(nc.vector.match_replace(work[:, :], top8[:, :], src[:, :], -1.0))
                        src = work
                    for _ in range(HEAVY % 8):
                        step(nc.vector.max(top8[:, :], work[:, :]))
                        step(nc.vector.scalar_tensor_tensor(out=code[:, :], in0=work[:, :], scalar=top8[:, 0:1],
                                                            in1=tab[0:NH, C_DESC:C_DESC + S],
                                                            op0=ALU.is_equal, op1=ALU.mult))
                        step(nc.vector.tensor_reduce(cmax[:, :], code[:, :], AX.X, ALU.max))
                        step(nc.vector.tensor_scalar(code[:, :], code[:, :], cmax[:, 0:1], -1e6,
                                                     ALU.is_equal, ALU.mult))
                        step(nc.vector.tensor_tensor(work[:, :], work[:, :], code[:, :], ALU.add))
                    step(nc.vector.tensor_scalar(light[:, :], work[:, :], 0.0, None, ALU.is_ge))
                    assert c[0] == K_STEPS
                    dve.wait_ge(p_l, b + 1)
                    nc.vector.tensor_copy(lcol[:, :, :].rearrange("p c h -> p (c h)"), ps[:, 5, 0:KS * NH])\
                        .then_inc(v_l, 1)

                    for h in range(NH + 1):
                        if h < NH:
                            maxima(b, 1, h)
                        if h >= 1:
                            g = h - 1
                            recip(b, 1, g)
                            if g >= NEX:
                                dve.wait_ge(p_t, b * NH + g - NEX + 1)
                            nc.vector.tensor_scalar(En[:, g % NEX, 0:P], E[:, g % NEX, 0:P], rl[:, 1, g, 0:1], None,
                                                    ALU.mult).then_inc(v_n, 1)
                            nc.vector.tensor_scalar(En[:, g % NEX, P:P + S], E[:, g % NEX, P:P + S], rl[:, 1, g, 1:2],
                                                    None, ALU.mult).then_inc(v_n, 1)
                    if more:
                        rotate(b + 1)
                    for m in range(KD):
                        dve.wait_ge(p_o, b * KD + m + 1)
                        xv = x1T[:, m, :, bass.ds(b, 1)].rearrange("p s a -> p (s a)")
                        nc.vector.tensor_tensor(xv, ps[:, m, 0:S], xv, ALU.add).then_inc(v_x, 1)

                rotate(0)
                with dve.Fori(0, B - 1) as b:
                    batch(b, True)
                batch(B - 1, False)


AHEAD = 2
NEX = 3
NDG = 3
K_STEPS = 2 + 2 * (HEAVY // 8) + 5 * (HEAVY % 8)


NCH = NE * FC
UP_AT = [1 + i for i in range(NCH)]
ACT_AT = [x + 1 for x in UP_AT]
GATE_AT = [max(ACT_AT[i] + 1, 6 + 2 * (i // FC) + i % FC // 2) for i in range(NCH)]
CAST_AT = [x + 1 for x in GATE_AT]
REST_AT = [x + 2 for x in GATE_AT]
DOWN_FIRST, DOWN_LAST = 9, SPT - 3
DOWN_AT = [[max(REST_AT[i] + 1, DOWN_FIRST + (2 * i + half) * (DOWN_LAST - DOWN_FIRST + 1) // (2 * NCH))
            for half in range(2)] for i in range(NCH)]
BCAST_AT = [GATE_AT[e * FC] - 2 for e in range(NE)]
B2_AT = 5
TB = max(sum(ACT_AT[j] <= REST_AT[i] for j in range(i, NCH)) for i in range(NCH))
RING = max(sum(CAST_AT[j] <= DOWN_AT[i][1] for j in range(i, NCH)) for i in range(NCH))
assert all(UP_AT[i] > ACT_AT[i - 2] - 1 for i in range(2, NCH))
assert all(CAST_AT[i] > DOWN_AT[i - RING][1] for i in range(RING, NCH))
assert all(ACT_AT[i] > REST_AT[i - TB] for i in range(TB, NCH))
assert all(BCAST_AT[e] > BCAST_AT[e - 1] + 1 for e in range(1, NE)) and BCAST_AT[0] >= 4
assert all(BCAST_AT[e] + 1 > GATE_AT[(e - 1) * FC - 1] for e in range(2, NE))
assert DOWN_AT[NCH - 1][1] < SPT - 2
R_STEPS = 17


def gru_and_ffn(nc, ins, out, ps, cst, ident, x1T, sb, sem):
    top = ExitStack()
    with top:
        whf = sb(top, "whf", [P, KD, G3])
        w1f = sb(top, "w1f", [P, KD, 2, EH * HFP])
        w2f = sb(top, "w2f", [P, FC, 2, EH * D])
        gi = sb(top, "gi", [P, NQ, SPT, B])
        h32 = sb(top, "h32", [P, KD, B])
        hp = sb(top, "hp", [P, KD, 2, B], F16)
        gwp = sb(top, "gwp", [P, KD, 2, NE], F16)
        b1 = sb(top, "b1", [P, FC, NE])
        b1s = sb(top, "b1s", [P, FC, NE])
        b2 = sb(top, "b2", [NE, D])
        gb = sb(top, "gb", [P, NE])
        bhp = sb(top, "bhp", [2, D], F16)
        ones2 = sb(top, "ones2", [2, 2 * B], F16)
        sc = sb(top, "sc", [P, N_SC])
        gi_d = nc.dram_tensor("gi_d", [P, NQ, S, B], F32).ap()
        prepare(nc, ins, ps, cst, ident, x1T, whf, w1f, w2f, gi_d, h32, hp, gwp, b1, b1s, b2, gb, bhp, ones2, sc, sb, sem)
        recurrence_and_ffn(nc, ins, out, ps, cst, ident, x1T, whf, w1f, w2f, gi, gi_d, h32, hp, gwp, b1, b1s, b2, gb,
                           bhp, ones2, sc, sb, sem)


BEFORE = 3
O_WHH, O_H, O_W1, O_W2, O_GW, O_B1 = range(6)
S_H, S_WHH, S_W1, S_W2, S_GW, S_UNG, S_UN1, S_UN1I, S_CB, S_UN2, S_UN2I, S_UNR, S_U, S_T = range(6, 20)
N_SC = 20


def prepare(nc, ins, ps, cst, ident, x1T, whf, w1f, w2f, gi_d, h32, hp, gwp, b1, b1s, b2, gb, bhp, ones2, sc, sb, sem):
    st = ExitStack()
    with st:
        wi = sb(st, "wi", [P, KD, G3])
        stage = sb(st, "stage", [P, 4, TT])
        tmp = sb(st, "wtmp", [P, EH * D])
        bgi = sb(st, "bgi", [P, 2, NQ])
        bsum = sb(st, "bsum", [P, NQ])
        gw = sb(st, "gw", [P, KD, NE])
        gb2 = sb(st, "gb2", [P, 2, NE])
        mx = sb(st, "mx", [P, 6, KD + 1])
        mxa = sb(st, "mxa", [P, 6])
        mx1 = sb(st, "mx1", [1, 6])
        ones1 = sb(st, "ones1", [1, P])
        bh32 = sb(st, "bh32", [2, D])
        d_i = sem(st, "q_wi")
        d_s = sem(st, "q_small")
        d_w = sem(st, "q_big")
        d_g = [sem(st, f"q_gi{j}") for j in range(4)]
        v_z = sem(st, "q_zero")
        v_b = sem(st, "q_bias")
        v_a = sem(st, "q_v")
        p_a = sem(st, "q_p")
        p_i = sem(st, "q_pi")
        a_i = sem(st, "q_ai")

        with nc.Block() as block:
            @block.sync
            def _(sp):
                sp.dma_start(wi[:, :, :], ins["W_ih"].rearrange("(k p) n -> p k n", p=P)).then_inc(d_i, 16)
                sp.dma_start(bgi[:, 0, :], ins["b_ih"]).then_inc(d_s, 16)
                sp.dma_start(bgi[:, 1, :], ins["b_hh"]).then_inc(d_s, 16)
                sp.dma_start(h32[:, :, :], ins["condT"].rearrange("(k p) b -> p k b", p=P)).then_inc(d_s, 16)
                sp.dma_start(gw[:, :, :], ins["gate_wT"].rearrange("(k p) e -> p k e", p=P)).then_inc(d_s, 16)
                sp.dma_start(gb2[:, 0, :], ins["gate_b"].broadcast_to((P, NE))).then_inc(d_s, 16)
                sp.dma_start(gb2[:, 1, :], ins["bias"].broadcast_to((P, NE))).then_inc(d_s, 16)
                sp.dma_start(b2[:, :], ins["b2"]).then_inc(d_s, 16)
                sp.dma_start(bh32[:, :], ins["b_hh_n"].broadcast_to((2, D))).then_inc(d_s, 16)
                sp.wait_ge(v_z, 3)
                for c in range(FC):
                    rows = P if c < FC - 1 else HL
                    sp.dma_start(b1[0:rows, c, :], ins["b1T"][c * P:c * P + rows]).then_inc(d_s, 16)
                sp.dma_start(whf[:, :, :], ins["W_hh"].rearrange("(k p) n -> p k n", p=P)).then_inc(d_w, 16)
                for k in range(KD):
                    sp.dma_start(w1f[:, k, :, :].rearrange("p a (e h) -> p (a e) h", h=HFP)[:, :, 0:HF],
                                 ins["w1T"][k * P:(k + 1) * P, :].rearrange("p (e h) -> p e h", h=HF)).then_inc(d_w, 16)
                for c in range(FC):
                    rows = P if c < FC - 1 else HL
                    sp.dma_start(w2f[0:rows, c, :, :].rearrange("p a n -> p (a n)"),
                                 ins["w2T"][c * P:c * P + rows].rearrange("p e d -> p (e d)")).then_inc(d_w, 16)
                with sp.Fori(0, NT) as t:
                    for q in range(NQ):
                        sp.wait_ge(a_i, t * NQ + q + 2)
                        sp.dma_start(gi_d[:, q, bass.ds(t * SPT, SPT), :].rearrange("p s b -> p (s b)"),
                                     stage[:, q % 4, :]).then_inc(d_g[q % 4], 16)
                for j in range(4):
                    sp.wait_ge(d_g[j], 16 * NT * NQ // 4 + 16)

            @block.tensor
            def _(pe):
                def tiles(t0, t1):
                    with pe.Fori(t0, t1) as t:
                        for q in range(NQ):
                            if q < 4:
                                pe.wait_ge(a_i, t * NQ + 1)
                            else:
                                pe.wait_ge(a_i, t * NQ + q - 2)
                            for k in range(KD):
                                last = nc.tensor.matmul(
                                    ps[:, q % 4, 0:TT], wi[:, k, q * P:(q + 1) * P],
                                    x1T[:, k, bass.ds(t * SPT, SPT), :].rearrange("p s b -> p (s b)"),
                                    start=(k == 0), stop=(k == KD - 1))
                            last.then_inc(p_i, 1)

                pe.wait_ge(d_i, 16)
                tiles(0, BEFORE)
                pe.wait_ge(v_a, 9)
                for i in range(6):
                    last = nc.tensor.transpose(ps[0:1, 6 + i // 3, (i % 3) * P:(i % 3 + 1) * P], mxa[:, i:i + 1], ident)
                last.then_inc(p_a, 1)
                pe.wait_ge(v_a, 11)
                nc.tensor.matmul(ps[:, 6, 0:6], ones1[:, :], mx1[:, :], start=True, stop=True).then_inc(p_a, 1)
                tiles(BEFORE, NT)

            @block.scalar
            def _(act):
                act.wait_ge(v_b, 1)
                act.nop().then_inc(a_i, 1)
                with act.Fori(0, NT) as t:
                    for q in range(NQ):
                        act.wait_ge(d_g[q % 4], t * (16 * NQ // 4) + 16 * (q // 4) + 16)
                        act.wait_ge(p_i, t * NQ + q + 1)
                        nc.scalar.activation(stage[:, q % 4, :], ps[:, q % 4, 0:TT], ACT.Identity,
                                             bias=bsum[:, q:q + 1]).then_inc(a_i, 1)

            @block.gpsimd
            def _(pool):
                for j in range(4):
                    pool.nop().then_inc(d_g[j], 16)
                nc.gpsimd.memset(w1f[:, :, :, :].rearrange("p k a (e h) -> p (k a e) h", h=HFP)[:, :, HF:HFP], 0.0)\
                    .then_inc(v_z, 1)
                pool.wait_ge(v_z, 1)
                nc.gpsimd.memset(w2f[HL:P, FC - 1, :, :], 0.0).then_inc(v_z, 1)
                pool.wait_ge(v_z, 2)
                nc.gpsimd.memset(b1[:, :, :], 0.0).then_inc(v_z, 1)

            @block.vector
            def _(dve):
                n = [0]

                def step(i_):
                    n[0] += 1
                    i_.then_inc(v_a, 1)
                    dve.wait_ge(v_a, n[0])

                def big(o, i_):
                    return nc.vector.tensor_reduce(o, i_, AX.XY if len(i_.shape) == 3 else AX.X, ALU.max,
                                                   apply_absolute_value=True)

                dve.wait_ge(d_s, 16 * (8 + FC))
                step(nc.vector.tensor_copy(bsum[:, :], bgi[:, 0, :]))
                nc.vector.tensor_tensor(bsum[:, 0:2 * KD], bgi[:, 0, 0:2 * KD], bgi[:, 1, 0:2 * KD], ALU.add)\
                    .then_inc(v_b, 1)
                step(nc.vector.memset(ones2[:, :], 0.0))
                step(nc.vector.tensor_tensor(gb[:, :], gb2[:, 0, :], gb2[:, 1, :], ALU.add))
                step(nc.vector.memset(mx[:, :, :], 0.0))
                step(nc.vector.memset(ones1[:, :], 1.0))
                big(mx[:, O_H, 0:1], h32[:, :, :])
                big(mx[:, O_GW, 0:1], gw[:, :, :])
                big(mx[:, O_WHH, KD:KD + 1], bgi[:, 1, 2 * KD:NQ])
                step(big(mx[:, O_B1, 0:1], b1[:, :, :]))
                dve.wait_ge(d_w, 16 * (1 + KD + FC))
                for k in range(KD):
                    big(mx[:, O_WHH, k:k + 1], whf[:, k, :])
                    big(mx[:, O_W1, k:k + 1], w1f[:, k, :, :])
                for c in range(FC):
                    last = big(mx[:, O_W2, c:c + 1], w2f[:, c, :, :])
                step(last)
                step(nc.vector.tensor_reduce(mxa[:, :], mx[:, :, :], AX.X, ALU.max))
                dve.wait_ge(v_a, 8)
                step(nc.vector.memset(mx1[:, :], 0.0))
                dve.wait_ge(p_a, 1)
                nc.vector.tensor_reduce(mx1[:, 0:3], ps[0:1, 6, 0:3 * P].rearrange("p (i n) -> p i n", i=3), AX.X, ALU.max)
                step(nc.vector.tensor_reduce(mx1[:, 3:6], ps[0:1, 7, 0:3 * P].rearrange("p (i n) -> p i n", i=3),
                                             AX.X, ALU.max))
                nc.vector.tensor_scalar(mx1[:, O_H:O_H + 1], mx1[:, O_H:O_H + 1], 1.0, None, ALU.max).then_inc(v_a, 1)
                n[0] += 1
                dve.wait_ge(p_a, 2)
                dve.wait_ge(v_a, n[0])
                step(nc.vector.tensor_scalar(sc[:, 0:6], ps[:, 6, 0:6], 1e-6, None, ALU.max))

                def pow2(i, j):
                    step(nc.vector.tensor_scalar(sc[:, i:j].bitcast(I32), sc[:, i:j].bitcast(I32), 0x7F800000, None,
                                                 ALU.bitwise_and))

                def times(o, a, b, f=1.0):
                    step(nc.vector.tensor_scalar(sc[:, o:o + 1], sc[:, a:a + 1], sc[:, b:b + 1], f, ALU.mult, ALU.mult))

                def inverse(o, a, f=1.0):
                    step(nc.vector.reciprocal(sc[:, o:o + 1], sc[:, a:a + 1]))
                    if f != 1.0:
                        step(nc.vector.tensor_scalar(sc[:, o:o + 1], sc[:, o:o + 1], f, None, ALU.mult))

                pow2(0, 6)
                for o, a in ((S_H, O_H), (S_WHH, O_WHH), (S_W1, O_W1), (S_W2, O_W2), (S_GW, O_GW)):
                    inverse(o, a, 2.0 ** 14)
                times(S_T, O_W1, O_H, 4.0 * D)
                step(nc.vector.scalar_tensor_tensor(out=sc[:, S_U:S_U + 1], in0=sc[:, O_B1:O_B1 + 1], scalar=2.0,
                                                    in1=sc[:, S_T:S_T + 1], op0=ALU.mult, op1=ALU.add))
                pow2(S_U, S_U + 1)
                step(nc.vector.reciprocal(sc[:, S_U:S_U + 1], sc[:, S_U:S_U + 1]))
                step(nc.vector.tensor_scalar(sc[:, S_U:S_U + 1], sc[:, S_U:S_U + 1], 2.0 ** 14, None, ALU.mult))
                times(S_T, S_WHH, S_H)
                inverse(S_UNG, S_T)
                times(S_UN1I, S_W1, S_H)
                inverse(S_UN1, S_UN1I)
                times(S_CB, S_U, S_UN1)
                times(S_UN2I, S_W2, S_U)
                inverse(S_UN2, S_UN2I)
                times(S_T, S_GW, S_H)
                inverse(S_UNR, S_T)

                def split(f32, s, width):
                    t = tmp[:, 0:width]
                    half = f32.bitcast(F16)
                    step(nc.vector.tensor_scalar(t, f32, sc[:, s:s + 1], None, ALU.mult))
                    step(nc.vector.tensor_copy(half[:, 0:width], t))
                    step(nc.vector.tensor_tensor(half[:, width:2 * width], t, half[:, 0:width], ALU.subtract))

                for k in range(KD):
                    split(whf[:, k, :], S_WHH, G3)
                for k in range(KD):
                    for a in range(2):
                        split(w1f[:, k, a, :], S_W1, EH * HFP)
                for c in range(FC):
                    for a in range(2):
                        split(w2f[:, c, a, :], S_W2, EH * D)
                bhi = tmp[0:2, 0:D // 2].bitcast(F16)
                step(nc.vector.tensor_copy(ones2[:, 0:B], sc[0:2, S_H:S_H + 1].broadcast_to((2, B))))
                step(nc.vector.tensor_scalar(bh32[:, :], bh32[:, :], sc[0:2, S_WHH:S_WHH + 1], None, ALU.mult))
                step(nc.vector.tensor_copy(bhi, bh32[:, :]))
                step(nc.vector.tensor_tensor(bh32[:, :], bh32[:, :], bhi, ALU.subtract))
                step(nc.vector.tensor_scalar(bh32[:, :], bh32[:, :], ident[0:2, 1:2], None, ALU.mult))
                step(nc.vector.scalar_tensor_tensor(out=bhp[:, :], in0=bhi, scalar=ident[0:2, 0:1],
                                                    in1=bh32[:, :], op0=ALU.mult, op1=ALU.add))
                step(nc.vector.tensor_scalar(h32[:, :, :], h32[:, :, :], sc[:, S_H:S_H + 1], None, ALU.mult))
                step(nc.vector.tensor_copy(hp[:, :, 0, :], h32[:, :, :]))
                step(nc.vector.tensor_tensor(hp[:, :, 1, :], h32[:, :, :], hp[:, :, 0, :], ALU.subtract))
                step(nc.vector.tensor_scalar(gw[:, :, :], gw[:, :, :], sc[:, S_GW:S_GW + 1], None, ALU.mult))
                step(nc.vector.tensor_copy(gwp[:, :, 0, :], gw[:, :, :]))
                step(nc.vector.tensor_tensor(gwp[:, :, 1, :], gw[:, :, :], gwp[:, :, 0, :], ALU.subtract))
                step(nc.vector.tensor_scalar(b1s[:, :, :], b1[:, :, :], sc[:, S_UN1I:S_UN1I + 1], None, ALU.mult))
                step(nc.vector.tensor_scalar(b2[:, :], b2[:, :], sc[0:NE, S_UN2I:S_UN2I + 1], None, ALU.mult))


def recurrence_and_ffn(nc, ins, out, ps, cst, ident, x1T, whf, w1f, w2f, gi, gi_d, h32, hp, gwp, b1, b1s, b2, gb,
                       bhp, ones2, sc, sb, sem):
    whp = whf[:, :, :].bitcast(F16).rearrange("p k (w q n) -> p k w q n", w=2, q=3)
    w1p = w1f[:, :, :, :].rearrange("p k a n -> p (k a) n").bitcast(F16)
    w2p = w2f[:, :, :, :].rearrange("p c a n -> p (c a) n").bitcast(F16)
    st = ExitStack()
    with st:
        s1 = sb(st, "s1", [P, 2, KD, B])
        rz = sb(st, "rz", [P, 2, KD, B])
        cn = sb(st, "cn", [P, KD, B])
        ab = sb(st, "ab", [P, KD, 2, B])
        hn = sb(st, "hn", [P, KD, B])
        nn = sb(st, "nn", [P, KD, B])
        ns = sb(st, "ns", [P, KD, B])
        dh = sb(st, "dh", [P, KD, B])
        nxt = sb(st, "nxt", [P, KD, 2, SPT, B], F16)
        cur = sb(st, "cur", [P, KD, 2, SPT, B], F16)
        scr = sb(st, "scr", [P, 2, NE])
        m1 = sb(st, "m1", [P, 2])
        m2 = sb(st, "m2", [P, 2])
        o1 = sb(st, "o1", [P, 2, NE])
        o2 = sb(st, "o2", [P, 2, NE])
        cd = sb(st, "cd", [P, 2, NE])
        cm = sb(st, "cm", [P, 2])
        dg = sb(st, "dgap", [P, 2])
        g1 = sb(st, "g1", [P, 2, 2])
        comb = sb(st, "comb", [P, 2, NE])
        combT = sb(st, "combT", [NE, TT])
        cb = sb(st, "cb", [P, 2, TT])
        sg = sb(st, "sg", [P, 2, TT])
        tb = sb(st, "tb", [P, TB, TT])
        hh = sb(st, "hh", [P, RING, 2, TT], F16)

        d_g = [sem(st, "d_g0"), sem(st, "d_g1")]
        p_r = sem(st, "p_r")
        p_n = sem(st, "p_n")
        p_z = sem(st, "p_z")
        v_sr = sem(st, "v_sr")
        a_r = sem(st, "a_r")
        v_sz = sem(st, "v_sz")
        a_z = sem(st, "a_z")
        v_ab = sem(st, "v_ab")
        v_d = sem(st, "v_d")
        a_t = sem(st, "a_t")
        v_h = sem(st, "v_h")
        a_ar = sem(st, "a_ar")
        v_cur = sem(st, "v_cur")
        p_sc = sem(st, "p_sc")
        v_rt = sem(st, "v_rt")
        a_g = sem(st, "a_g")
        p_ct = sem(st, "p_ct")
        v_ct = sem(st, "v_ct")
        p_bc = sem(st, "p_bc")
        a_cb = sem(st, "a_cb")
        p_up = sem(st, "p_up")
        a_sg = sem(st, "a_sg")
        v_t = sem(st, "v_t")
        v_u = sem(st, "v_u")
        a_h = sem(st, "a_h")
        g_l = sem(st, "g_l")
        p_dn = sem(st, "p_dn")
        v_y = sem(st, "v_y")
        d_o = sem(st, "d_o")

        def ready(eng, s, count):
            eng.wait_ge(s, count + 1)

        def start(eng, *sems):
            for s in sems:
                eng.nop().then_inc(s, 1)

        with nc.Block() as block:
            @block.sync
            def _(sp):
                def load(t, half):
                    s0 = half * (SPT // 2)
                    sp.dma_start(gi[:, :, s0:s0 + SPT // 2, :].rearrange("p q s b -> p q (s b)"),
                                 gi_d[:, :, bass.ds(t * SPT + s0, SPT // 2), :].rearrange("p q s b -> p q (s b)"))\
                        .then_inc(d_g[half], 16)

                def store(f):
                    ready(sp, v_y, (f + 1) * KD)
                    sp.dma_start(out[:, bass.ds(f * TT, TT)].rearrange("(k p) n -> p k n", p=P),
                                 x1T[:, :, bass.ds(f * SPT, SPT), :].rearrange("p k s b -> p k (s b)"))\
                        .then_inc(d_o, 16)

                def next_loads(t):
                    for half in range(2):
                        ready(sp, v_h, (t * SPT + (half + 1) * (SPT // 2)) * 4)
                        load(t + 1, half)

                for half in range(2):
                    load(0, half)
                next_loads(0)
                with sp.Fori(1, NT - 1) as t:
                    next_loads(t)
                    store(t - 1)
                store(NT - 2)
                store(NT - 1)
                sp.wait_ge(d_o, 16 * NT)

            @block.tensor
            def _(pe):
                def up(f, i):
                    e, c = i // FC, i % FC
                    ready(pe, v_t, f * NCH + max(i - 1, 0))
                    for k in range(KD):
                        w = w1p[:, k * 2 + e // EH, :].rearrange("p (w e h) -> p w e h", w=2, e=EH)
                        for n, (wp, hq) in enumerate(((0, 0), (0, 1), (1, 0))):
                            last = nc.tensor.matmul(ps[:, 6 + i % 2, 0:TT], w[:, wp, e % EH, c * P:(c + 1) * P],
                                                    cur[:, k, hq, :, :].rearrange("p s b -> p (s b)"),
                                                    start=(k == 0 and n == 0), stop=(k == KD - 1 and n == 2))
                    last.then_inc(p_up, 1)

                def second_biases(f, m):
                    if m == 0:
                        ready(pe, v_y, f * KD)
                    nc.tensor.matmul(ps[:, 4 + m // 2, (m % 2) * TT:(m % 2 + 1) * TT], b2[:, m * P:(m + 1) * P],
                                     combT[:, :], start=(m % 2 == 0), stop=False, skip_group_check=True)

                def down(f, i, half):
                    e, c = i // FC, i % FC
                    if half == 0:
                        ready(pe, a_h, f * NCH + i + 1)
                        ready(pe, g_l, f * NCH + i + 1)
                    w = w2p[:, c * 2 + e // EH, :].rearrange("p (w e d) -> p w e d", w=2, e=EH)
                    for m in range(2 * half, 2 * half + 2):
                        for n, (wp, hq) in enumerate(((0, 0), (0, 1), (1, 0))):
                            last = nc.tensor.matmul(ps[:, 4 + m // 2, (m % 2) * TT:(m % 2 + 1) * TT],
                                                    w[:, wp, e % EH, m * P:(m + 1) * P], hh[:, i % RING, hq, :],
                                                    start=False, stop=(i == NCH - 1 and n == 2),
                                                    skip_group_check=True)
                    if half:
                        last.then_inc(p_dn, 1)

                def ffn_slice(f, s):
                    if s == 0:
                        ready(pe, v_cur, f + 1)
                        ready(pe, a_cb, f * NE)
                        for g in range(2):
                            for k in range(KD):
                                for hq in range(2):
                                    last = nc.tensor.matmul(
                                        ps[:, 3, g * 2 * NE:(g + 1) * 2 * NE],
                                        cur[:, k, hq, g * P // B:(g + 1) * P // B, :].rearrange("p s b -> p (s b)"),
                                        gwp[:, k, :, :].rearrange("p a e -> p (a e)"),
                                        start=(k == 0 and hq == 0 and g == 0), stop=(k == KD - 1 and hq == 1),
                                        skip_group_check=True)
                        last.then_inc(p_sc, 1)
                    if s == 3:
                        ready(pe, v_rt, (f + 1) * R_STEPS)
                        for g in range(2):
                            last = nc.tensor.transpose(ps[0:NE, 3, g * P:(g + 1) * P], comb[:, g, :], ident)
                        last.then_inc(p_ct, 1)
                    if B2_AT <= s < B2_AT + KD:
                        second_biases(f, s - B2_AT)
                    for e in range(NE):
                        if BCAST_AT[e] == s:
                            if e == 0:
                                ready(pe, v_ct, f + 1)
                            ready(pe, a_cb, f * NE + e)
                            nc.tensor.matmul(ps[:, 3, 0:TT], ident[0:NE, e:e + 1].broadcast_to((NE, P)),
                                             combT[:, :], start=True, stop=True).then_inc(p_bc, 1)
                    for i in range(NCH):
                        if UP_AT[i] == s:
                            up(f, i)
                        for half in range(2):
                            if DOWN_AT[i][half] == s:
                                down(f, i, half)

                def products(bank, q):
                    for g in range(KD):
                        if q == 2:
                            nc.tensor.matmul(ps[:, bank, g * 2 * B:(g + 1) * 2 * B], bhp[:, g * P:(g + 1) * P],
                                             ones2[:, :], start=True, stop=False)
                        for k in range(KD):
                            for w in range(2):
                                last = nc.tensor.matmul(ps[:, bank, g * 2 * B:(g + 1) * 2 * B],
                                                        whp[:, k, w, q, g * P:(g + 1) * P],
                                                        hp[:, k, :, :].rearrange("p a b -> p (a b)"),
                                                        start=(k == 0 and w == 0 and q != 2),
                                                        stop=(k == KD - 1 and w == 1))
                    return last

                def step(n):
                    ready(pe, v_h, n * 4)
                    products(0, 0).then_inc(p_r, 1)
                    products(1, 2).then_inc(p_n, 1)
                    products(2, 1).then_inc(p_z, 1)

                def tile(t, recur, ffn):
                    for s in range(SPT):
                        if recur:
                            step(t * SPT + s)
                        if ffn:
                            ffn_slice(t - 1, s)

                start(pe, p_r, p_n, p_z, p_sc, p_ct, p_bc, p_up, p_dn)
                tile(0, True, False)
                with pe.Fori(1, NT) as t:
                    tile(t, True, True)
                tile(NT, False, True)

            @block.scalar
            def _(act):
                def step(n):
                    def unary(o, i_, func, done):
                        nc.scalar.activation(o.rearrange("p g b -> p (g b)"), i_.rearrange("p g b -> p (g b)"), func)\
                            .then_inc(done, 1)

                    ready(act, v_sr, (n + 1) * 2)
                    unary(rz[:, 0, :, :], s1[:, 0, :, :], ACT.Sigmoid, a_r)
                    ready(act, v_ab, (n + 1) * 3)
                    unary(nn[:, :, :], hn[:, :, :], ACT.Tanh, a_t)
                    ready(act, v_sz, (n + 1) * 2)
                    unary(rz[:, 1, :, :], s1[:, 1, :, :], ACT.Sigmoid, a_z)

                def keep(n, t, s):
                    ready(act, v_h, (n + 1) * 4)
                    if s == 0:
                        ready(act, v_cur, t)
                    nc.scalar.activation(nxt[:, :, :, s, :].rearrange("p k a b -> p (k a) b"),
                                         hp[:, :, :, :].rearrange("p k a b -> p (k a) b"), ACT.Copy)\
                        .then_inc(a_ar, 1)

                def ffn_slice(f, s):
                    if s == 2:
                        ready(act, v_rt, f * R_STEPS + 14)
                        nc.scalar.activation(g1[:, 0, :], dg[:, :], ACT.Sigmoid)
                        nc.scalar.activation(g1[:, 1, :], dg[:, :], ACT.Sigmoid, scale=-1.0).then_inc(a_g, 1)
                    for i in range(NCH):
                        e, c = i // FC, i % FC
                        if ACT_AT[i] == s:
                            ready(act, p_up, f * NCH + i + 1)
                            ready(act, v_t, f * NCH + max(i - 1, 0))
                            nc.scalar.activation(sg[:, i % 2, :], ps[:, 6 + i % 2, 0:TT], ACT.Sigmoid,
                                                 bias=b1[:, c, e:e + 1],
                                                 scale=sc[:, S_UN1:S_UN1 + 1]).then_inc(a_sg, 1)
                    for e in range(NE):
                        if BCAST_AT[e] + 1 == s:
                            ready(act, p_bc, f * NE + e + 1)
                            ready(act, v_u, f * NCH + max((e - 1) * FC, 0))
                            nc.scalar.activation(cb[:, e % 2, :], ps[:, 3, 0:TT], ACT.Copy,
                                                 scale=sc[:, S_CB:S_CB + 1]).then_inc(a_cb, 1)
                    for i in range(NCH):
                        if CAST_AT[i] == s:
                            ready(act, v_u, f * NCH + i + 1)
                            ready(act, p_dn, f * NCH + max(i - RING + 1, 0))
                            nc.scalar.activation(hh[:, i % RING, 0, :], tb[:, i % TB, :], ACT.Copy).then_inc(a_h, 1)

                def tile(t, recur, ffn):
                    for s in range(SPT):
                        if recur:
                            step(t * SPT + s)
                        if ffn:
                            ffn_slice(t - 1, s)
                        if recur:
                            keep(t * SPT + s, t, s)

                act.preload_act_table_set("sigmoid_and_others")
                start(act, a_r, a_z, a_t, a_ar, a_g, a_cb, a_sg, a_h)
                tile(0, True, False)
                with act.Fori(1, NT) as t:
                    tile(t, True, True)
                tile(NT, False, True)

            @block.gpsimd
            def _(pool):
                def ffn_slice(f, s):
                    for i in range(NCH):
                        if REST_AT[i] == s:
                            ready(pool, a_h, f * NCH + i + 1)
                            nc.gpsimd.tensor_tensor(hh[:, i % RING, 1, :], tb[:, i % TB, :], hh[:, i % RING, 0, :],
                                                    ALU.subtract).then_inc(g_l, 1)

                def tile(t):
                    for s in range(SPT):
                        ffn_slice(t - 1, s)

                start(pool, g_l)
                with pool.Fori(1, NT) as t:
                    tile(t)
                tile(NT)

            @block.vector
            def _(dve):
                def of_bank(bank):
                    return ps[:, bank, 0:KD * 2 * B].rearrange("p (g a b) -> p g a b", a=2, b=B)

                un_g = sc[:, S_UNG:S_UNG + 1]

                def add_scaled(o, products_, addend, done):
                    nc.vector.scalar_tensor_tensor(out=o, in0=products_, scalar=un_g, in1=addend,
                                                   op0=ALU.mult, op1=ALU.add).then_inc(done, 1)

                def step(n, s):
                    ready(dve, p_r, n + 1)
                    add_scaled(s1[:, 0, :, :], of_bank(0)[:, :, 0, :], gi[:, 0:KD, s, :], v_sr)
                    ready(dve, v_sr, n * 2 + 1)
                    add_scaled(s1[:, 0, :, :], of_bank(0)[:, :, 1, :], s1[:, 0, :, :], v_sr)
                    ready(dve, a_r, n + 1)
                    ready(dve, p_n, n + 1)
                    nc.vector.tensor_tensor(ab[:, :, :, :], of_bank(1),
                                            rz[:, 0, :, :].unsqueeze(2).broadcast_to((P, KD, 2, B)), ALU.mult)\
                        .then_inc(v_ab, 1)
                    ready(dve, v_ab, n * 3 + 1)
                    add_scaled(hn[:, :, :], ab[:, :, 0, :], gi[:, 2 * KD:NQ, s, :], v_ab)
                    ready(dve, v_ab, n * 3 + 2)
                    add_scaled(hn[:, :, :], ab[:, :, 1, :], hn[:, :, :], v_ab)
                    ready(dve, p_z, n + 1)
                    add_scaled(s1[:, 1, :, :], of_bank(2)[:, :, 0, :], gi[:, KD:2 * KD, s, :], v_sz)
                    ready(dve, v_sz, n * 2 + 1)
                    add_scaled(s1[:, 1, :, :], of_bank(2)[:, :, 1, :], s1[:, 1, :, :], v_sz)
                    ready(dve, a_t, n + 1)
                    nc.vector.scalar_tensor_tensor(out=dh[:, :, :], in0=nn[:, :, :], scalar=sc[:, S_H:S_H + 1],
                                                   in1=h32[:, :, :], op0=ALU.mult, op1=ALU.subtract).then_inc(v_d, 1)
                    nc.vector.tensor_scalar(ns[:, :, :], nn[:, :, :], sc[:, S_H:S_H + 1], None, ALU.mult)\
                        .then_inc(v_d, 1)
                    ready(dve, v_d, n * 2 + 1)
                    ready(dve, a_z, n + 1)
                    nc.vector.tensor_tensor(dh[:, :, :], rz[:, 1, :, :], dh[:, :, :], ALU.mult).then_inc(v_h, 1)
                    ready(dve, v_d, n * 2 + 2)
                    ready(dve, a_ar, n)
                    ready(dve, v_h, n * 4 + 1)
                    nc.vector.tensor_tensor(hp[:, :, 0, :], ns[:, :, :], dh[:, :, :], ALU.subtract).then_inc(v_h, 1)
                    nc.vector.tensor_tensor(h32[:, :, :], ns[:, :, :], dh[:, :, :], ALU.subtract).then_inc(v_h, 1)
                    ready(dve, v_h, n * 4 + 3)
                    nc.vector.tensor_tensor(hp[:, :, 1, :], h32[:, :, :], hp[:, :, 0, :], ALU.subtract)\
                        .then_inc(v_h, 1)

                bc = lambda x: x.unsqueeze(2).broadcast_to((P, 2, NE))
                desc = cst[:, C_DESC8:C_DESC8 + NE].unsqueeze(1).broadcast_to((P, 2, NE))

                def choose(f, s):
                    c = [{0: 0, 1: 7, 2: 14}[s]]

                    def link(i_):
                        c[0] += 1
                        i_.then_inc(v_rt, 1)
                        ready(dve, v_rt, f * R_STEPS + c[0])

                    sp = ps[:, 3, 0:4 * NE].rearrange("p (g a e) -> p g a e", g=2, a=2)
                    un = sc[:, S_UNR:S_UNR + 1]
                    tt = nc.vector.tensor_tensor
                    if s == 0:
                        ready(dve, p_sc, f + 1)
                        link(nc.vector.scalar_tensor_tensor(out=scr[:, :, :], in0=sp[:, :, 0, :], scalar=un,
                                                            in1=gb[:, :].unsqueeze(1).broadcast_to((P, 2, NE)),
                                                            op0=ALU.mult, op1=ALU.add))
                        link(nc.vector.scalar_tensor_tensor(out=scr[:, :, :], in0=sp[:, :, 1, :], scalar=un,
                                                            in1=scr[:, :, :], op0=ALU.mult, op1=ALU.add))
                        link(nc.vector.tensor_reduce(m1[:, :], scr[:, :, :], AX.X, ALU.max))
                        link(tt(o1[:, :, :], scr[:, :, :], bc(m1[:, :]), ALU.is_equal))
                        link(tt(cd[:, :, :], o1[:, :, :], desc, ALU.mult))
                        link(nc.vector.tensor_reduce(cm[:, :], cd[:, :, :], AX.X, ALU.max))
                        link(tt(o1[:, :, :], cd[:, :, :], bc(cm[:, :]), ALU.is_equal))
                    if s == 1:
                        link(nc.vector.scalar_tensor_tensor(out=scr[:, :, :], in0=o1[:, :, :], scalar=-3e38,
                                                            in1=scr[:, :, :], op0=ALU.mult, op1=ALU.add))
                        link(nc.vector.tensor_reduce(m2[:, :], scr[:, :, :], AX.X, ALU.max))
                        link(tt(o2[:, :, :], scr[:, :, :], bc(m2[:, :]), ALU.is_equal))
                        link(tt(cd[:, :, :], o2[:, :, :], desc, ALU.mult))
                        link(nc.vector.tensor_reduce(cm[:, :], cd[:, :, :], AX.X, ALU.max))
                        link(tt(o2[:, :, :], cd[:, :, :], bc(cm[:, :]), ALU.is_equal))
                        link(tt(dg[:, :], m1[:, :], m2[:, :], ALU.subtract))
                    if s == 2:
                        ready(dve, a_g, f + 1)
                        link(tt(o1[:, :, :], o1[:, :, :], bc(g1[:, 0, :]), ALU.mult))
                        link(tt(o2[:, :, :], o2[:, :, :], bc(g1[:, 1, :]), ALU.mult))
                        link(tt(comb[:, :, :], o1[:, :, :], o2[:, :, :], ALU.add))

                def ffn_slice(f, s):
                    if s < 3:
                        choose(f, s)
                    if s == 3:
                        ready(dve, p_ct, f + 1)
                        nc.vector.tensor_copy(combT[:, :], ps[0:NE, 3, 0:TT]).then_inc(v_ct, 1)
                    for i in range(NCH):
                        e, c = i // FC, i % FC
                        if GATE_AT[i] == s:
                            ready(dve, a_cb, f * NE + e + 1)
                            ready(dve, v_t, f * NCH + i + 1)
                            nc.vector.tensor_tensor(tb[:, i % TB, :], tb[:, i % TB, :], cb[:, e % 2, :], ALU.mult)\
                                .then_inc(v_u, 1)
                    for i in range(NCH):
                        e, c = i // FC, i % FC
                        if ACT_AT[i] == s:
                            ready(dve, a_sg, f * NCH + i + 1)
                            ready(dve, g_l, f * NCH + max(i - TB + 1, 0))
                            nc.vector.scalar_tensor_tensor(out=tb[:, i % TB, :], in0=ps[:, 6 + i % 2, 0:TT],
                                                           scalar=b1s[:, c, e:e + 1], in1=sg[:, i % 2, :],
                                                           op0=ALU.add, op1=ALU.mult).then_inc(v_t, 1)
                    if s >= SPT - 2:
                        if s == SPT - 2:
                            ready(dve, p_dn, (f + 1) * NCH)
                        for m in range(2 * (s - SPT + 2), 2 * (s - SPT + 2) + 2):
                            xr = x1T[:, m, bass.ds(f * SPT, SPT), :].rearrange("p s b -> p (s b)")
                            nc.vector.scalar_tensor_tensor(out=xr, in0=ps[:, 4 + m // 2, (m % 2) * TT:(m % 2 + 1) * TT],
                                                           scalar=sc[:, S_UN2:S_UN2 + 1], in1=xr,
                                                           op0=ALU.mult, op1=ALU.add).then_inc(v_y, 1)

                def tile(t, recur, ffn):
                    for s in range(SPT):
                        if recur:
                            if s % (SPT // 2) == 0:
                                dve.wait_ge(d_g[s // (SPT // 2)], t * 16 + 16)
                            step(t * SPT + s, s)
                        if ffn:
                            ffn_slice(t - 1, s)
                    if recur:
                        ready(dve, a_ar, t * SPT + SPT)
                        if ffn:
                            ready(dve, p_up, t * NCH)
                        nc.vector.tensor_copy(cur[:, :, :, :, :].rearrange("p k a s b -> p (k a s b)"),
                                              nxt[:, :, :, :, :].rearrange("p k a s b -> p (k a s b)"))\
                            .then_inc(v_cur, 1)

                start(dve, v_sr, v_sz, v_ab, v_d, v_h, v_cur, v_rt, v_ct, v_t, v_u, v_y)
                tile(0, True, False)
                with dve.Fori(1, NT) as t:
                    tile(t, True, True)
                tile(NT, False, True)


def constants():
    import numpy as np

    i = np.arange(P)
    own = np.concatenate([np.eye(P, dtype=np.float32),
                          np.broadcast_to(np.arange(NE, 0, -1, dtype=np.float32), (P, NE))], axis=1)
    c = np.zeros((P, T_ALL), np.float32)
    half = DH2 // 2
    partner = np.where(i % DH2 < half, i + half, i - half)
    c[partner, C_ROT + i] = 1.0
    c[:, C_CAUS:C_CAUS + P] = np.where(i[None, :] <= i[:, None], 0.0, NEG)
    c[:, C_NB0:C_NB0 + P] = np.where(np.abs(i[None, :] - i[:, None]) <= RECENT, 0.0, NEG)
    c[:, C_NB1:C_NB1 + P] = np.where(np.abs(i[None, :] + P - i[:, None]) <= RECENT, 0.0, NEG)
    inv = (np.float32(1.0) / np.float32(10000.0) ** (np.arange(0, DH2, 2, dtype=np.float32) / np.float32(DH2)))
    ang = np.arange(S, dtype=np.float32)[None, :] * inv.astype(np.float32)[i % half][:, None]
    sign = np.where(i % DH2 < half, -1.0, 1.0)[:, None]
    cos, sin = np.cos(ang), np.sin(ang) * sign
    c[:, C_COSQ:C_COSQ + S] = cos * DH2 ** -0.5
    c[:, C_SINQ:C_SINQ + S] = sin * DH2 ** -0.5
    c[:, C_COSK:C_COSK + S] = cos
    c[:, C_SINK:C_SINK + S] = sin
    for q in range(HPC):
        c[q * DH2:(q + 1) * DH2, C_HEAD + q] = 1.0
    c[:, C_DESC:C_DESC + S] = np.arange(S, 0, -1)
    return own, c


def kernel(x, cond_2048, L0_cond_Wq, L0_cond_Wk, L0_cond_Wv, L0_cond_b, L0_attn_Wq, L0_attn_Wk, L0_attn_Wv,
           L0_attn_Wo, L0_cond2_W_ih, L0_cond2_W_hh, L0_cond2_b_ih, L0_cond2_b_hh, L0_ffn_gate_w, L0_ffn_gate_b,
           L0_ffn_bias, L0_ffn_w1, L0_ffn_b1, L0_ffn_w2, L0_ffn_b2):
    import numpy as np
    import concourse.bacc as bacc
    from concourse.bass_utils import run_bass_kernel_spmd

    n = np.asarray
    heads = [n(w).reshape(NH, DH1, KS, P).transpose(0, 3, 2, 1) for w in (L0_cond_Wq, L0_cond_Wk, L0_cond_Wv)]
    own, table = constants()
    arrays = {
        "consts": own,
        "table": table,
        "x": n(x),
        "xT": n(x).transpose(2, 1, 0).reshape(D, S * B),
        "cond": n(cond_2048),
        "condT": n(cond_2048).T,
        "cond_b": np.broadcast_to(n(L0_cond_b).reshape(1, 1), (B, 1)),
        "cond_WvT": n(L0_cond_Wv).T,
        "cond_Wh": np.stack(heads, axis=3),
        "attn_WqT": n(L0_attn_Wq).T,
        "attn_WkT": n(L0_attn_Wk).T,
        "attn_WvT": n(L0_attn_Wv).T,
        "attn_WoT": n(L0_attn_Wo).T,
        "W_ih": n(L0_cond2_W_ih),
        "W_hh": n(L0_cond2_W_hh),
        "b_ih": n(L0_cond2_b_ih).reshape(NQ, P).T,
        "b_hh": n(L0_cond2_b_hh).reshape(NQ, P).T,
        "b_hh_n": n(L0_cond2_b_hh)[2 * D:].reshape(1, D),
        "gate_wT": n(L0_ffn_gate_w).T,
        "gate_b": n(L0_ffn_gate_b).reshape(1, NE),
        "bias": n(L0_ffn_bias).reshape(1, NE),
        "w1T": n(L0_ffn_w1).transpose(2, 0, 1).reshape(D, NE * HF),
        "b1T": n(L0_ffn_b1).T,
        "w2T": n(L0_ffn_w2).transpose(2, 0, 1),
        "b2": n(L0_ffn_b2),
    }
    arrays = {k: np.ascontiguousarray(v) for k, v in arrays.items()}
    nc = bacc.Bacc("TRN2", target_bir_lowering=False, num_devices=1)
    ins = {k: nc.dram_tensor(f"in_{k}", v.shape, mybir.dt.from_np(v.dtype), kind="ExternalInput").ap()
           for k, v in arrays.items()}
    out = nc.dram_tensor("out_0", (D, S * B), F32, kind="ExternalOutput").ap()
    program(nc, ins, out)
    r = run_bass_kernel_spmd(nc, [{f"in_{k}": v for k, v in arrays.items()}], core_ids=[0])
    got = r.results[0]["out_0"]
    return np.ascontiguousarray(got.reshape(D, S, B).transpose(2, 1, 0))
```

```python
from contextlib import ExitStack

import concourse.bass as bass
from concourse import mybir

F32 = mybir.dt.float32
F16 = mybir.dt.float16
BF16 = mybir.dt.bfloat16
I32 = mybir.dt.int32
ALU = mybir.AluOpType
ACT = mybir.ActivationFunctionType
AX = mybir.AxisListType

P = 128
B, S, D = 8, 256, 512
KD = D // P
KS = S // P
NH = 16
DH1 = S // NH
DH2 = D // NH
HPC = P // DH2
NEG = -1e30
HEAVY = int(0.1 * S)
RECENT = int(0.1 * S)
G3 = 3 * D
NQ = G3 // P
NE, HF = 8, 352
TOK = B * S
FC = (HF + P - 1) // P
HL = HF - (FC - 1) * P
SPT = 32
TT = SPT * B
NT = S // SPT
HFP = FC * P
EH = NE // 2

C_ID = 0
C_DESC8 = C_ID + P
C_ALL = C_DESC8 + NE
C_ROT = 0
C_CAUS = C_ROT + P
C_NB0 = C_CAUS + P
C_NB1 = C_NB0 + P
C_COSQ = C_NB1 + P
C_SINQ = C_COSQ + S
C_COSK = C_SINQ + S
C_SINK = C_COSK + S
C_HEAD = C_SINK + S
C_DESC = C_HEAD + HPC
T_ALL = C_DESC + S


def program(nc, ins, out):
    ctx = ExitStack()
    with ctx:
        def sb(stack, name, shape, dt=F32):
            return stack.enter_context(nc.sbuf_tensor(name, shape, dt))

        def sem(stack, name):
            return stack.enter_context(nc.semaphore(name))

        ps = ctx.enter_context(nc.psum_tensor("ps", [P, 8, 512], F32))
        cst = sb(ctx, "cst", [P, C_ALL])
        x1T = sb(ctx, "x1T", [P, KD, S, B])
        ident = cst[:, C_ID:C_ID + P]

        att = ExitStack()
        with att:
            hT = sb(att, "hT", [P, KD, B, S])
            tab = sb(att, "tab", [P, T_ALL])
            weights = [sb(att, name, [P, KD, D]) for name in ("wq", "wk", "wv2", "wo")]
            d_w = sem(att, "e_w")
            d_tab = sem(att, "e_tab")
            d_xT = sem(att, "d_xT")
            first_attention_uniform_and_general(nc, ins, ps, cst, ident, x1T, hT, tab, weights, d_w, d_tab, d_xT,
                                                sb, sem)
            second_attention(nc, ps, cst, ident, x1T, hT, tab, weights, d_w, d_tab, d_xT, sb, sem)
        gru_and_ffn(nc, ins, out, ps, cst, ident, x1T, sb, sem)


def first_attention_uniform_and_general(nc, ins, ps, cst, ident, x1T, hT, tab, weights, d_w, d_tab, d_xT, sb, sem):
    st = ExitStack()
    with st:
        xall = sb(st, "xall", [P, KS, B, D])
        wv = sb(st, "wv", [P, KS, S])
        mask = sb(st, "mask", [B, D])
        b0 = sb(st, "b0", [B, 1])
        pen = sb(st, "pen", [B, D])
        top = sb(st, "top", [B, 1])
        zf = sb(st, "zf", [B, 1])
        wm = sb(st, "wm", [B, D])
        cnt = sb(st, "cnt", [B, 1])
        rcnt = sb(st, "rcnt", [B, 1])
        bz = sb(st, "bz", [B, 1])
        bias = sb(st, "bias", [B, D])
        ksc = sb(st, "ksc", [B, D])
        xw = sb(st, "xw", [P, KS, B])
        junk = sb(st, "junk", [P, D])
        ones = sb(st, "ones", [P, P])
        xwb = sb(st, "xwb", [P, KS, B, P])
        flag = sb(st, "flag", [1, 1], I32)
        scr_bias = nc.dram_tensor("scr_bias", [B, D], F32).ap()
        scr_ksc = nc.dram_tensor("scr_ksc", [B, D], F32).ap()

        d_mask = sem(st, "d_mask")
        d_cst = sem(st, "d_cst")
        d_x = sem(st, "d_x")
        d_wv = sem(st, "d_wv")
        d_scr = sem(st, "d_scr")
        v_step = sem(st, "v_step")
        v_ones = sem(st, "v_ones")
        v_w = sem(st, "v_w")
        v_rows = sem(st, "v_rows")
        p_w = sem(st, "p_w")
        v_xw = sem(st, "v_xw")
        v_xwb = sem(st, "v_xwb")
        p_y = sem(st, "p_y")
        a_hT = sem(st, "a_hT")
        p_flag = sem(st, "p_flag")

        with nc.Block() as block:
            @block.sync
            def _(sp):
                sp.dma_start(mask[:, :], ins["cond"]).then_inc(d_mask, 16)
                sp.dma_start(b0[:, :], ins["cond_b"]).then_inc(d_mask, 16)
                sp.dma_start(cst[:, :], ins["consts"]).then_inc(d_cst, 16)
                for k in range(KS):
                    for b in range(0, B, 4):
                        sp.dma_start(xall[:, k, b:b + 4, :],
                                     ins["x"][b:b + 4, k * P:(k + 1) * P, :].rearrange("b p t -> p b t"))\
                            .then_inc(d_x, 16)
                sp.dma_start(wv[:, :, :], ins["cond_WvT"].rearrange("(k p) o -> p k o", p=P)).then_inc(d_wv, 16)
                sp.wait_ge(v_rows, 2)
                sp.dma_start(scr_bias, bias[:, :]).then_inc(d_scr, 16)
                sp.dma_start(scr_ksc, ksc[:, :]).then_inc(d_scr, 16)
                sp.dma_start(tab[:, :], ins["table"]).then_inc(d_tab, 16)
                for t, name in zip(weights, ("attn_WqT", "attn_WkT", "attn_WvT", "attn_WoT")):
                    sp.dma_start(t[:, :, :], ins[name].rearrange("(k p) o -> p k o", p=P)).then_inc(d_w, 16)
                sp.dma_start(x1T[:, :, :, :].rearrange("p k s b -> p k (s b)"),
                             ins["xT"].rearrange("(k p) n -> p k n", p=P)).then_inc(d_xT, 16)
                sp.wait_ge(d_scr, 32)

            @block.vector
            def _(dve):
                n = [0]

                def step(ins_):
                    n[0] += 1
                    ins_.then_inc(v_step, 1)
                    dve.wait_ge(v_step, n[0])

                nc.vector.memset(ones[:, :], 1.0).then_inc(v_ones, 1)
                dve.wait_ge(d_mask, 32)
                step(nc.vector.tensor_scalar(pen[:, :], mask[:, :], -1.0, 1.0, ALU.mult, ALU.add))
                step(nc.vector.tensor_scalar(pen[:, :], pen[:, :], NEG, None, ALU.mult))
                step(nc.vector.tensor_reduce(top[:, :], pen[:, :], AX.X, ALU.max))
                step(nc.vector.tensor_scalar(wm[:, :], pen[:, :], top[:, 0:1], None, ALU.is_equal))
                step(nc.vector.tensor_reduce(cnt[:, :], wm[:, :], AX.X, ALU.add))
                step(nc.vector.reciprocal(rcnt[:, :], cnt[:, :]))
                nc.vector.tensor_scalar(wm[:, :], wm[:, :], rcnt[:, 0:1], None, ALU.mult).then_inc(v_w, 1)
                step(nc.vector.tensor_scalar(zf[:, :], top[:, :], 0.0, None, ALU.is_equal))
                step(nc.vector.tensor_tensor(bz[:, :], b0[:, :], zf[:, :], ALU.mult))
                step(nc.vector.tensor_scalar(pen[:, :], pen[:, :], top[:, 0:1], None, ALU.subtract))
                nc.vector.scalar_tensor_tensor(out=bias[:, :], in0=mask[:, :], scalar=bz[:, 0:1],
                                               in1=pen[:, :], op0=ALU.mult, op1=ALU.add).then_inc(v_rows, 1)
                nc.vector.tensor_scalar(ksc[:, :], mask[:, :], zf[:, 0:1], DH1 ** -0.5, ALU.mult, ALU.mult)\
                    .then_inc(v_rows, 1)
                dve.wait_ge(d_x, 16 * 2 * KS)
                for b in range(B):
                    dve.wait_ge(p_w, b + 1)
                    for k in range(KS):
                        step(nc.vector.tensor_tensor_reduce(junk[:, :], xall[:, k, b, :], ps[:, b, :], 1.0, 0.0,
                                                            ALU.mult, ALU.add, xw[:, k, b:b + 1]))
                for b in range(B):
                    for k in range(KS):
                        nc.vector.tensor_scalar(xwb[:, k, b, :], ones[:, :], xw[:, k, b:b + 1], None, ALU.mult)\
                            .then_inc(v_xwb, 1)
                dve.wait_ge(p_flag, 1)
                nc.vector.tensor_copy(flag[:, :], ps[0:1, 7, 0:1]).then_inc(v_step, 1)
                dve.wait_ge(v_step, n[0] + 1)

            @block.tensor
            def _(pe):
                pe.wait_ge(v_w, 1)
                pe.wait_ge(d_cst, 16)
                for b in range(B):
                    nc.tensor.matmul(ps[:, b, :], ident[0:B, b:b + 1].broadcast_to((B, P)), wm[:, :],
                                     start=True, stop=True).then_inc(p_w, 1)
                pe.wait_ge(d_wv, 16)
                pe.wait_ge(v_xwb, B * KS)
                for b in range(B):
                    bank = b % 4
                    if b >= 4:
                        pe.wait_ge(a_hT, KD * (b - 3))
                    for k in range(KS):
                        last = nc.tensor.matmul(ps[:, bank, 0:S], xwb[:, k, b, :], wv[:, k, :],
                                                start=(k == 0), stop=(k == KS - 1))
                    last.then_inc(p_y, 1)
                nc.tensor.matmul(ps[0:1, 7, 0:1], zf[:, :], ones[0:B, 0:1], start=True, stop=True)\
                    .then_inc(p_flag, 1)

            @block.scalar
            def _(act):
                for b in range(B):
                    act.wait_ge(p_y, b + 1)
                    for t in range(KD):
                        nc.scalar.activation(hT[:, t, b, :], ps[:, b % 4, 0:S], ACT.Copy).then_inc(a_hT, 1)
                act.wait_ge(a_hT, B * KD)

        general = ExitStack()
        with general:
            wh = sb(general, "g_wh", [P, KS, 3, DH1])
            gbias = sb(general, "g_bias", [1, D])
            gks = sb(general, "g_ks", [DH1, D])
            qh = sb(general, "g_q", [DH1, D])
            kh = sb(general, "g_k", [DH1, D])
            vh = sb(general, "g_v", [DH1, D])
            vT = sb(general, "g_vT", [P, KD, DH1])
            nmax = sb(general, "g_nmax", [P, KD])
            lsum = sb(general, "g_lsum", [P, KD])
            rl = sb(general, "g_rl", [P, KD])
            e = sb(general, "g_e", [P, D])
            eT = sb(general, "g_eT", [P, KD, P])
            g_in = sem(general, "g_in")
            g_proj = sem(general, "g_proj")
            g_qkv = sem(general, "g_qkv")
            g_vt = sem(general, "g_vt")
            g_vs = sem(general, "g_vs")
            g_s = sem(general, "g_s")
            g_m = sem(general, "g_m")
            g_e = sem(general, "g_e")
            g_t = sem(general, "g_t")
            g_ts = sem(general, "g_ts")
            g_o = sem(general, "g_o")
            g_r = sem(general, "g_r")
            g_done = sem(general, "g_done")

            with nc.Block() as block:
                @block.sync
                def _(sp):
                    go = sp.value_load(flag[0:1, 0:1], min_val=0, max_val=B)
                    with sp.If(go > 0):
                        with sp.Fori(0, B) as b:
                            with sp.Fori(0, NH) as h:
                                n = b * NH + h
                                sp.wait_ge(g_done, n * KD + 1)
                                sp.dma_start(wh[:, :, :, :],
                                             ins["cond_Wh"][bass.ds(h, 1)].rearrange("a p k w d -> p (a k) w d"))\
                                    .then_inc(g_in, 16)
                                sp.dma_start(gbias[:, :], scr_bias[bass.ds(b, 1), :]).then_inc(g_in, 16)
                                sp.dma_start(gks[:, :], scr_ksc[bass.ds(b, 1), :].broadcast_to((DH1, D)))\
                                    .then_inc(g_in, 16)

                @block.tensor
                def _(pe):
                    go = pe.value_load(flag[0:1, 0:1], min_val=0, max_val=B)
                    with pe.If(go > 0):
                        with pe.Fori(0, B) as b:
                            with pe.Fori(0, NH) as h:
                                n = b * NH + h
                                pe.wait_ge(g_in, (n + 1) * 48)
                                for w in range(3):
                                    for k in range(KS):
                                        last = nc.tensor.matmul(
                                            ps[0:DH1, w, :], wh[:, k, w, :],
                                            xall[:, k, bass.ds(b, 1), :].rearrange("p a t -> p (a t)"),
                                            start=(k == 0), stop=(k == KS - 1))
                                last.then_inc(g_proj, 1)
                                pe.wait_ge(g_qkv, (n + 1) * 3)
                                for t in range(KD):
                                    last = nc.tensor.matmul(ps[:, 3, t * DH1:(t + 1) * DH1],
                                                            vh[:, t * P:(t + 1) * P], ident[0:DH1, 0:DH1],
                                                            start=True, stop=True)
                                last.then_inc(g_vt, 1)
                                for q in range(KD):
                                    nq = n * KD + q
                                    pe.wait_ge(g_e, nq + 1)
                                    nc.tensor.matmul(ps[:, 4, :], qh[:, q * P:(q + 1) * P], kh[:, :],
                                                     start=True, stop=False)
                                    nc.tensor.matmul(ps[:, 4, :], ones[0:1, :], gbias[:, :],
                                                     start=False, stop=True).then_inc(g_s, 1)
                                    pe.wait_ge(g_e, nq + 2)
                                    for t in range(KD):
                                        last = nc.tensor.transpose(ps[:, 5, t * P:(t + 1) * P],
                                                                   e[:, t * P:(t + 1) * P], ident)
                                    last.then_inc(g_t, 1)
                                    pe.wait_ge(g_ts, nq + 1)
                                    pe.wait_ge(g_vs, n + 1)
                                    for t in range(KD):
                                        last = nc.tensor.matmul(ps[:, 6, 0:DH1], eT[:, t, :], vT[:, t, :],
                                                                start=(t == 0), stop=(t == KD - 1))
                                    last.then_inc(g_o, 1)
                                pe.wait_ge(g_done, (n + 1) * KD + 1)

                @block.vector
                def _(dve):
                    go = dve.value_load(flag[0:1, 0:1], min_val=0, max_val=B)
                    with dve.If(go > 0):
                        dve.nop().then_inc(g_done, 1)
                        with dve.Fori(0, B) as b:
                            with dve.Fori(0, NH) as h:
                                n = b * NH + h
                                dve.wait_ge(g_proj, n + 1)
                                nc.vector.tensor_copy(qh[:, :], ps[0:DH1, 0, :]).then_inc(g_qkv, 1)
                                nc.vector.tensor_tensor(kh[:, :], ps[0:DH1, 1, :], gks[:, :], ALU.mult)\
                                    .then_inc(g_qkv, 1)
                                nc.vector.tensor_copy(vh[:, :], ps[0:DH1, 2, :]).then_inc(g_qkv, 1)
                                dve.wait_ge(g_vt, n + 1)
                                nc.vector.tensor_copy(vT[:, :, :].rearrange("p t d -> p (t d)"),
                                                      ps[:, 3, 0:KD * DH1]).then_inc(g_vs, 1)
                                for q in range(KD):
                                    nq = n * KD + q
                                    dve.wait_ge(g_s, nq + 1)
                                    nc.vector.tensor_reduce(nmax[:, q:q + 1], ps[:, 4, :], AX.X, ALU.max,
                                                            negate=True).then_inc(g_m, 1)
                                    dve.wait_ge(g_t, nq + 1)
                                    nc.vector.tensor_copy(eT[:, :, :].rearrange("p t d -> p (t d)"), ps[:, 5, :])\
                                        .then_inc(g_ts, 1)
                                    dve.wait_ge(g_e, nq + 2)
                                    nc.vector.reciprocal(rl[:, q:q + 1], lsum[:, q:q + 1]).then_inc(g_r, 1)
                                    dve.wait_ge(g_r, nq + 1)
                                    dve.wait_ge(g_o, nq + 1)
                                    nc.vector.tensor_scalar(
                                        hT[:, q, bass.ds(b, 1), bass.ds(h * DH1, DH1)].rearrange("p a d -> p (a d)"),
                                        ps[:, 6, 0:DH1], rl[:, q:q + 1], None, ALU.mult).then_inc(g_done, 1)

                @block.scalar
                def _(act):
                    go = act.value_load(flag[0:1, 0:1], min_val=0, max_val=B)
                    with act.If(go > 0):
                        act.nop().then_inc(g_e, 1)
                        with act.Fori(0, B) as b:
                            with act.Fori(0, NH) as h:
                                n = b * NH + h
                                for q in range(KD):
                                    nq = n * KD + q
                                    act.wait_ge(g_m, nq + 1)
                                    nc.scalar.activation(e[:, :], ps[:, 4, :], ACT.Exp, bias=nmax[:, q:q + 1],
                                                         accum_out=lsum[:, q:q + 1]).then_inc(g_e, 1)


def second_attention(nc, ps, cst, ident, x1T, hT, tab, weights, d_w, d_tab, d_xT, sb, sem):
    st = ExitStack()
    with st:
        wq, wk, wv, wo = weights
        masks = sb(st, "masks", [P, 4, P], BF16)
        hb = sb(st, "hb", [P, KD, S])
        raw = sb(st, "raw", [P, 2, KD, S])
        rot = sb(st, "rot", [P, 2, KD, S])
        kz = sb(st, "kz", [P, HPC, KD, S])
        v = sb(st, "v", [P, KS, D])
        tmp = sb(st, "tmp", [P, KD, S])
        E = sb(st, "E", [P, NEX, P + S])
        En = sb(st, "En", [P, NEN, P + S])
        ET = sb(st, "ET", [P, HPC, P + S])
        nm = sb(st, "nm", [P, 2, NH, 2])
        ls = sb(st, "ls", [P, 2, NH, 2])
        rl = sb(st, "rl", [P, 2, NH, 2])
        rdiag = sb(st, "rdiag", [P, NH, 2, CG])
        tsum = sb(st, "tsum", [P, S])
        work = sb(st, "work", [P, S])
        top8 = sb(st, "top8", [P, 8])
        code = sb(st, "code", [P, S])
        cmax = sb(st, "cmax", [P, 1])
        light = sb(st, "light", [P, S])
        lcol = sb(st, "lcol", [P, KS, P])
        dg = sb(st, "dg", [P, NDG, KS, P], BF16)
        oT = sb(st, "oT", [P, KD, S])

        v_init = sem(st, "e_init")
        c_hb = sem(st, "c_hb")
        p_qk = sem(st, "p_qk")
        a_raw = sem(st, "a_raw")
        p_rot = sem(st, "p_rot")
        v_rot = sem(st, "v_rot")
        a_kz = sem(st, "a_kz")
        v_kz = sem(st, "v_kz")
        p_v = sem(st, "p_v")
        a_v = sem(st, "a_v")
        p_s = sem(st, "p_s")
        v_m = sem(st, "v_m")
        a_e = sem(st, "a_e")
        v_r = sem(st, "v_r")
        v_d = sem(st, "v_d")
        p_c = sem(st, "p_c")
        v_k = sem(st, "v_k")
        p_l = sem(st, "p_l")
        v_l = sem(st, "v_l")
        g_d = sem(st, "g_d")
        v_n = sem(st, "v_n")
        p_t = sem(st, "p_t")
        a_t = sem(st, "a_t")
        p_av = sem(st, "p_av")
        a_o = sem(st, "a_o")
        p_o = sem(st, "p_o")
        v_x = sem(st, "v_x")

        with nc.Block() as block:
            @block.gpsimd
            def _(pool):
                def diagonals(b):
                    pool.wait_ge(v_l, b + 1)
                    for h in range(NH):
                        if h >= NDG:
                            pool.wait_ge(p_s, b * 2 * NH + NH + h - NDG + 2)
                        nc.gpsimd.tensor_tensor(dg[:, h % NDG, :, :],
                                                masks[:, 0, :].unsqueeze(1).broadcast_to((P, KS, P)),
                                                lcol[:, :, row_of(h):row_of(h) + 1].broadcast_to((P, KS, P)), ALU.mult)\
                            .then_inc(g_d, 1)

                with pool.Fori(0, B) as b:
                    pool.wait_ge(p_v, b + 1)
                    nc.gpsimd.tensor_copy(hb[:, :, :], hT[:, :, bass.ds(b, 1), :].rearrange("p k a s -> p k (a s)"))\
                        .then_inc(c_hb, 1)
                    diagonals(b)

            @block.tensor
            def _(pe):
                pe.nop().then_inc(p_v, 1)
                pe.nop().then_inc(p_s, 1)
                pe.wait_ge(d_w, 64)
                pe.wait_ge(d_tab, 16)
                pe.wait_ge(v_init, 3)

                def scores(b, r, h, more=False):
                    n = b * (2 * NH) + r * NH + h
                    bank = h % 4
                    m, q = h // HPC, h % HPC
                    if r == 0 and h < 4:
                        if h == 0:
                            pe.wait_ge(v_x, b * KD + 1)
                    else:
                        pe.wait_ge(a_e, (n - 4 + 1) * 2)
                    if r == 0 and h == 0:
                        pe.wait_ge(v_rot, b * 6 + 6)
                    if r == 0 and h < 2:
                        pe.wait_ge(a_kz, b * 2 + h + 2)
                    elif r == 0 and h < HPC:
                        pe.wait_ge(v_kz, b * 2 + h - 1)
                    if r == 1 and h == 0 and more:
                        pe.wait_ge(a_raw, b * 2 + 4)
                    kw = dict(stop=False, skip_group_check=True)
                    nc.tensor.matmul(ps[:, bank, 0:P], masks[:, 0, :], masks[:, 1, :], start=True, **kw)
                    nc.tensor.matmul(ps[:, bank, 2 * P:3 * P], masks[:, 0, :], masks[:, 1, :], start=False, **kw)
                    if r == 1:
                        pe.wait_ge(g_d, b * NH + h + 1)
                        d = dg[:, h % NDG, :, :]
                        nc.tensor.matmul(ps[:, bank, 0:P], masks[:, 2, :], d[:, 0, :], start=False, **kw)
                        nc.tensor.matmul(ps[:, bank, P:2 * P], masks[:, 3, :], d[:, 0, :], start=False, **kw)
                        nc.tensor.matmul(ps[:, bank, 2 * P:3 * P], masks[:, 2, :], d[:, 1, :], start=False, **kw)
                    nc.tensor.matmul(ps[:, bank, 0:P], rot[:, 0, m, 0:P], kz[:, q, m, 0:P],
                                     start=False, stop=True, skip_group_check=True)
                    nc.tensor.matmul(ps[:, bank, P:P + S], rot[:, 0, m, P:S], kz[:, q, m, :],
                                     start=False, stop=True, skip_group_check=True).then_inc(p_s, 1)

                def project(b):
                    for i, w in enumerate((wq, wk)):
                        for m in range(KD):
                            for k in range(KD):
                                last = nc.tensor.matmul(ps[:, 2 * i + m // 2, (m % 2) * S:(m % 2 + 1) * S],
                                                        w[:, k, m * P:(m + 1) * P],
                                                        hT[:, k, bass.ds(b, 1), :].rearrange("p a s -> p (a s)"),
                                                        start=(k == 0 and m % 2 == 0), stop=(k == KD - 1),
                                                        skip_group_check=True)
                        last.then_inc(p_qk, 1)

                def swap(b, i):
                    pe.wait_ge(a_raw, b * 2 + i + 1)
                    for m in range(KD):
                        last = nc.tensor.matmul(ps[:, 4 + 2 * i + m // 2, (m % 2) * S:(m % 2 + 1) * S],
                                                tab[:, C_ROT:C_ROT + P], raw[:, i, m, :],
                                                start=(m % 2 == 0), stop=True, skip_group_check=True)
                    last.then_inc(p_rot, 1)

                def batch(b, more):
                    for h in range(NH + AHEAD_SUMS):
                        if h < NH:
                            scores(b, 0, h)
                        if h == NH:
                            pe.wait_ge(c_hb, b + 1)
                            for c in range(KS):
                                for k in range(KD):
                                    last = nc.tensor.matmul(ps[:, 6 + c, :], hb[:, k, c * P:(c + 1) * P], wv[:, k, :],
                                                            start=(k == 0), stop=(k == KD - 1))
                            last.then_inc(p_v, 1)
                        g = h - AHEAD_SUMS
                        if g >= 0 and g % CGS == CGS - 1:
                            g0 = g - CGS + 1
                            pe.wait_ge(v_d, b * NH + g + 1)
                            for part, (e0, e1) in enumerate(((0, P), (P, P + S))):
                                for g in range(g0, g0 + CGS):
                                    rows = (g % CGS) * CG
                                    last = nc.tensor.matmul(ps[rows:rows + CG, 4, 0:e1 - e0], rdiag[:, g, part, :],
                                                            E[:, g % NEX, e0:e1], start=(g0 == 0 and part == 0),
                                                            stop=(g0 + CGS == NH and part == 1),
                                                            tile_position=(0, rows), skip_group_check=True)
                            last.then_inc(p_c, 1)
                    if more:
                        pe.wait_ge(a_e, (b * 2 * NH + NH) * 2)
                        project(b + 1)
                    pe.wait_ge(v_k, b * K_STEPS + K_STEPS)
                    for c in range(KS):
                        last = nc.tensor.matmul(ps[:, 5, c * P:(c + 1) * P], light[:, c * P:(c + 1) * P],
                                                ident, start=True, stop=True)
                    last.then_inc(p_l, 1)
                    for h in range(NH + AHEAD + 1):
                        if h < NH:
                            scores(b, 1, h, more)
                        g = h - AHEAD
                        if 0 <= g < NH:
                            n = b * NH + g
                            pe.wait_ge(v_n, (n + 1) * 2 + 1)
                            if g < 2:
                                if g == 0:
                                    pe.wait_ge(v_l, b + 1)
                            else:
                                pe.wait_ge(a_t, n - 1)
                            bank = 4 + g % 2
                            for c in range(3):
                                last = nc.tensor.transpose(ps[:, bank, c * P:(c + 1) * P],
                                                           En[:, g % NEN, c * P:(c + 1) * P], ident)
                            last.then_inc(p_t, 1)
                        g = h - AHEAD - 1
                        if g >= 0 and g % HPC == HPC - 1:
                            m = g // HPC
                            pe.wait_ge(a_t, b * NH + g + 1)
                            if m == 0:
                                pe.wait_ge(a_v, b + 1)
                            if m >= 2:
                                pe.wait_ge(a_o, b * KD + m - 1)
                            for q in range(HPC):
                                hh = m * HPC + q
                                o = ps[q * DH2:(q + 1) * DH2, 6 + m % 2, :]
                                nc.tensor.matmul(o[:, 0:S], v[:, 0, hh * DH2:(hh + 1) * DH2], ET[:, q, 0:S],
                                                 start=True, stop=False, tile_position=(0, q * DH2),
                                                 skip_group_check=True)
                                last = nc.tensor.matmul(o[:, P:S], v[:, 1, hh * DH2:(hh + 1) * DH2], ET[:, q, S:S + P],
                                                        start=False, stop=True, tile_position=(0, q * DH2),
                                                        skip_group_check=True)
                            last.then_inc(p_av, 1)
                    if more:
                        swap(b + 1, 0)
                    pe.wait_ge(a_o, (b + 1) * KD)
                    if more:
                        swap(b + 1, 1)
                    for m in range(KD):
                        for k in range(KD):
                            last = nc.tensor.matmul(ps[:, m, 0:S], wo[:, k, m * P:(m + 1) * P], oT[:, k, :],
                                                    start=(k == 0), stop=(k == KD - 1))
                        last.then_inc(p_o, 1)

                project(0)
                for i in range(2):
                    swap(0, i)
                with pe.Fori(0, B - 1) as b:
                    batch(b, True)
                batch(B - 1, False)

            @block.scalar
            def _(act):
                def exps(b, r, h):
                    n = b * (2 * NH) + r * NH + h
                    act.wait_ge(v_m, n + 1)
                    if r == 0:
                        if h >= NEX:
                            act.wait_ge(p_c, b * (NH // CGS) + (h - NEX) // CGS + 1)
                        else:
                            act.wait_ge(v_n, b * (2 * NH) + 1)
                    else:
                        if h >= NEX:
                            act.wait_ge(v_n, (b * NH + h - NEX + 1) * 2 + 1)
                        else:
                            act.wait_ge(p_c, (b + 1) * (NH // CGS))
                    bank = h % 4
                    nc.scalar.activation(E[:, h % NEX, 0:P], ps[:, bank, 0:P], ACT.Exp, bias=nm[:, r, h, 0:1],
                                         accum_out=ls[:, r, h, 0:1]).then_inc(a_e, 1)
                    nc.scalar.activation(E[:, h % NEX, P:P + S], ps[:, bank, P:P + S], ACT.Exp,
                                         bias=nm[:, r, h, 1:2], accum_out=ls[:, r, h, 1:2]).then_inc(a_e, 1)

                act.nop().then_inc(a_kz, 1)
                act.wait_ge(d_tab, 16)
                def copy_raw(b):
                    for i in range(2):
                        act.wait_ge(p_qk, b * 2 + i + 1)
                        nc.scalar.activation(raw[:, i, :, :].rearrange("p m s -> p (m s)"),
                                             ps[:, 2 * i:2 * i + 2, :].rearrange("p a n -> p (a n)"),
                                             ACT.Copy).then_inc(a_raw, 1)

                def batch(b, more):
                    act.wait_ge(v_rot, b * 6 + 6)
                    for q in range(2):
                        nc.scalar.activation(kz[:, q, :, :].rearrange("p m s -> p (m s)"),
                                             rot[:, 1, :, :].rearrange("p m s -> p (m s)"), ACT.Copy,
                                             scale=tab[:, C_HEAD + q:C_HEAD + q + 1]).then_inc(a_kz, 1)
                    for h in range(NH):
                        exps(b, 0, h)
                    act.wait_ge(p_v, b + 2)
                    nc.scalar.activation(v[:, :, :].rearrange("p c d -> p (c d)"),
                                         ps[:, 6:8, :].rearrange("p a n -> p (a n)"), ACT.Copy).then_inc(a_v, 1)
                    if more:
                        copy_raw(b + 1)
                    for h in range(NH + 2):
                        if h < NH:
                            exps(b, 1, h)
                        g = h - 2
                        if g >= 0:
                            n = b * NH + g
                            act.wait_ge(p_t, n + 1)
                            if g % HPC == 0 and g >= HPC:
                                act.wait_ge(p_av, b * KD + g // HPC)
                            nc.scalar.activation(ET[:, g % HPC, :], ps[:, 4 + g % 2, 0:P + S], ACT.Copy)\
                                .then_inc(a_t, 1)
                            if g % HPC == 1 and g >= HPC:
                                m = g // HPC - 1
                                act.wait_ge(p_av, b * KD + m + 1)
                                nc.scalar.activation(oT[:, m, :], ps[:, 6 + m % 2, 0:S], ACT.Copy).then_inc(a_o, 1)
                    act.wait_ge(p_av, (b + 1) * KD)
                    nc.scalar.activation(oT[:, KD - 1, :], ps[:, 6 + (KD - 1) % 2, 0:S], ACT.Copy).then_inc(a_o, 1)

                copy_raw(0)
                with act.Fori(0, B - 1) as b:
                    batch(b, True)
                batch(B - 1, False)

            @block.vector
            def _(dve):
                dve.wait_ge(d_tab, 16)
                nc.vector.tensor_copy(masks[:, 0, :], ident)
                for i, c in enumerate((C_CAUS, C_NB0, C_NB1)):
                    last = nc.vector.tensor_copy(masks[:, i + 1, :], tab[:, c:c + P])
                last.then_inc(v_init, 1)
                nc.vector.memset(rdiag[:, :, :, :], 0.0).then_inc(v_init, 1)
                nc.vector.memset(ls[:, :, :, :], 1.0).then_inc(v_init, 1)
                dve.nop().then_inc(v_x, 1)
                dve.nop().then_inc(v_n, 1)
                dve.wait_ge(v_init, 3)

                def maxima(b, r, h):
                    n = b * (2 * NH) + r * NH + h
                    dve.wait_ge(p_s, n + 2)
                    bank = h % 4
                    nc.vector.tensor_reduce(nm[:, r, h, 0:1], ps[:, bank, 0:P], AX.X, ALU.max, negate=True)
                    nc.vector.tensor_reduce(nm[:, r, h, 1:2], ps[:, bank, P:P + S], AX.X, ALU.max,
                                            negate=True).then_inc(v_m, 1)

                def recip(b, r, h):
                    n = b * (2 * NH) + r * NH + h
                    dve.wait_ge(a_e, (n + 1) * 2)
                    nc.vector.reciprocal(rl[:, r, h, :], ls[:, r, h, :]).then_inc(v_r, 1)
                    dve.wait_ge(v_r, n + 1)

                def rotate(b):
                    for i, (c, s) in enumerate(((C_COSQ, C_SINQ), (C_COSK, C_SINK))):
                        dve.wait_ge(p_rot, b * 2 + i + 1)
                        if i == 0:
                            dve.wait_ge(p_s, b * 2 * NH + 1)
                            dve.wait_ge(a_kz, b * 2 + 1)
                        cos = tab[:, c:c + S].unsqueeze(1).broadcast_to((P, KD, S))
                        sin = tab[:, s:s + S].unsqueeze(1).broadcast_to((P, KD, S))
                        nc.vector.tensor_tensor(tmp[:, :, :],
                                                ps[:, 4 + 2 * i:6 + 2 * i, :].rearrange("p a (m s) -> p (a m) s", s=S),
                                                sin, ALU.mult).then_inc(v_rot, 1)
                        nc.vector.tensor_tensor(rot[:, i, :, :], raw[:, i, :, :], cos, ALU.mult).then_inc(v_rot, 1)
                        dve.wait_ge(v_rot, b * 6 + 3 * i + 2)
                        nc.vector.tensor_tensor(rot[:, i, :, :], rot[:, i, :, :], tmp[:, :, :], ALU.add)\
                            .then_inc(v_rot, 1)
                        dve.wait_ge(v_rot, b * 6 + 3 * i + 3)
                    for q in range(2, HPC):
                        nc.vector.tensor_scalar(kz[:, q, :, :], rot[:, 1, :, :], tab[:, C_HEAD + q:C_HEAD + q + 1],
                                                None, ALU.mult).then_inc(v_kz, 1)

                def batch(b, more):
                    for h in range(NH + 1):
                        if h < NH:
                            maxima(b, 0, h)
                        if h >= 1:
                            g = h - 1
                            recip(b, 0, g)
                            nc.vector.tensor_copy(rdiag[:, g, :, g // CGS], rl[:, 0, g, :]).then_inc(v_d, 1)
                    dve.wait_ge(p_c, (b + 1) * (NH // CGS))
                    c = [0]

                    def step(i_):
                        c[0] += 1
                        i_.then_inc(v_k, 1)
                        dve.drain()

                    step(nc.vector.tensor_copy(tsum[:, :], ps[:, 4, 0:S]))
                    src = tsum
                    for _ in range(HEAVY // 8):
                        step(nc.vector.max(top8[:, :], src[:, :]))
                        step(nc.vector.match_replace(work[:, :], top8[:, :], src[:, :], -1.0))
                        src = work
                    for _ in range(HEAVY % 8):
                        step(nc.vector.max(top8[:, :], work[:, :]))
                        step(nc.vector.scalar_tensor_tensor(out=code[:, :], in0=work[:, :], scalar=top8[:, 0:1],
                                                            in1=tab[:, C_DESC:C_DESC + S],
                                                            op0=ALU.is_equal, op1=ALU.mult))
                        step(nc.vector.tensor_reduce(cmax[:, :], code[:, :], AX.X, ALU.max))
                        step(nc.vector.tensor_scalar(code[:, :], code[:, :], cmax[:, 0:1], -1e6,
                                                     ALU.is_equal, ALU.mult))
                        step(nc.vector.tensor_tensor(work[:, :], work[:, :], code[:, :], ALU.add))
                    step(nc.vector.tensor_scalar(light[:, :], work[:, :], 0.0, None, ALU.is_ge))
                    assert c[0] == K_STEPS
                    dve.wait_ge(p_l, b + 1)
                    nc.vector.tensor_copy(lcol[:, :, :].rearrange("p c h -> p (c h)"), ps[:, 5, 0:KS * P])\
                        .then_inc(v_l, 1)

                    for h in range(NH + 1):
                        if h < NH:
                            maxima(b, 1, h)
                        if h >= 1:
                            g = h - 1
                            recip(b, 1, g)
                            if g >= NEN:
                                dve.wait_ge(p_t, b * NH + g - NEN + 1)
                            nc.vector.tensor_scalar(En[:, g % NEN, 0:P], E[:, g % NEX, 0:P], rl[:, 1, g, 0:1], None,
                                                    ALU.mult).then_inc(v_n, 1)
                            nc.vector.tensor_scalar(En[:, g % NEN, P:P + S], E[:, g % NEX, P:P + S], rl[:, 1, g, 1:2],
                                                    None, ALU.mult).then_inc(v_n, 1)
                    if more:
                        rotate(b + 1)
                    dve.wait_ge(d_xT, 16)
                    for m in range(KD):
                        dve.wait_ge(p_o, b * KD + m + 1)
                        xv = x1T[:, m, :, bass.ds(b, 1)].rearrange("p s a -> p (s a)")
                        nc.vector.tensor_tensor(xv, ps[:, m, 0:S], xv, ALU.add).then_inc(v_x, 1)

                rotate(0)
                with dve.Fori(0, B - 1) as b:
                    batch(b, True)
                batch(B - 1, False)


AHEAD_SUMS, AHEAD = 3, 3
NEX = 8
NEN = 3
CGS = 4
CG = P // CGS


def row_of(h):
    return (h % CGS) * CG + h // CGS


NDG = 3
K_STEPS = 2 + 2 * (HEAVY // 8) + 5 * (HEAVY % 8)


NCH = NE * FC
DOWN_FIRST, DOWN_LAST = 10, 38
DOWN_AT = [DOWN_FIRST + n * (DOWN_LAST - DOWN_FIRST + 1) // (2 * NCH) for n in range(2 * NCH)]


def room_for_ups():
    load = [sum(x % SPT == s for x in DOWN_AT) for s in range(SPT)]
    at, s = [], 1
    for _ in range(2 * NCH):
        while load[s] >= 3 + (s % MORE == 1) or at[-2:] == [s, s]:
            s += 1
        at.append(s)
        load[s] += 1
    return at


MORE = 4
UP_AT = room_for_ups()
ACT_AT = [x + 1 for x in UP_AT[1::2]]
GATE_AT = [max(ACT_AT[i] + 1, 6 + 2 * (i // FC) + i % FC // 2) for i in range(NCH)]
CAST_AT = [x + 1 for x in GATE_AT]
REST_AT = [x + 2 for x in GATE_AT]
BCAST_AT = [GATE_AT[e * FC] - 2 for e in range(NE)]
CB_AT = [x + 1 for x in BCAST_AT]
B2_AT = [9, 10, 9, 9]
Y_AT = [39, 39, 40, 40]
TB = 8
RING = 8


def earlier(at, i, back):
    return at[i - back] if i >= back else at[i - back + len(at)] - SPT


assert NCH % TB == 0 and NCH % RING == 0 and NCH % 2 == 0 and NE % 2 == 0
for _i in range(NCH):
    assert UP_AT[2 * _i] >= earlier(ACT_AT, _i, 2)
    assert DOWN_AT[2 * _i] > REST_AT[_i]
    assert CAST_AT[_i] > earlier(DOWN_AT[1::2], _i, RING)
    assert ACT_AT[_i] > earlier(REST_AT, _i, TB)
for _e in range(NE):
    assert BCAST_AT[_e] > earlier(CB_AT, _e, 1)
    assert CB_AT[_e] > earlier(GATE_AT[FC - 1::FC], _e, 2)
assert UP_AT[-1] < SPT - 1 and BCAST_AT[0] >= 4 and CB_AT[NE - 1] < SPT
assert DOWN_AT[-1] < Y_AT[0] and Y_AT[KD - 1] - SPT < B2_AT[0] and B2_AT[KD - 1] <= DOWN_AT[0]


LAST_STEPS = Y_AT[-1] - SPT + 1


def due(at, s, f, now, late):
    return ([(i, f - 1) for i, x in enumerate(at) if late and x == s + SPT] +
            [(i, f) for i, x in enumerate(at) if now and x == s])


def so_far(f, per_tile, n):
    return max(f * per_tile + n, 0) if isinstance(f, int) else f * per_tile + n


WIDE = 2
R_STEPS = 17


def gru_and_ffn(nc, ins, out, ps, cst, ident, x1T, sb, sem):
    top = ExitStack()
    with top:
        whf = sb(top, "whf", [P, KD, G3])
        w1f = sb(top, "w1f", [P, KD, 2, EH * HFP])
        w2f = sb(top, "w2f", [P, FC, 2, EH * D])
        gi = sb(top, "gi", [P, NQ, SPT, B])
        h32 = sb(top, "h32", [P, KD, B])
        hp = sb(top, "hp", [P, KD, 2, B], F16)
        gwp = sb(top, "gwp", [P, KD, 2, NE], F16)
        b1 = sb(top, "b1", [P, FC, NE])
        b1s = sb(top, "b1s", [P, FC, NE])
        b2 = sb(top, "b2", [NE, D])
        gb = sb(top, "gb", [P, NE])
        bhp = sb(top, "bhp", [2, D], F16)
        ones2 = sb(top, "ones2", [2, 2 * B], F16)
        sc = sb(top, "sc", [P, N_SC])
        gi_d = nc.dram_tensor("gi_d", [P, NQ, S, B], F32).ap()
        prepare(nc, ins, ps, cst, ident, x1T, whf, w1f, w2f, gi_d, h32, hp, gwp, b1, b1s, b2, gb, bhp, ones2, sc, sb, sem)
        recurrence_and_ffn(nc, ins, out, ps, cst, ident, x1T, whf, w1f, w2f, gi, gi_d, h32, hp, gwp, b1, b1s, b2, gb,
                           bhp, ones2, sc, sb, sem)


BEFORE = 4
O_WHH, O_H, O_W1, O_W2, O_GW, O_B1 = range(6)
S_H, S_WHH, S_W1, S_W2, S_GW, S_UNG, S_UN1, S_UN1I, S_CB, S_UN2, S_UN2I, S_UNR, S_U, S_T = range(6, 20)
N_SC = 20


def prepare(nc, ins, ps, cst, ident, x1T, whf, w1f, w2f, gi_d, h32, hp, gwp, b1, b1s, b2, gb, bhp, ones2, sc, sb, sem):
    st = ExitStack()
    with st:
        wi = sb(st, "wi", [P, KD, G3])
        stage = sb(st, "stage", [P, 4, TT])
        tmp = sb(st, "wtmp", [P, EH * D])
        bgi = sb(st, "bgi", [P, 2, NQ])
        bsum = sb(st, "bsum", [P, NQ])
        gw = sb(st, "gw", [P, KD, NE])
        gb2 = sb(st, "gb2", [P, 2, NE])
        mx = sb(st, "mx", [P, 6, KD + 1])
        mxa = sb(st, "mxa", [P, 6])
        mx1 = sb(st, "mx1", [1, 6])
        ones1 = sb(st, "ones1", [1, P])
        bh32 = sb(st, "bh32", [2, D])
        d_i = sem(st, "q_wi")
        d_b = sem(st, "q_gate_biases")
        d_s = sem(st, "q_small")
        d_w = sem(st, "q_big")
        d_g = [sem(st, f"q_gi{j}") for j in range(4)]
        v_z = sem(st, "q_zero")
        v_b = sem(st, "q_bias")
        v_a = sem(st, "q_v")
        p_a = sem(st, "q_p")
        p_i = sem(st, "q_pi")
        a_i = sem(st, "q_ai")

        with nc.Block() as block:
            @block.sync
            def _(sp):
                sp.dma_start(bgi[:, 0, :], ins["b_ih"]).then_inc(d_b, 16)
                sp.dma_start(bgi[:, 1, :], ins["b_hh"]).then_inc(d_b, 16)
                sp.dma_start(wi[:, :, :], ins["W_ih"].rearrange("(k p) n -> p k n", p=P)).then_inc(d_i, 16)
                sp.dma_start(h32[:, :, :], ins["condT"].rearrange("(k p) b -> p k b", p=P)).then_inc(d_s, 16)
                sp.dma_start(gw[:, :, :], ins["gate_wT"].rearrange("(k p) e -> p k e", p=P)).then_inc(d_s, 16)
                sp.dma_start(gb2[:, 0, :], ins["gate_b"].broadcast_to((P, NE))).then_inc(d_s, 16)
                sp.dma_start(gb2[:, 1, :], ins["bias"].broadcast_to((P, NE))).then_inc(d_s, 16)
                sp.dma_start(b2[:, :], ins["b2"]).then_inc(d_s, 16)
                sp.dma_start(bh32[:, :], ins["b_hh_n"].broadcast_to((2, D))).then_inc(d_s, 16)
                sp.wait_ge(v_z, 3)
                for c in range(FC):
                    rows = P if c < FC - 1 else HL
                    sp.dma_start(b1[0:rows, c, :], ins["b1T"][c * P:c * P + rows]).then_inc(d_s, 16)
                with sp.Fori(0, NT) as t:
                    for q in range(NQ):
                        sp.wait_ge(a_i, t * NQ + q + 2)
                        sp.dma_start(gi_d[:, q, bass.ds(t * SPT, SPT), :].rearrange("p s b -> p (s b)"),
                                     stage[:, q % 4, :]).then_inc(d_g[q % 4], 16)
                for j in range(4):
                    sp.wait_ge(d_g[j], 16 * NT * NQ // 4 + 16)

            @block.tensor
            def _(pe):
                def tiles(t0, t1):
                    with pe.Fori(t0, t1) as t:
                        for q in range(NQ):
                            if q < 4:
                                pe.wait_ge(a_i, t * NQ + 1)
                            else:
                                pe.wait_ge(a_i, t * NQ + q - 2)
                            for k in range(KD):
                                last = nc.tensor.matmul(
                                    ps[:, q % 4, 0:TT], wi[:, k, q * P:(q + 1) * P],
                                    x1T[:, k, bass.ds(t * SPT, SPT), :].rearrange("p s b -> p (s b)"),
                                    start=(k == 0), stop=(k == KD - 1))
                            last.then_inc(p_i, 1)

                pe.wait_ge(d_i, 16)
                tiles(0, BEFORE)
                pe.wait_ge(v_a, 9)
                for i in range(6):
                    last = nc.tensor.transpose(ps[0:1, 6 + i // 3, (i % 3) * P:(i % 3 + 1) * P], mxa[:, i:i + 1], ident)
                last.then_inc(p_a, 1)
                pe.wait_ge(v_a, 11)
                nc.tensor.matmul(ps[:, 6, 0:6], ones1[:, :], mx1[:, :], start=True, stop=True).then_inc(p_a, 1)
                tiles(BEFORE, NT)

            @block.scalar
            def _(act):
                act.wait_ge(v_b, 1)
                act.nop().then_inc(a_i, 1)
                with act.Fori(0, NT) as t:
                    for q in range(NQ):
                        act.wait_ge(d_g[q % 4], t * (16 * NQ // 4) + 16 * (q // 4) + 16)
                        act.wait_ge(p_i, t * NQ + q + 1)
                        nc.scalar.activation(stage[:, q % 4, :], ps[:, q % 4, 0:TT], ACT.Identity,
                                             bias=bsum[:, q:q + 1]).then_inc(a_i, 1)

            @block.gpsimd
            def _(pool):
                for j in range(4):
                    pool.nop().then_inc(d_g[j], 16)
                nc.gpsimd.memset(w1f[:, :, :, :].rearrange("p k a (e h) -> p (k a e) h", h=HFP)[:, :, HF:HFP], 0.0)\
                    .then_inc(v_z, 1)
                pool.wait_ge(v_z, 1)
                nc.gpsimd.memset(w2f[HL:P, FC - 1, :, :], 0.0).then_inc(v_z, 1)
                pool.wait_ge(v_z, 2)
                nc.gpsimd.memset(b1[:, :, :], 0.0).then_inc(v_z, 1)
                pool.wait_ge(v_z, 3)
                pieces = [(whf[:, k, :], ins["W_hh"][k * P:(k + 1) * P, :]) for k in range(KD)]
                pieces += [(w1f[:, k, :, :].rearrange("p a (e h) -> p (a e) h", h=HFP)[:, :, 0:HF],
                            ins["w1T"][k * P:(k + 1) * P, :].rearrange("p (e h) -> p e h", h=HF)) for k in range(KD)]
                pieces += [(w2f[0:min(P, HF - c * P), c, :, :].rearrange("p a n -> p (a n)"),
                            ins["w2T"][c * P:min((c + 1) * P, HF)].rearrange("p e d -> p (e d)")) for c in range(FC)]
                for j, (to, source) in enumerate(pieces):
                    pool.wait_ge(a_i, 5 * j // 2 + 2)
                    pool.dma_start(to, source).then_inc(d_w, 16)

            @block.vector
            def _(dve):
                n = [0]

                def step(i_):
                    n[0] += 1
                    i_.then_inc(v_a, 1)
                    dve.wait_ge(v_a, n[0])

                def big(o, i_):
                    return nc.vector.tensor_reduce(o, i_, AX.XY if len(i_.shape) == 3 else AX.X, ALU.max,
                                                   apply_absolute_value=True)

                dve.wait_ge(d_b, 32)
                step(nc.vector.tensor_copy(bsum[:, :], bgi[:, 0, :]))
                nc.vector.tensor_tensor(bsum[:, 0:2 * KD], bgi[:, 0, 0:2 * KD], bgi[:, 1, 0:2 * KD], ALU.add)\
                    .then_inc(v_b, 1)
                step(nc.vector.memset(ones2[:, :], 0.0))
                dve.wait_ge(d_s, 16 * (6 + FC))
                step(nc.vector.tensor_tensor(gb[:, :], gb2[:, 0, :], gb2[:, 1, :], ALU.add))
                step(nc.vector.memset(mx[:, :, :], 0.0))
                step(nc.vector.memset(ones1[:, :], 1.0))
                big(mx[:, O_H, 0:1], h32[:, :, :])
                big(mx[:, O_GW, 0:1], gw[:, :, :])
                big(mx[:, O_WHH, KD:KD + 1], bgi[:, 1, 2 * KD:NQ])
                step(big(mx[:, O_B1, 0:1], b1[:, :, :]))
                dve.wait_ge(d_w, 16 * (2 * KD + FC))
                for k in range(KD):
                    big(mx[:, O_WHH, k:k + 1], whf[:, k, :])
                    big(mx[:, O_W1, k:k + 1], w1f[:, k, :, :])
                for c in range(FC):
                    last = big(mx[:, O_W2, c:c + 1], w2f[:, c, :, :])
                step(last)
                step(nc.vector.tensor_reduce(mxa[:, :], mx[:, :, :], AX.X, ALU.max))
                dve.wait_ge(v_a, 8)
                step(nc.vector.memset(mx1[:, :], 0.0))
                dve.wait_ge(p_a, 1)
                nc.vector.tensor_reduce(mx1[:, 0:3], ps[0:1, 6, 0:3 * P].rearrange("p (i n) -> p i n", i=3), AX.X, ALU.max)
                step(nc.vector.tensor_reduce(mx1[:, 3:6], ps[0:1, 7, 0:3 * P].rearrange("p (i n) -> p i n", i=3),
                                             AX.X, ALU.max))
                nc.vector.tensor_scalar(mx1[:, O_H:O_H + 1], mx1[:, O_H:O_H + 1], 1.0, None, ALU.max).then_inc(v_a, 1)
                n[0] += 1
                dve.wait_ge(p_a, 2)
                dve.wait_ge(v_a, n[0])
                step(nc.vector.tensor_scalar(sc[:, 0:6], ps[:, 6, 0:6], 1e-6, None, ALU.max))

                def pow2(i, j):
                    step(nc.vector.tensor_scalar(sc[:, i:j].bitcast(I32), sc[:, i:j].bitcast(I32), 0x7F800000, None,
                                                 ALU.bitwise_and))

                def times(o, a, b, f=1.0):
                    step(nc.vector.tensor_scalar(sc[:, o:o + 1], sc[:, a:a + 1], sc[:, b:b + 1], f, ALU.mult, ALU.mult))

                def inverse(o, a, f=1.0):
                    step(nc.vector.reciprocal(sc[:, o:o + 1], sc[:, a:a + 1]))
                    if f != 1.0:
                        step(nc.vector.tensor_scalar(sc[:, o:o + 1], sc[:, o:o + 1], f, None, ALU.mult))

                pow2(0, 6)
                for o, a in ((S_H, O_H), (S_WHH, O_WHH), (S_W1, O_W1), (S_W2, O_W2), (S_GW, O_GW)):
                    inverse(o, a, 2.0 ** 14)
                times(S_T, O_W1, O_H, 4.0 * D)
                step(nc.vector.scalar_tensor_tensor(out=sc[:, S_U:S_U + 1], in0=sc[:, O_B1:O_B1 + 1], scalar=2.0,
                                                    in1=sc[:, S_T:S_T + 1], op0=ALU.mult, op1=ALU.add))
                pow2(S_U, S_U + 1)
                step(nc.vector.reciprocal(sc[:, S_U:S_U + 1], sc[:, S_U:S_U + 1]))
                step(nc.vector.tensor_scalar(sc[:, S_U:S_U + 1], sc[:, S_U:S_U + 1], 2.0 ** 14, None, ALU.mult))
                times(S_T, S_WHH, S_H)
                inverse(S_UNG, S_T)
                times(S_UN1I, S_W1, S_H)
                inverse(S_UN1, S_UN1I)
                times(S_CB, S_U, S_UN1)
                times(S_UN2I, S_W2, S_U)
                inverse(S_UN2, S_UN2I)
                times(S_T, S_GW, S_H)
                inverse(S_UNR, S_T)

                def split(f32, s, width):
                    t = tmp[:, 0:width]
                    half = f32.bitcast(F16)
                    step(nc.vector.tensor_scalar(t, f32, sc[:, s:s + 1], None, ALU.mult))
                    step(nc.vector.tensor_copy(half[:, 0:width], t))
                    step(nc.vector.tensor_tensor(half[:, width:2 * width], t, half[:, 0:width], ALU.subtract))

                for k in range(KD):
                    split(whf[:, k, :], S_WHH, G3)
                for k in range(KD):
                    for a in range(2):
                        split(w1f[:, k, a, :], S_W1, EH * HFP)
                for c in range(FC):
                    for a in range(2):
                        split(w2f[:, c, a, :], S_W2, EH * D)
                bhi = tmp[0:2, 0:D // 2].bitcast(F16)
                step(nc.vector.tensor_copy(ones2[:, 0:B], sc[0:2, S_H:S_H + 1].broadcast_to((2, B))))
                step(nc.vector.tensor_scalar(bh32[:, :], bh32[:, :], sc[0:2, S_WHH:S_WHH + 1], None, ALU.mult))
                step(nc.vector.tensor_copy(bhi, bh32[:, :]))
                step(nc.vector.tensor_tensor(bh32[:, :], bh32[:, :], bhi, ALU.subtract))
                step(nc.vector.tensor_scalar(bh32[:, :], bh32[:, :], ident[0:2, 1:2], None, ALU.mult))
                step(nc.vector.scalar_tensor_tensor(out=bhp[:, :], in0=bhi, scalar=ident[0:2, 0:1],
                                                    in1=bh32[:, :], op0=ALU.mult, op1=ALU.add))
                step(nc.vector.tensor_scalar(h32[:, :, :], h32[:, :, :], sc[:, S_H:S_H + 1], None, ALU.mult))
                step(nc.vector.tensor_copy(hp[:, :, 0, :], h32[:, :, :]))
                step(nc.vector.tensor_tensor(hp[:, :, 1, :], h32[:, :, :], hp[:, :, 0, :], ALU.subtract))
                step(nc.vector.tensor_scalar(gw[:, :, :], gw[:, :, :], sc[:, S_GW:S_GW + 1], None, ALU.mult))
                step(nc.vector.tensor_copy(gwp[:, :, 0, :], gw[:, :, :]))
                step(nc.vector.tensor_tensor(gwp[:, :, 1, :], gw[:, :, :], gwp[:, :, 0, :], ALU.subtract))
                step(nc.vector.tensor_scalar(b1s[:, :, :], b1[:, :, :], sc[:, S_UN1I:S_UN1I + 1], None, ALU.mult))
                step(nc.vector.tensor_scalar(b2[:, :], b2[:, :], sc[0:NE, S_UN2I:S_UN2I + 1], None, ALU.mult))


def recurrence_and_ffn(nc, ins, out, ps, cst, ident, x1T, whf, w1f, w2f, gi, gi_d, h32, hp, gwp, b1, b1s, b2, gb,
                       bhp, ones2, sc, sb, sem):
    whp = whf[:, :, :].bitcast(F16).rearrange("p k (w q n) -> p k w q n", w=2, q=3)
    w1p = w1f[:, :, :, :].rearrange("p k a n -> p (k a) n").bitcast(F16)
    w2p = w2f[:, :, :, :].rearrange("p c a n -> p (c a) n").bitcast(F16)
    st = ExitStack()
    with st:
        s1 = sb(st, "s1", [P, 2, KD, B])
        rz = sb(st, "rz", [P, 2, KD, B])
        cn = sb(st, "cn", [P, KD, B])
        ab = sb(st, "ab", [P, KD, 2, B])
        hn = sb(st, "hn", [P, KD, B])
        nn = sb(st, "nn", [P, KD, B])
        ns = sb(st, "ns", [P, KD, B])
        dh = sb(st, "dh", [P, KD, B])
        nxt = sb(st, "nxt", [P, KD, 2, SPT, B], F16)
        cur = sb(st, "cur", [P, KD, 2, SPT, B], F16)
        scr = sb(st, "scr", [P, 2, NE])
        m1 = sb(st, "m1", [P, 2])
        m2 = sb(st, "m2", [P, 2])
        o1 = sb(st, "o1", [P, 2, NE])
        o2 = sb(st, "o2", [P, 2, NE])
        cd = sb(st, "cd", [P, 2, NE])
        cm = sb(st, "cm", [P, 2])
        dg = sb(st, "dgap", [P, 2])
        g1 = sb(st, "g1", [P, 2, 2])
        comb = sb(st, "comb", [P, 2, NE])
        combT = sb(st, "combT", [NE, TT])
        cb = sb(st, "cb", [P, 2, TT])
        sg = sb(st, "sg", [P, 2, TT])
        tb = sb(st, "tb", [P, TB, TT])
        hh = sb(st, "hh", [P, RING, 2, TT], F16)

        d_g = [sem(st, "d_g0"), sem(st, "d_g1")]
        p_r = sem(st, "p_r")
        p_n = sem(st, "p_n")
        p_z = sem(st, "p_z")
        v_sr = sem(st, "v_sr")
        a_r = sem(st, "a_r")
        v_sz = sem(st, "v_sz")
        a_z = sem(st, "a_z")
        v_ab = sem(st, "v_ab")
        v_d = sem(st, "v_d")
        a_t = sem(st, "a_t")
        v_h = sem(st, "v_h")
        a_ar = sem(st, "a_ar")
        v_cur = sem(st, "v_cur")
        p_sc = sem(st, "p_sc")
        v_rt = sem(st, "v_rt")
        a_g = sem(st, "a_g")
        p_ct = sem(st, "p_ct")
        v_ct = sem(st, "v_ct")
        p_bc = sem(st, "p_bc")
        a_cb = sem(st, "a_cb")
        p_up = sem(st, "p_up")
        a_sg = sem(st, "a_sg")
        v_t = sem(st, "v_t")
        v_u = sem(st, "v_u")
        a_h = sem(st, "a_h")
        g_l = sem(st, "g_l")
        p_dn = sem(st, "p_dn")
        v_y = sem(st, "v_y")
        d_o = sem(st, "d_o")

        def ready(eng, s, count):
            eng.wait_ge(s, count + 1)

        def start(eng, *sems):
            for s in sems:
                eng.nop().then_inc(s, 1)

        with nc.Block() as block:
            @block.sync
            def _(sp):
                def load(t, half):
                    s0 = half * (SPT // 2)
                    sp.dma_start(gi[:, :, s0:s0 + SPT // 2, :].rearrange("p q s b -> p q (s b)"),
                                 gi_d[:, :, bass.ds(t * SPT + s0, SPT // 2), :].rearrange("p q s b -> p q (s b)"))\
                        .then_inc(d_g[half], 16)

                def store(f):
                    ready(sp, v_y, (f + 1) * KD)
                    sp.dma_start(out[:, bass.ds(f * TT, TT)].rearrange("(k p) n -> p k n", p=P),
                                 x1T[:, :, bass.ds(f * SPT, SPT), :].rearrange("p k s b -> p k (s b)"))\
                        .then_inc(d_o, 16)

                def next_loads(t):
                    for half in range(2):
                        ready(sp, v_h, (t * SPT + (half + 1) * (SPT // 2)) * 4)
                        load(t + 1, half)

                for half in range(2):
                    load(0, half)
                next_loads(0)
                next_loads(1)
                with sp.Fori(2, NT - 1) as t:
                    store(t - 2)
                    next_loads(t)
                for f in range(NT - 3, NT):
                    store(f)
                sp.wait_ge(d_o, 16 * NT)

            @block.tensor
            def _(pe):
                def up(f, i, half):
                    e, c = i // FC, i % FC
                    if half == 0:
                        ready(pe, v_t, so_far(f, NCH, i - 1))
                    for k in range(2 * half, 2 * half + 2):
                        w = w1p[:, k * 2 + e // EH, :].rearrange("p (w e h) -> p w e h", w=2, e=EH)
                        for n, (wp, hq) in enumerate(((0, 0), (0, 1), (1, 0))):
                            last = nc.tensor.matmul(ps[:, 6 + i % 2, 0:TT], w[:, wp, e % EH, c * P:(c + 1) * P],
                                                    cur[:, k, hq, :, :].rearrange("p s b -> p (s b)"),
                                                    start=(k == 0 and n == 0), stop=(k == KD - 1 and n == 2))
                    if half:
                        last.then_inc(p_up, 1)

                def second_biases(f, m):
                    if m == 0:
                        ready(pe, v_y, f * KD)
                    nc.tensor.matmul(ps[:, 4 + m // 2, (m % 2) * TT:(m % 2 + 1) * TT], b2[:, m * P:(m + 1) * P],
                                     combT[:, :], start=(m % 2 == 0), stop=False, skip_group_check=True)

                def down(f, i, half):
                    e, c = i // FC, i % FC
                    if half == 0:
                        ready(pe, a_h, f * NCH + i + 1)
                        ready(pe, g_l, f * NCH + i + 1)
                    w = w2p[:, c * 2 + e // EH, :].rearrange("p (w e d) -> p w e d", w=2, e=EH)
                    for m in range(2 * half, 2 * half + 2):
                        for n, (wp, hq) in enumerate(((0, 0), (0, 1), (1, 0))):
                            last = nc.tensor.matmul(ps[:, 4 + m // 2, (m % 2) * TT:(m % 2 + 1) * TT],
                                                    w[:, wp, e % EH, m * P:(m + 1) * P], hh[:, i % RING, hq, :],
                                                    start=False, stop=(i == NCH - 1 and n == 2),
                                                    skip_group_check=True)
                    if half:
                        last.then_inc(p_dn, 1)

                def ffn_slice(f, s, now, late):
                    if s == 0 and now:
                        ready(pe, v_cur, f + 1)
                        ready(pe, a_cb, f * NE)
                        for g in range(2):
                            for k in range(KD):
                                for hq in range(2):
                                    last = nc.tensor.matmul(
                                        ps[:, 3, g * 2 * NE:(g + 1) * 2 * NE],
                                        cur[:, k, hq, g * P // B:(g + 1) * P // B, :].rearrange("p s b -> p (s b)"),
                                        gwp[:, k, :, :].rearrange("p a e -> p (a e)"),
                                        start=(k == 0 and hq == 0 and g == 0), stop=(k == KD - 1 and hq == 1),
                                        skip_group_check=True)
                        last.then_inc(p_sc, 1)
                    if s == 3 and now:
                        ready(pe, v_rt, (f + 1) * R_STEPS)
                        for g in range(2):
                            last = nc.tensor.transpose(ps[0:NE, 3, g * P:(g + 1) * P], comb[:, g, :], ident)
                        last.then_inc(p_ct, 1)
                    for m, g in due(B2_AT, s, f, now, late):
                        second_biases(g, m)
                    for e, g in due(BCAST_AT, s, f, now, late):
                        if e == 0:
                            ready(pe, v_ct, g + 1)
                        ready(pe, a_cb, g * NE + e)
                        nc.tensor.matmul(ps[:, 3, 0:TT], ident[0:NE, e:e + 1].broadcast_to((NE, P)),
                                         combT[:, :], start=True, stop=True).then_inc(p_bc, 1)
                    for i, g in due(DOWN_AT, s, f, now, late):
                        down(g, i // 2, i % 2)
                    for i, g in due(UP_AT, s, f, now, late):
                        up(g, i // 2, i % 2)

                def wide(x):
                    return x.unsqueeze(1).broadcast_to((x.shape[0], WIDE, 2 * B))

                def products(bank, q):
                    for g in range(KD):
                        if q == 2:
                            nc.tensor.matmul(ps[:, bank, g * WIDE * 2 * B:(g + 1) * WIDE * 2 * B], bhp[:, g * P:(g + 1) * P],
                                             wide(ones2[:, :]), start=True, stop=False)
                        for k in range(KD):
                            for w in range(2):
                                last = nc.tensor.matmul(ps[:, bank, g * WIDE * 2 * B:(g + 1) * WIDE * 2 * B],
                                                        whp[:, k, w, q, g * P:(g + 1) * P],
                                                        wide(hp[:, k, :, :].rearrange("p a b -> p (a b)")),
                                                        start=(k == 0 and w == 0 and q != 2),
                                                        stop=(k == KD - 1 and w == 1))
                    return last

                def step(n):
                    ready(pe, v_h, n * 4)
                    products(0, 0).then_inc(p_r, 1)
                    products(1, 2).then_inc(p_n, 1)
                    products(2, 1).then_inc(p_z, 1)

                def tile(t, recur, now, late, steps=SPT):
                    for s in range(steps):
                        if recur:
                            step(t * SPT + s)
                        ffn_slice(t - 1, s, now, late)

                start(pe, p_r, p_n, p_z, p_sc, p_ct, p_bc, p_up, p_dn)
                tile(0, True, False, False)
                tile(1, True, True, False)
                with pe.Fori(2, NT) as t:
                    tile(t, True, True, True)
                tile(NT, False, True, True)
                tile(NT + 1, False, False, True, LAST_STEPS)

            @block.scalar
            def _(act):
                def step(n):
                    def unary(o, i_, func, done):
                        nc.scalar.activation(o.rearrange("p g b -> p (g b)"), i_.rearrange("p g b -> p (g b)"), func)\
                            .then_inc(done, 1)

                    ready(act, v_sr, (n + 1) * 2)
                    unary(rz[:, 0, :, :], s1[:, 0, :, :], ACT.Sigmoid, a_r)
                    ready(act, v_ab, (n + 1) * 3)
                    unary(nn[:, :, :], hn[:, :, :], ACT.Tanh, a_t)
                    ready(act, v_sz, (n + 1) * 2)
                    unary(rz[:, 1, :, :], s1[:, 1, :, :], ACT.Sigmoid, a_z)

                def keep(n, t, s):
                    ready(act, v_h, (n + 1) * 4)
                    if s == 0:
                        ready(act, v_cur, t)
                    nc.scalar.activation(nxt[:, :, :, s, :].rearrange("p k a b -> p (k a) b"),
                                         hp[:, :, :, :].rearrange("p k a b -> p (k a) b"), ACT.Copy)\
                        .then_inc(a_ar, 1)

                def ffn_slice(f, s, now, late):
                    if s == 2 and now:
                        ready(act, v_rt, f * R_STEPS + 14)
                        nc.scalar.activation(g1[:, 0, :], dg[:, :], ACT.Sigmoid)
                        nc.scalar.activation(g1[:, 1, :], dg[:, :], ACT.Sigmoid, scale=-1.0).then_inc(a_g, 1)
                    for i, g in due(ACT_AT, s, f, now, late):
                        e, c = i // FC, i % FC
                        ready(act, p_up, g * NCH + i + 1)
                        ready(act, v_t, so_far(g, NCH, i - 1))
                        nc.scalar.activation(sg[:, i % 2, :], ps[:, 6 + i % 2, 0:TT], ACT.Sigmoid,
                                             bias=b1[:, c, e:e + 1], scale=sc[:, S_UN1:S_UN1 + 1]).then_inc(a_sg, 1)
                    for e, g in due(CB_AT, s, f, now, late):
                        ready(act, p_bc, g * NE + e + 1)
                        ready(act, v_u, so_far(g, NCH, (e - 1) * FC))
                        nc.scalar.activation(cb[:, e % 2, :], ps[:, 3, 0:TT], ACT.Copy,
                                             scale=sc[:, S_CB:S_CB + 1]).then_inc(a_cb, 1)
                    for i, g in due(CAST_AT, s, f, now, late):
                        ready(act, v_u, g * NCH + i + 1)
                        ready(act, p_dn, so_far(g, NCH, i - RING + 1))
                        nc.scalar.activation(hh[:, i % RING, 0, :], tb[:, i % TB, :], ACT.Copy).then_inc(a_h, 1)

                def tile(t, recur, now, late, steps=SPT):
                    for s in range(steps):
                        if recur:
                            step(t * SPT + s)
                        ffn_slice(t - 1, s, now, late)
                        if recur:
                            keep(t * SPT + s, t, s)

                act.preload_act_table_set("sigmoid_and_others")
                start(act, a_r, a_z, a_t, a_ar, a_g, a_cb, a_sg, a_h)
                tile(0, True, False, False)
                tile(1, True, True, False)
                with act.Fori(2, NT) as t:
                    tile(t, True, True, True)
                tile(NT, False, True, True)
                tile(NT + 1, False, False, True, LAST_STEPS)

            @block.gpsimd
            def _(pool):
                def tile(t, now, late, steps=SPT):
                    for s in range(steps):
                        for i, g in due(REST_AT, s, t - 1, now, late):
                            ready(pool, a_h, g * NCH + i + 1)
                            nc.gpsimd.tensor_tensor(hh[:, i % RING, 1, :], tb[:, i % TB, :], hh[:, i % RING, 0, :],
                                                    ALU.subtract).then_inc(g_l, 1)

                start(pool, g_l)
                tile(1, True, False)
                with pool.Fori(2, NT) as t:
                    tile(t, True, True)
                tile(NT, True, True)
                tile(NT + 1, False, True, LAST_STEPS)

            @block.vector
            def _(dve):
                def of_bank(bank):
                    return ps[:, bank, 0:KD * WIDE * 2 * B].rearrange("p (g w b) -> p g w b", g=KD, b=B)[:, :, 0:2, :]

                un_g = sc[:, S_UNG:S_UNG + 1]

                def add_scaled(o, products_, addend, done):
                    nc.vector.scalar_tensor_tensor(out=o, in0=products_, scalar=un_g, in1=addend,
                                                   op0=ALU.mult, op1=ALU.add).then_inc(done, 1)

                def step(n, s):
                    ready(dve, p_r, n + 1)
                    add_scaled(s1[:, 0, :, :], of_bank(0)[:, :, 0, :], gi[:, 0:KD, s, :], v_sr)
                    ready(dve, v_sr, n * 2 + 1)
                    add_scaled(s1[:, 0, :, :], of_bank(0)[:, :, 1, :], s1[:, 0, :, :], v_sr)
                    ready(dve, a_r, n + 1)
                    ready(dve, p_n, n + 1)
                    nc.vector.tensor_tensor(ab[:, :, :, :], of_bank(1),
                                            rz[:, 0, :, :].unsqueeze(2).broadcast_to((P, KD, 2, B)), ALU.mult)\
                        .then_inc(v_ab, 1)
                    ready(dve, v_ab, n * 3 + 1)
                    add_scaled(hn[:, :, :], ab[:, :, 0, :], gi[:, 2 * KD:NQ, s, :], v_ab)
                    ready(dve, v_ab, n * 3 + 2)
                    add_scaled(hn[:, :, :], ab[:, :, 1, :], hn[:, :, :], v_ab)
                    ready(dve, p_z, n + 1)
                    add_scaled(s1[:, 1, :, :], of_bank(2)[:, :, 0, :], gi[:, KD:2 * KD, s, :], v_sz)
                    ready(dve, v_sz, n * 2 + 1)
                    add_scaled(s1[:, 1, :, :], of_bank(2)[:, :, 1, :], s1[:, 1, :, :], v_sz)
                    ready(dve, a_t, n + 1)
                    nc.vector.scalar_tensor_tensor(out=dh[:, :, :], in0=nn[:, :, :], scalar=sc[:, S_H:S_H + 1],
                                                   in1=h32[:, :, :], op0=ALU.mult, op1=ALU.subtract).then_inc(v_d, 1)
                    nc.vector.tensor_scalar(ns[:, :, :], nn[:, :, :], sc[:, S_H:S_H + 1], None, ALU.mult)\
                        .then_inc(v_d, 1)
                    ready(dve, v_d, n * 2 + 1)
                    ready(dve, a_z, n + 1)
                    nc.vector.tensor_tensor(dh[:, :, :], rz[:, 1, :, :], dh[:, :, :], ALU.mult).then_inc(v_h, 1)
                    ready(dve, v_d, n * 2 + 2)
                    ready(dve, a_ar, n)
                    ready(dve, v_h, n * 4 + 1)
                    nc.vector.tensor_tensor(hp[:, :, 0, :], ns[:, :, :], dh[:, :, :], ALU.subtract).then_inc(v_h, 1)
                    nc.vector.tensor_tensor(h32[:, :, :], ns[:, :, :], dh[:, :, :], ALU.subtract).then_inc(v_h, 1)
                    ready(dve, v_h, n * 4 + 3)
                    nc.vector.tensor_tensor(hp[:, :, 1, :], h32[:, :, :], hp[:, :, 0, :], ALU.subtract)\
                        .then_inc(v_h, 1)

                bc = lambda x: x.unsqueeze(2).broadcast_to((P, 2, NE))
                desc = cst[:, C_DESC8:C_DESC8 + NE].unsqueeze(1).broadcast_to((P, 2, NE))

                def choose(f, s):
                    c = [{0: 0, 1: 7, 2: 14}[s]]

                    def link(i_):
                        c[0] += 1
                        i_.then_inc(v_rt, 1)
                        ready(dve, v_rt, f * R_STEPS + c[0])

                    sp = ps[:, 3, 0:4 * NE].rearrange("p (g a e) -> p g a e", g=2, a=2)
                    un = sc[:, S_UNR:S_UNR + 1]
                    tt = nc.vector.tensor_tensor
                    if s == 0:
                        ready(dve, p_sc, f + 1)
                        link(nc.vector.scalar_tensor_tensor(out=scr[:, :, :], in0=sp[:, :, 0, :], scalar=un,
                                                            in1=gb[:, :].unsqueeze(1).broadcast_to((P, 2, NE)),
                                                            op0=ALU.mult, op1=ALU.add))
                        link(nc.vector.scalar_tensor_tensor(out=scr[:, :, :], in0=sp[:, :, 1, :], scalar=un,
                                                            in1=scr[:, :, :], op0=ALU.mult, op1=ALU.add))
                        link(nc.vector.tensor_reduce(m1[:, :], scr[:, :, :], AX.X, ALU.max))
                        link(tt(o1[:, :, :], scr[:, :, :], bc(m1[:, :]), ALU.is_equal))
                        link(tt(cd[:, :, :], o1[:, :, :], desc, ALU.mult))
                        link(nc.vector.tensor_reduce(cm[:, :], cd[:, :, :], AX.X, ALU.max))
                        link(tt(o1[:, :, :], cd[:, :, :], bc(cm[:, :]), ALU.is_equal))
                    if s == 1:
                        link(nc.vector.scalar_tensor_tensor(out=scr[:, :, :], in0=o1[:, :, :], scalar=-3e38,
                                                            in1=scr[:, :, :], op0=ALU.mult, op1=ALU.add))
                        link(nc.vector.tensor_reduce(m2[:, :], scr[:, :, :], AX.X, ALU.max))
                        link(tt(o2[:, :, :], scr[:, :, :], bc(m2[:, :]), ALU.is_equal))
                        link(tt(cd[:, :, :], o2[:, :, :], desc, ALU.mult))
                        link(nc.vector.tensor_reduce(cm[:, :], cd[:, :, :], AX.X, ALU.max))
                        link(tt(o2[:, :, :], cd[:, :, :], bc(cm[:, :]), ALU.is_equal))
                        link(tt(dg[:, :], m1[:, :], m2[:, :], ALU.subtract))
                    if s == 2:
                        ready(dve, a_g, f + 1)
                        link(tt(o1[:, :, :], o1[:, :, :], bc(g1[:, 0, :]), ALU.mult))
                        link(tt(o2[:, :, :], o2[:, :, :], bc(g1[:, 1, :]), ALU.mult))
                        link(tt(comb[:, :, :], o1[:, :, :], o2[:, :, :], ALU.add))

                def ffn_slice(f, s, now, late):
                    if s < 3 and now:
                        choose(f, s)
                    if s == 3 and now:
                        ready(dve, p_ct, f + 1)
                        nc.vector.tensor_copy(combT[:, :], ps[0:NE, 3, 0:TT]).then_inc(v_ct, 1)
                    for i, g in due(GATE_AT, s, f, now, late):
                        e = i // FC
                        ready(dve, a_cb, g * NE + e + 1)
                        ready(dve, v_t, g * NCH + i + 1)
                        nc.vector.tensor_tensor(tb[:, i % TB, :], tb[:, i % TB, :], cb[:, e % 2, :], ALU.mult)\
                            .then_inc(v_u, 1)
                    for i, g in due(ACT_AT, s, f, now, late):
                        e, c = i // FC, i % FC
                        ready(dve, a_sg, g * NCH + i + 1)
                        ready(dve, g_l, so_far(g, NCH, i - TB + 1))
                        nc.vector.scalar_tensor_tensor(out=tb[:, i % TB, :], in0=ps[:, 6 + i % 2, 0:TT],
                                                       scalar=b1s[:, c, e:e + 1], in1=sg[:, i % 2, :],
                                                       op0=ALU.add, op1=ALU.mult).then_inc(v_t, 1)
                    for m, g in due(Y_AT, s, f, now, late):
                        if m == 0:
                            ready(dve, p_dn, (g + 1) * NCH)
                        xr = x1T[:, m, bass.ds(g * SPT, SPT), :].rearrange("p s b -> p (s b)")
                        nc.vector.scalar_tensor_tensor(out=xr, in0=ps[:, 4 + m // 2, (m % 2) * TT:(m % 2 + 1) * TT],
                                                       scalar=sc[:, S_UN2:S_UN2 + 1], in1=xr,
                                                       op0=ALU.mult, op1=ALU.add).then_inc(v_y, 1)

                def tile(t, recur, now, late, steps=SPT):
                    for s in range(steps):
                        if recur:
                            if s % (SPT // 2) == 0:
                                dve.wait_ge(d_g[s // (SPT // 2)], t * 16 + 16)
                            step(t * SPT + s, s)
                        ffn_slice(t - 1, s, now, late)
                    if recur:
                        ready(dve, a_ar, t * SPT + SPT)
                        if now:
                            ready(dve, p_up, t * NCH)
                        nc.vector.tensor_copy(cur[:, :, :, :, :].rearrange("p k a s b -> p (k a s b)"),
                                              nxt[:, :, :, :, :].rearrange("p k a s b -> p (k a s b)"))\
                            .then_inc(v_cur, 1)

                start(dve, v_sr, v_sz, v_ab, v_d, v_h, v_cur, v_rt, v_ct, v_t, v_u, v_y)
                tile(0, True, False, False)
                tile(1, True, True, False)
                with dve.Fori(2, NT) as t:
                    tile(t, True, True, True)
                tile(NT, False, True, True)
                tile(NT + 1, False, False, True, LAST_STEPS)


def constants():
    import numpy as np

    i = np.arange(P)
    own = np.concatenate([np.eye(P, dtype=np.float32),
                          np.broadcast_to(np.arange(NE, 0, -1, dtype=np.float32), (P, NE))], axis=1)
    c = np.zeros((P, T_ALL), np.float32)
    half = DH2 // 2
    partner = np.where(i % DH2 < half, i + half, i - half)
    c[partner, C_ROT + i] = 1.0
    c[:, C_CAUS:C_CAUS + P] = np.where(i[None, :] <= i[:, None], 0.0, NEG)
    c[:, C_NB0:C_NB0 + P] = np.where(np.abs(i[None, :] - i[:, None]) <= RECENT, 0.0, NEG)
    c[:, C_NB1:C_NB1 + P] = np.where(np.abs(i[None, :] + P - i[:, None]) <= RECENT, 0.0, NEG)
    inv = (np.float32(1.0) / np.float32(10000.0) ** (np.arange(0, DH2, 2, dtype=np.float32) / np.float32(DH2)))
    ang = np.arange(S, dtype=np.float32)[None, :] * inv.astype(np.float32)[i % half][:, None]
    sign = np.where(i % DH2 < half, -1.0, 1.0)[:, None]
    cos, sin = np.cos(ang), np.sin(ang) * sign
    c[:, C_COSQ:C_COSQ + S] = cos * DH2 ** -0.5
    c[:, C_SINQ:C_SINQ + S] = sin * DH2 ** -0.5
    c[:, C_COSK:C_COSK + S] = cos
    c[:, C_SINK:C_SINK + S] = sin
    for q in range(HPC):
        c[q * DH2:(q + 1) * DH2, C_HEAD + q] = 1.0
    c[:, C_DESC:C_DESC + S] = np.arange(S, 0, -1)
    return own, c


def kernel(x, cond_2048, L0_cond_Wq, L0_cond_Wk, L0_cond_Wv, L0_cond_b, L0_attn_Wq, L0_attn_Wk, L0_attn_Wv,
           L0_attn_Wo, L0_cond2_W_ih, L0_cond2_W_hh, L0_cond2_b_ih, L0_cond2_b_hh, L0_ffn_gate_w, L0_ffn_gate_b,
           L0_ffn_bias, L0_ffn_w1, L0_ffn_b1, L0_ffn_w2, L0_ffn_b2):
    import numpy as np
    import concourse.bacc as bacc
    from concourse.bass_utils import run_bass_kernel_spmd

    n = np.asarray
    heads = [n(w).reshape(NH, DH1, KS, P).transpose(0, 3, 2, 1) for w in (L0_cond_Wq, L0_cond_Wk, L0_cond_Wv)]
    own, table = constants()
    arrays = {
        "consts": own,
        "table": table,
        "x": n(x),
        "xT": n(x).transpose(2, 1, 0).reshape(D, S * B),
        "cond": n(cond_2048),
        "condT": n(cond_2048).T,
        "cond_b": np.broadcast_to(n(L0_cond_b).reshape(1, 1), (B, 1)),
        "cond_WvT": n(L0_cond_Wv).T,
        "cond_Wh": np.stack(heads, axis=3),
        "attn_WqT": n(L0_attn_Wq).T,
        "attn_WkT": n(L0_attn_Wk).T,
        "attn_WvT": n(L0_attn_Wv).T,
        "attn_WoT": n(L0_attn_Wo).T,
        "W_ih": n(L0_cond2_W_ih),
        "W_hh": n(L0_cond2_W_hh),
        "b_ih": n(L0_cond2_b_ih).reshape(NQ, P).T,
        "b_hh": n(L0_cond2_b_hh).reshape(NQ, P).T,
        "b_hh_n": n(L0_cond2_b_hh)[2 * D:].reshape(1, D),
        "gate_wT": n(L0_ffn_gate_w).T,
        "gate_b": n(L0_ffn_gate_b).reshape(1, NE),
        "bias": n(L0_ffn_bias).reshape(1, NE),
        "w1T": n(L0_ffn_w1).transpose(2, 0, 1).reshape(D, NE * HF),
        "b1T": n(L0_ffn_b1).T,
        "w2T": n(L0_ffn_w2).transpose(2, 0, 1),
        "b2": n(L0_ffn_b2),
    }
    arrays = {k: np.ascontiguousarray(v) for k, v in arrays.items()}
    nc = bacc.Bacc("TRN2", target_bir_lowering=False, num_devices=1)
    ins = {k: nc.dram_tensor(f"in_{k}", v.shape, mybir.dt.from_np(v.dtype), kind="ExternalInput").ap()
           for k, v in arrays.items()}
    out = nc.dram_tensor("out_0", (D, S * B), F32, kind="ExternalOutput").ap()
    program(nc, ins, out)
    r = run_bass_kernel_spmd(nc, [{f"in_{k}": v for k, v in arrays.items()}], core_ids=[0])
    got = r.results[0]["out_0"]
    return np.ascontiguousarray(got.reshape(D, S, B).transpose(2, 1, 0))
```
